# Optimizing a Trainium2 kernel written in Bass

```python
import numpy as np
import jax
import jax.numpy as jnp

def _softmax(x, axis=-1):
    return jax.nn.softmax(x, axis=axis)

def _gelu(x):
    return jax.nn.gelu(x, approximate=True)

def _silu(x):
    return jax.nn.silu(x)

def _sigmoid(x):
    return jax.nn.sigmoid(x)

def _layernorm(x, axis=-1, eps=1e-05):
    m = jnp.mean(x, axis=axis, keepdims=True)
    v = jnp.var(x, axis=axis, keepdims=True)
    return (x - m) / jnp.sqrt(v + eps)

def _scatter_add(tgt, idx, src, axis=0):
    return tgt.at[idx].add(src)

def _segment_sum(src, seg, n):
    return jax.ops.segment_sum(src, seg, n)
kernel_name = 'mk_gnn_preln_d4_gnn_r64_290bc9'

def setup_inputs(seed: int=0):
    np.random.seed(seed)
    _w = jnp.asarray

    def _rec_inputs():
        import jax
        import jax.numpy as jnp
        _gk = jax.random.key(seed)
        x = -0.000202 + 1 * jax.random.normal(jax.random.fold_in(_gk, 1), (100000, 64), jnp.float32)
        src = jax.random.randint(jax.random.fold_in(_gk, 2), (25000,), 0, 100000, jnp.int32)
        dst = jax.random.randint(jax.random.fold_in(_gk, 3), (25000,), 0, 100000, jnp.int32)
        _o = jnp.argsort(dst, stable=True)
        src = src[_o]
        dst = dst[_o]
        edge_attr_64 = -2.25437e-05 + 0.999858 * jax.random.normal(jax.random.fold_in(_gk, 12), (25000, 64), jnp.float32)
        return (x, src, dst, edge_attr_64)
    x, src, dst, edge_attr_64 = _rec_inputs()

    def _L0_gnn_setup():
        import jax, jax.numpy as jnp
        import numpy as np
        N_NODES = 100000
        N_EDGES = 1250000
        IN_CH = 64
        HID_CH = 64
        NUM_LAYERS = 3

        def _glorot(key, shape):
            fan_in, fan_out = (shape[1], shape[0])
            lim = jnp.sqrt(6.0 / (fan_in + fan_out)).astype(jnp.float32)
            return jax.random.uniform(key, shape, jnp.float32, -lim, lim)

        def _sage_layer(x, src, dst, wl, bl, wr):
            agg = jax.ops.segment_sum(x[src], dst, num_segments=N_NODES)
            deg = jax.ops.segment_sum(jnp.ones((src.shape[0],), x.dtype), dst, num_segments=N_NODES)
            agg = agg / jnp.maximum(deg, 1.0)[:, None]
            return jax.nn.relu(agg @ wl.T + bl + x @ wr.T)
        key = jax.random.key(seed)
        ks = jax.random.split(key, 2 + 3 * NUM_LAYERS)
        inp = {'x': jax.random.normal(ks[0], (N_NODES, IN_CH), jnp.float32), 'edge_index': jax.random.randint(ks[1], (2, N_EDGES), 0, N_NODES, jnp.int64), 'batch': jnp.zeros((N_NODES,), jnp.int64)}
        dims = [(IN_CH, HID_CH)] + [(HID_CH, HID_CH)] * (NUM_LAYERS - 1)
        for i, (din, dout) in enumerate(dims):
            inp[f'wl{i}'] = _glorot(ks[2 + 3 * i], (dout, din))
            inp[f'bl{i}'] = jnp.zeros((dout,), jnp.float32)
            inp[f'wr{i}'] = _glorot(ks[3 + 3 * i], (dout, din))
        return inp
    _L0_gnn_all = _L0_gnn_setup()
    _L0_gnn_in = {k: v for k, v in _L0_gnn_all.items() if k in ('wl0', 'bl0', 'wr0', 'wl1', 'bl1', 'wr1', 'wl2', 'bl2', 'wr2')}
    del _L0_gnn_all

    def _L1_gnn_setup():
        import jax, jax.numpy as jnp
        import numpy as np
        N = 100000
        E = 25000
        D = 64
        H = 128
        L = 3
        BN_EPS = 1e-05
        key = jax.random.key(seed)
        ks = jax.random.split(key, 9)
        x = jax.random.normal(ks[0], (N, D), jnp.float32)
        edge_index = jax.random.randint(ks[1], (2, E), 0, N, dtype=jnp.int64)
        W1 = jax.random.normal(ks[2], (L, D, H), jnp.float32) * (1.0 / np.sqrt(D))
        b1 = jnp.zeros((L, H), jnp.float32)
        gamma = jnp.ones((L, H), jnp.float32)
        beta = jnp.zeros((L, H), jnp.float32)
        W2 = jax.random.normal(ks[3], (L, H, D), jnp.float32) * (1.0 / np.sqrt(H))
        b2 = jnp.zeros((L, D), jnp.float32)
        eps = jnp.zeros((L,), jnp.float32)
        return {'x': x, 'W1': W1, 'b1': b1, 'gamma': gamma, 'beta': beta, 'W2': W2, 'b2': b2, 'eps': eps, 'edge_index': edge_index}
    _L1_gnn_all = _L1_gnn_setup()
    _L1_gnn_in = {k: v for k, v in _L1_gnn_all.items() if k in ('W1', 'b1', 'gamma', 'beta', 'W2', 'b2', 'eps')}
    del _L1_gnn_all

    def _L2_gnn_setup():
        import jax, jax.numpy as jnp
        import numpy as np
        N_NODES = 100000
        N_EDGES = 25000
        HIDDEN = 64
        HEADS = 8
        HEAD_DIM = HIDDEN // HEADS
        key = jax.random.key(seed)
        ks = jax.random.split(key, 11)
        s = 1.0 / np.sqrt(HIDDEN)
        x = jax.random.normal(ks[0], (N_NODES, HIDDEN), dtype=jnp.float32)
        edge_index = jax.random.randint(ks[1], (2, N_EDGES), 0, N_NODES, dtype=jnp.int64)
        Wq = jax.random.normal(ks[2], (HIDDEN, HIDDEN), dtype=jnp.float32) * s
        bq = jax.random.normal(ks[3], (HIDDEN,), dtype=jnp.float32) * s
        Wk = jax.random.normal(ks[4], (HIDDEN, HIDDEN), dtype=jnp.float32) * s
        bk = jax.random.normal(ks[5], (HIDDEN,), dtype=jnp.float32) * s
        Wv = jax.random.normal(ks[6], (HIDDEN, HIDDEN), dtype=jnp.float32) * s
        bv = jax.random.normal(ks[7], (HIDDEN,), dtype=jnp.float32) * s
        Wo = jax.random.normal(ks[8], (HIDDEN, HIDDEN), dtype=jnp.float32) * s
        bo = jax.random.normal(ks[9], (HIDDEN,), dtype=jnp.float32) * s
        return {'x': x, 'edge_index': edge_index, 'Wq': Wq, 'bq': bq, 'Wk': Wk, 'bk': bk, 'Wv': Wv, 'bv': bv, 'Wo': Wo, 'bo': bo}
    _L2_gnn_all = _L2_gnn_setup()
    _L2_gnn_in = {k: v for k, v in _L2_gnn_all.items() if k in ('Wq', 'bq', 'Wk', 'bk', 'Wv', 'bv', 'Wo', 'bo')}
    del _L2_gnn_all

    def _L3_gnn_setup():
        import jax, jax.numpy as jnp
        import numpy as np
        N_NODES = 100000
        N_EDGES = 15625
        D_NODE = 64
        D_EDGE = 64
        NUM_LAYERS = 3
        EPS = 1e-12

        def _l2norm(h):
            n = jnp.sqrt(jnp.sum(h * h, axis=-1, keepdims=True))
            return h / jnp.maximum(n, EPS)
        key = jax.random.key(seed)
        ks = jax.random.split(key, 10)
        s = 0.05
        inp = {'x': jax.random.normal(ks[0], (N_NODES, D_NODE), jnp.float32), 'edge_attr': jax.random.normal(ks[1], (N_EDGES, D_EDGE), jnp.float32), 'edge_index': jax.random.randint(ks[2], (2, N_EDGES), 0, N_NODES, jnp.int32), 'msg_W': jax.random.normal(ks[3], (NUM_LAYERS, D_NODE + D_EDGE, D_NODE), jnp.float32) * s, 'msg_b': jnp.zeros((NUM_LAYERS, D_NODE), jnp.float32), 'agg_W': jax.random.normal(ks[4], (NUM_LAYERS, D_NODE + D_NODE, D_NODE), jnp.float32) * s, 'agg_b': jnp.zeros((NUM_LAYERS, D_NODE), jnp.float32), 'edge_W': jax.random.normal(ks[5], (NUM_LAYERS - 1, 2 * D_NODE + D_EDGE, D_EDGE), jnp.float32) * s, 'edge_b': jnp.zeros((NUM_LAYERS - 1, D_EDGE), jnp.float32)}
        return inp
    _L3_gnn_all = _L3_gnn_setup()
    _L3_gnn_in = {k: v for k, v in _L3_gnn_all.items() if k in ('msg_W', 'msg_b', 'agg_W', 'agg_b', 'edge_W', 'edge_b')}
    del _L3_gnn_all
    return {'x': x, 'src': src, 'dst': dst, 'edge_attr_64': edge_attr_64, 'L0_gnn_wl0': _L0_gnn_in['wl0'], 'L0_gnn_bl0': _L0_gnn_in['bl0'], 'L0_gnn_wr0': _L0_gnn_in['wr0'], 'L0_gnn_wl1': _L0_gnn_in['wl1'], 'L0_gnn_bl1': _L0_gnn_in['bl1'], 'L0_gnn_wr1': _L0_gnn_in['wr1'], 'L0_gnn_wl2': _L0_gnn_in['wl2'], 'L0_gnn_bl2': _L0_gnn_in['bl2'], 'L0_gnn_wr2': _L0_gnn_in['wr2'], 'L1_gnn_W1': _L1_gnn_in['W1'], 'L1_gnn_b1': _L1_gnn_in['b1'], 'L1_gnn_gamma': _L1_gnn_in['gamma'], 'L1_gnn_beta': _L1_gnn_in['beta'], 'L1_gnn_W2': _L1_gnn_in['W2'], 'L1_gnn_b2': _L1_gnn_in['b2'], 'L1_gnn_eps': _L1_gnn_in['eps'], 'L2_gnn_Wq': _L2_gnn_in['Wq'], 'L2_gnn_bq': _L2_gnn_in['bq'], 'L2_gnn_Wk': _L2_gnn_in['Wk'], 'L2_gnn_bk': _L2_gnn_in['bk'], 'L2_gnn_Wv': _L2_gnn_in['Wv'], 'L2_gnn_bv': _L2_gnn_in['bv'], 'L2_gnn_Wo': _L2_gnn_in['Wo'], 'L2_gnn_bo': _L2_gnn_in['bo'], 'L3_gnn_msg_W': _L3_gnn_in['msg_W'], 'L3_gnn_msg_b': _L3_gnn_in['msg_b'], 'L3_gnn_agg_W': _L3_gnn_in['agg_W'], 'L3_gnn_agg_b': _L3_gnn_in['agg_b'], 'L3_gnn_edge_W': _L3_gnn_in['edge_W'], 'L3_gnn_edge_b': _L3_gnn_in['edge_b']}

def reference(x, src, dst, edge_attr_64, L0_gnn_wl0, L0_gnn_bl0, L0_gnn_wr0, L0_gnn_wl1, L0_gnn_bl1, L0_gnn_wr1, L0_gnn_wl2, L0_gnn_bl2, L0_gnn_wr2, L1_gnn_W1, L1_gnn_b1, L1_gnn_gamma, L1_gnn_beta, L1_gnn_W2, L1_gnn_b2, L1_gnn_eps, L2_gnn_Wq, L2_gnn_bq, L2_gnn_Wk, L2_gnn_bk, L2_gnn_Wv, L2_gnn_bv, L2_gnn_Wo, L2_gnn_bo, L3_gnn_msg_W, L3_gnn_msg_b, L3_gnn_agg_W, L3_gnn_agg_b, L3_gnn_edge_W, L3_gnn_edge_b):
    import jax
    import jax.numpy as jnp

    def _L0_gnn_ref(x, edge_index, batch, wl0, bl0, wr0, wl1, bl1, wr1, wl2, bl2, wr2):
        import jax, jax.numpy as jnp
        import numpy as np
        N_NODES = 100000
        N_EDGES = 1250000
        IN_CH = 64
        HID_CH = 64
        NUM_LAYERS = 3

        def _glorot(key, shape):
            fan_in, fan_out = (shape[1], shape[0])
            lim = jnp.sqrt(6.0 / (fan_in + fan_out)).astype(jnp.float32)
            return jax.random.uniform(key, shape, jnp.float32, -lim, lim)

        def _sage_layer(x, src, dst, wl, bl, wr):
            agg = jax.ops.segment_sum(x[src], dst, num_segments=N_NODES)
            deg = jax.ops.segment_sum(jnp.ones((src.shape[0],), x.dtype), dst, num_segments=N_NODES)
            agg = agg / jnp.maximum(deg, 1.0)[:, None]
            return jax.nn.relu(agg @ wl.T + bl + x @ wr.T)
        src, dst = (edge_index[0], edge_index[1])
        x = _sage_layer(x, src, dst, wl0, bl0, wr0)
        x = _sage_layer(x, src, dst, wl1, bl1, wr1)
        x = _sage_layer(x, src, dst, wl2, bl2, wr2)
        return x

    def _L1_gnn_ref(x, W1, b1, gamma, beta, W2, b2, eps, edge_index):
        import jax, jax.numpy as jnp
        import numpy as np
        N = 100000
        E = 25000
        D = 64
        H = 128
        L = 3
        BN_EPS = 1e-05
        src, dst = (edge_index[0], edge_index[1])
        for l in range(L):
            agg = jax.ops.segment_sum(x[src], dst, num_segments=N)
            h = (1.0 + eps[l]) * x + agg
            h = h @ W1[l] + b1[l]
            mu = jnp.mean(h, axis=0)
            var = jnp.var(h, axis=0)
            h = (h - mu) * jax.lax.rsqrt(var + BN_EPS) * gamma[l] + beta[l]
            h = jax.nn.relu(h)
            x = h @ W2[l] + b2[l]
        return x

    def _L2_gnn_ref(x, edge_index, Wq, bq, Wk, bk, Wv, bv, Wo, bo):
        import jax, jax.numpy as jnp
        import numpy as np
        N_NODES = 100000
        N_EDGES = 25000
        HIDDEN = 64
        HEADS = 8
        HEAD_DIM = HIDDEN // HEADS
        N = x.shape[0]
        scale = np.float32(np.sqrt(HEAD_DIM))
        Q = (x @ Wq + bq).reshape(N, HEADS, HEAD_DIM)
        K = (x @ Wk + bk).reshape(N, HEADS, HEAD_DIM)
        V = (x @ Wv + bv).reshape(N, HEADS, HEAD_DIM)
        row, col = (edge_index[0], edge_index[1])
        q_i = Q[row]
        k_j = K[col]
        v_j = V[col]
        scores = (q_i * k_j).sum(axis=-1) / scale
        edge_max = scores.max(axis=1)
        node_max = jax.ops.segment_max(edge_max, row, num_segments=N)
        exp = jnp.exp(scores - node_max[row][:, None])
        sums = jax.ops.segment_sum(exp, row, num_segments=N)
        attn = exp / (sums[row] + 1e-08)
        agg = jax.ops.segment_sum(attn[:, :, None] * v_j, row, num_segments=N)
        return agg.reshape(N, HIDDEN) @ Wo + bo

    def _L3_gnn_ref(x, edge_attr, edge_index, msg_W, msg_b, agg_W, agg_b, edge_W, edge_b):
        import jax, jax.numpy as jnp
        import numpy as np
        N_NODES = 100000
        N_EDGES = 15625
        D_NODE = 64
        D_EDGE = 64
        NUM_LAYERS = 3
        EPS = 1e-12

        def _l2norm(h):
            n = jnp.sqrt(jnp.sum(h * h, axis=-1, keepdims=True))
            return h / jnp.maximum(n, EPS)
        src = edge_index[0]
        dst = edge_index[1]
        n = x.shape[0]
        num_layers = msg_W.shape[0]
        cnt = jax.ops.segment_sum(jnp.ones((src.shape[0],), x.dtype), dst, num_segments=n)
        inv_cnt = (1.0 / jnp.maximum(cnt, 1.0))[:, None]
        for l in range(num_layers):
            m = jnp.concatenate([x[src], edge_attr], axis=-1) @ msg_W[l] + msg_b[l]
            m = jax.nn.relu(m)
            aggr = jax.ops.segment_sum(m, dst, num_segments=n) * inv_cnt
            h = jnp.concatenate([aggr, x], axis=-1) @ agg_W[l] + agg_b[l]
            x = _l2norm(jax.nn.relu(h))
            if l < num_layers - 1:
                e = jnp.concatenate([x[src], x[dst], edge_attr], axis=-1) @ edge_W[l] + edge_b[l]
                edge_attr = jax.nn.relu(e)
        return x
    edge_index = jnp.stack([src, dst])
    batch0 = jnp.zeros((100000,), jnp.int32)
    h = jnp.maximum(_layernorm(x, axis=-1), 0.0)
    x = x + _L0_gnn_ref(h, edge_index, batch0, L0_gnn_wl0, L0_gnn_bl0, L0_gnn_wr0, L0_gnn_wl1, L0_gnn_bl1, L0_gnn_wr1, L0_gnn_wl2, L0_gnn_bl2, L0_gnn_wr2)
    h = jnp.maximum(_layernorm(x, axis=-1), 0.0)
    x = x + _L1_gnn_ref(h, L1_gnn_W1, L1_gnn_b1, L1_gnn_gamma, L1_gnn_beta, L1_gnn_W2, L1_gnn_b2, L1_gnn_eps, edge_index)
    h = jnp.maximum(_layernorm(x, axis=-1), 0.0)
    x = x + _L2_gnn_ref(h, edge_index, L2_gnn_Wq, L2_gnn_bq, L2_gnn_Wk, L2_gnn_bk, L2_gnn_Wv, L2_gnn_bv, L2_gnn_Wo, L2_gnn_bo)
    h = jnp.maximum(_layernorm(x, axis=-1), 0.0)
    x = x + _L3_gnn_ref(h, edge_attr_64, edge_index, L3_gnn_msg_W, L3_gnn_msg_b, L3_gnn_agg_W, L3_gnn_agg_b, L3_gnn_edge_W, L3_gnn_edge_b)
    return x

_drawn_inputs = setup_inputs


def setup_inputs(seed=0):
    import zlib

    import numpy as np

    out = dict(_drawn_inputs(seed))
    spreads = {'L0_gnn_bl0': (0.0, 0.1),
     'L0_gnn_bl1': (0.0, 0.1),
     'L0_gnn_bl2': (0.0, 0.1),
     'L1_gnn_b1': (0.0, 0.8),
     'L1_gnn_gamma': (1.0, 0.2),
     'L1_gnn_beta': (0.0, 0.1),
     'L1_gnn_b2': (0.0, 0.1),
     'L1_gnn_eps': (0.0, 0.419),
     'L3_gnn_msg_b': (0.0, 0.8),
     'L3_gnn_agg_b': (0.0, 0.1),
     'L3_gnn_edge_b': (0.0, 0.8)}
    factors = {'edge_attr_64': 8.0,
     'L2_gnn_Wq': 7.163,
     'L2_gnn_bq': 8.0,
     'L2_gnn_Wk': 7.034,
     'L2_gnn_bk': 8.0,
     'L3_gnn_msg_W': 5.506,
     'L3_gnn_edge_W': 8.0}
    for name, (base, spread) in spreads.items():
        noise = np.random.default_rng([zlib.crc32(name.encode()), seed]).standard_normal(out[name].shape)
        drawn = base * np.exp(spread * noise) if base else spread * noise
        out[name] = jnp.asarray(drawn.astype(out[name].dtype))
    for name, factor in factors.items():
        out[name] = (out[name] * factor).astype(out[name].dtype)
    return out
```

```python
class Counted:

    def __init__(self, sem):
        self.sem, self.base = sem, 0


def hold(engine, passed, sem, value):
    engine.wait_ge(sem, value)
    engine.sem_inc(passed.sem, 1)


def build_program(nc, t, out):
    import concourse.bass as bass
    from concourse import mybir
    from contextlib import ExitStack
    import numpy as np

    f32, i32, bf16 = mybir.dt.float32, mybir.dt.int32, mybir.dt.bfloat16
    ALU = mybir.AluOpType
    ACT = mybir.ActivationFunctionType
    AX = mybir.AxisListType.X
    ds = bass.ds

    P = 128
    N, D = t["x"].shape
    E = t["src"].shape[0]
    J = 8
    BLK = P * J
    H = t["L1_gnn_W1"].shape[2]
    HEADS = 8
    HD = D // HEADS
    EB = -(-E // BLK)
    EP = EB * BLK
    ET = EB * J
    NB = -(-N // BLK)
    OVER = (NB * BLK - N) // J
    assert NB * BLK - N == OVER * J and E % J == 0
    BIG = 1 << 22
    NEG = -1.0e30
    LN_EPS, BN_EPS, L2_EPS, SM_EPS = 1e-5, 1e-5, 1e-12, 1e-8
    DL, EL = 3, 2
    REC = 80
    DIGIT = 6
    RADIX = 1 << DIGIT
    PASSES = -(-int(N).bit_length() // DIGIT)

    ctx = ExitStack()
    with ctx:
        def dram(name, shape, dt=f32):
            return nc.dram_tensor(name, shape, dt).ap()

        def sb(name, shape, dt=f32, c=ctx):
            return c.enter_context(nc.sbuf_tensor(name, shape, dt))

        def counted(name):
            return Counted(ctx.enter_context(nc.semaphore(name)))

        x1_nodes = dram("x1_nodes", (N, D))
        x2_nodes = dram("x2_nodes", (N, D))
        h_nodes = [dram(f"h_nodes{k}", (N, D)) for k in range(2)]
        attn_nodes = dram("attn_nodes", (N, D))
        pos_nodes = dram("pos_nodes", (N, 1), i32)
        sd = [dram(f"sd{k}", (EP, 2 * D)) for k in range(2)]
        sd_resid = dram("sd_resid", (EP, 2 * D))
        gin_x = dram("gin_x", (EB, P, BLK))
        gin_agg = dram("gin_agg", (EB, D, BLK))
        edge_state = dram("edge_state", (EB, D, BLK))
        records = dram("records", (EP, REC))
        src_pad = dram("src_pad", (EP,), i32)
        dst_pad = dram("dst_pad", (EP + 2 * J,), i32)
        key_pad = dram("key_pad", (EP + 2 * J,), i32)
        same_dst = dram("same_dst", (EP,))
        inv_deg = dram("inv_deg", (EP,))
        neg_start = dram("neg_start", (EP,))
        sorting = [dram(f"sorting{k}", (EP, 2), i32) for k in range(2)]

        def rows(table, b, width=None):
            return table[ds(b * BLK, BLK), :].rearrange("(p j) d -> p j d", j=J)

        def cols_bj(vec):
            return vec.rearrange("(b p j) -> p b j", p=P, j=J)

        chain = [counted(f"lane{k}_steps_done") for k in range(DL)]
        loaded = [counted(f"lane{k}_loaded") for k in range(DL)]
        stored = [counted(f"lane{k}_stored") for k in range(DL)]
        gathered = [counted(f"lane{k}_gathered") for k in range(DL)]
        waits_passed = counted("waits_passed")
        waits_passed_sp = counted("waits_passed_sp")
        staged = counted("indices_staged")
        setup_dma = counted("setup_dma")
        setup_step = counted("setup_step")
        weights_in = counted("weights_in")
        zeroed = counted("weights_zeroed")
        attn_zeroed = counted("attention_table_zeroed")

        ident = sb("ident", [P, P])
        src_clamped = sb("src_clamped", [P, ET], i32)
        dst_clamped = sb("dst_clamped", [P, ET], i32)
        link_idx = sb("link_idx", [P, ET], i32)
        home_idx = sb("home_idx", [P, ET], i32)
        last_dst_idx = sb("last_dst_idx", [P, ET], i32)
        rep_mask = sb("rep_mask", [P, ET])
        node_mask = sb("node_mask", [P, NB * J])
        sorted_edge = sb("sorted_edge", [P, ET], i32)
        attn_out_idx = sb("attn_out_idx", [P, ET], i32)
        idx_stage = [sb(f"idx_stage{k}", [P, 2 * J], i32) for k in range(2)]
        eps_ln = sb("eps_ln", [P, 1])
        eps_bn = sb("eps_bn", [P, 1])
        ones = sb("ones", [P, P])

        work = ctx.enter_context(nc.psum_tensor("work", [P, 6 * 512], f32))
        gram_nodes = ctx.enter_context(nc.psum_tensor("gram_nodes", [P, 512], f32))
        gram_edges = ctx.enter_context(nc.psum_tensor("gram_edges", [P, 512], f32))

        zero_tiles, weight_loads = [], []

        def weight(name, shape, parts, zero=False):
            tile = sb(name, shape)
            if zero:
                zero_tiles.append(tile)
            for where, src in parts(tile):
                weight_loads.append((where, src))
            return tile

        def column(name, vec, copies):
            n = vec.shape[0]
            return weight(name, [P, 1], lambda w: [
                (w[k * n:(k + 1) * n, :], vec.rearrange("(n o) -> n o", o=1)) for k in range(copies)])

        def block_diag(name, m):
            return weight(name, [P, P], lambda w: [(w[0:D, 0:D], m), (w[D:P, D:P], m)], zero=True)

        def to_dst(name, m, at=0):
            return weight(name, [P, P], lambda w: [(w[at:at + m.shape[0], D:P], m)], zero=True)

        sage = []
        for l in range(3):
            sage.append(dict(own=block_diag(f"sage_own{l}", t[f"L0_gnn_wr{l}"]),
                             agg=to_dst(f"sage_agg{l}", t[f"L0_gnn_wl{l}"]),
                             bias=column(f"sage_bias{l}", t[f"L0_gnn_bl{l}"], 2)))
        gin = []
        for l in range(3):
            w1, w2 = t["L1_gnn_W1"][l], t["L1_gnn_W2"][l]
            eps_all = t["L1_gnn_eps"]
            gin.append(dict(
                w1=weight(f"gin_w1_{l}", [P, H], lambda w: [(w[0:D, :], w1), (w[D:P, :], w1)]),
                w1_own=sb(f"gin_w1_own{l}", [P, H]),
                w1_dst=sb(f"gin_w1_dst{l}", [P, H]),
                keep=weight(f"gin_keep{l}", [P, 1], lambda w: [(w[:, :], eps_all[l:l + 1].partition_broadcast(P))]),
                keep_ident=sb(f"gin_keep_ident{l}", [P, D]),
                w2_src=weight(f"gin_w2_src{l}", [P, P], lambda w: [(w[:, 0:D], w2)], zero=True),
                w2_dst=weight(f"gin_w2_dst{l}", [P, P], lambda w: [(w[:, D:P], w2)], zero=True),
                b1=column(f"gin_b1_{l}", t["L1_gnn_b1"][l], 1),
                gamma=column(f"gin_gamma{l}", t["L1_gnn_gamma"][l], 1),
                beta=column(f"gin_beta{l}", t["L1_gnn_beta"][l], 1),
                b2=column(f"gin_b2_{l}", t["L1_gnn_b2"][l], 2),
                scale=sb(f"gin_scale{l}", [P, 1]), shift=sb(f"gin_shift{l}", [P, 1])))
        w_qkv = weight("w_qkv", [P, 2 * D], lambda w: [
            (w[0:D, 0:D], t["L2_gnn_Wq"]), (w[D:P, 0:D], t["L2_gnn_Wk"]), (w[D:P, D:P], t["L2_gnn_Wv"])], zero=True)
        b_qkv = weight("b_qkv", [P, 3, D], lambda w: [
            (w[:, k, :], t[f"L2_gnn_b{c}"].partition_broadcast(P)) for k, c in enumerate("qkv")])
        w_o = block_diag("w_o", t["L2_gnn_Wo"])
        b_o = column("b_o", t["L2_gnn_bo"], 2)
        gnn = []
        for l in range(3):
            aw = t["L3_gnn_agg_W"][l]
            g = dict(msg=weight(f"gnn_msg{l}", [P, D], lambda w: [(w[:, :], t["L3_gnn_msg_W"][l])]),
                     msg_b=column(f"gnn_msg_b{l}", t["L3_gnn_msg_b"][l], 1),
                     own=block_diag(f"gnn_own{l}", aw[D:2 * D, :]),
                     agg=to_dst(f"gnn_agg{l}", aw[0:D, :]),
                     bias=column(f"gnn_bias{l}", t["L3_gnn_agg_b"][l], 2))
            if l > 0:
                ew, eb = t["L3_gnn_edge_W"][l - 1], t["L3_gnn_edge_b"][l - 1]
                g.update(edge_nodes=to_dst(f"gnn_edge_nodes{l}", ew[0:2 * D, :]),
                         edge_own=to_dst(f"gnn_edge_own{l}", ew[2 * D:3 * D, :], at=D),
                         edge_b=column(f"gnn_edge_b{l}", eb, 2))
            gnn.append(g)
        pick_max = sb("pick_max", [P, 72])
        pick_score = sb("pick_score", [P, 72])

        def engine_setup_counts(n):
            setup_step.base += n

        with nc.Block() as block:
            @block.gpsimd
            def _(pool):
                for tile in zero_tiles:
                    pool.memset(tile[:, :], 0.0).then_inc(zeroed.sem, 1)
                pool.memset(ones[:, :], 1.0).then_inc(setup_step.sem, 1)
                pool.memset(eps_ln[:, :], LN_EPS).then_inc(setup_step.sem, 1)
                pool.memset(eps_bn[:, :], BN_EPS).then_inc(setup_step.sem, 1)
                pool.memset(ident[:, :], 0.0).then_inc(setup_step.sem, 1)
                pool.memset(pick_max[:, :], 0.0).then_inc(setup_step.sem, 1)
                pool.memset(pick_score[:, :], 0.0).then_inc(setup_step.sem, 1)
                pool.sem_inc(staged.sem, 64)
                pool.wait_ge(setup_step.sem, 6)
                pool.affine_select(out=ident[:, :], in_=ident[:, :], compare_op=ALU.not_equal, fill=1.0,
                                   base=0, pattern=[[-1, P]], channel_multiplier=1).then_inc(setup_step.sem, 1)
                pool.affine_select(out=pick_max[:, :], in_=pick_max[:, :], compare_op=ALU.not_equal, fill=1.0,
                                   base=-72, pattern=[[0, 72]], channel_multiplier=1).then_inc(setup_step.sem, 1)
                pool.affine_select(out=pick_score[:, 0:D].rearrange("p (h d) -> p h d", d=HD),
                                   in_=pick_score[:, 0:D].rearrange("p (h d) -> p h d", d=HD),
                                   compare_op=ALU.not_equal, fill=1.0, base=-D,
                                   pattern=[[-1, HEADS], [0, HD]], channel_multiplier=1).then_inc(setup_step.sem, 1)
                pool.affine_select(out=pick_score[:, D:72], in_=pick_score[:, D:72],
                                   compare_op=ALU.not_equal, fill=1.0, base=-D,
                                   pattern=[[-1, HEADS]], channel_multiplier=1).then_inc(setup_step.sem, 1)
                pool.wait_ge(setup_step.sem, 10)

            @block.sync
            def _(sp):
                sp.wait_ge(zeroed.sem, len(zero_tiles))
                for where, src in weight_loads:
                    sp.dma_start(where, src).then_inc(weights_in.sem, 16)

            @block.vector
            def _(dve):
                dve.wait_ge(weights_in.sem, 16 * len(weight_loads))
                dve.wait_ge(setup_step.sem, 10)
                for g in gin:
                    dve.tensor_scalar(g["keep"][:, :], g["keep"][:, :], 1.0, None, ALU.add).then_inc(setup_step.sem, 1)
                dve.wait_ge(setup_step.sem, 13)
                for g in gin:
                    dve.tensor_scalar(g["w1_own"][:, :], g["w1"][:, :], g["keep"][:, :], None, ALU.mult)
                    dve.memset(g["w1_dst"][0:D, :], 0.0)
                    dve.tensor_scalar(g["w1_dst"][D:P, :], g["w1"][D:P, :], g["keep"][D:P, :], None, ALU.mult)
                    dve.memset(g["keep_ident"][0:D, :], 0.0)
                    dve.tensor_scalar(g["keep_ident"][D:P, :], ident[D:P, D:P], g["keep"][D:P, :], None,
                                      ALU.mult).then_inc(setup_step.sem, 1)
                dve.wait_ge(setup_step.sem, 16)
        setup_step.base = 16
        staged.base = 64

        def segment_phase(key_table, first_name, with_inverse, out_idx, rep, start_table):
            with ExitStack() as c:
                keys = sb(first_name + "_keys", [P, 3, EB, J], i32, c)
                keysf = sb(first_name + "_keysf", [P, 3, ET], f32, c)
                start = sb(first_name + "_start", [P, ET], f32, c)
                last = sb(first_name + "_last", [P, ET], f32, c)
                valid = sb(first_name + "_valid", [P, ET], f32, c)
                idxf = sb(first_name + "_idxf", [P, ET], f32, c)
                if with_inverse:
                    CH = EP // EB * 5 if EB % 5 == 0 else BLK
                    run = sb("run", [1, CH], f32, c)
                    length = sb("length", [1, CH + 1], f32, c)
                    one_row = sb("one_row", [1, CH], f32, c)
                with nc.Block() as block:
                    d0, s0 = setup_dma.base, setup_step.base

                    @block.sync
                    def _(sp):
                        for k, shift in enumerate((J - 1, J, J + 1)):
                            sp.dma_start(keys[:, k, :, :], cols_bj(key_table[shift:shift + EP])).then_inc(setup_dma.sem, 16)
                        sp.wait_ge(setup_step.sem, s0 + 7)
                        sp.dma_start(cols_bj(start_table[:]), start[:, :].rearrange("p (b j) -> p b j", j=J)).then_inc(setup_dma.sem, 16)
                        sp.wait_ge(setup_dma.sem, d0 + 64)
                        if with_inverse:
                            for k in range(EP // CH):
                                if k:
                                    sp.wait_ge(setup_step.sem, s0 + 8 + 2 * k)
                                sp.dma_start(run[0:1, :], start_table[k * CH:(k + 1) * CH].rearrange("(o n) -> o n", o=1)).then_inc(setup_dma.sem, 16)
                                sp.wait_ge(setup_step.sem, s0 + 8 + 2 * (k + 1))
                                sp.dma_start(inv_deg[k * CH:(k + 1) * CH].rearrange("(o n) -> o n", o=1), run[0:1, :]).then_inc(setup_dma.sem, 16)
                                sp.wait_ge(setup_dma.sem, d0 + 64 + 32 * (k + 1))

                    @block.vector
                    def _(dve):
                        step = [s0]

                        def link(op):
                            step[0] += 1
                            op.then_inc(setup_step.sem, 1)
                            dve.wait_ge(setup_step.sem, step[0])

                        dve.wait_ge(setup_dma.sem, d0 + 48)
                        link(dve.tensor_copy(keysf[:, :, :], keys[:, :, :, :].rearrange("p k b j -> p k (b j)")))
                        link(dve.tensor_tensor(start[:, :], keysf[:, 1, :], keysf[:, 0, :], ALU.is_equal))
                        link(dve.tensor_tensor(last[:, :], keysf[:, 1, :], keysf[:, 2, :], ALU.not_equal))
                        link(dve.scalar_tensor_tensor(rep, keysf[:, 1, :], float(N), last[:, :], ALU.is_lt, ALU.mult))
                        link(dve.scalar_tensor_tensor(idxf[:, :], keysf[:, 1, :], -float(BIG), rep, ALU.add, ALU.mult))
                        link(dve.tensor_scalar(out_idx, idxf[:, :], float(BIG), None, ALU.add))
                        if with_inverse:
                            link(dve.tensor_scalar(start[:, :], start[:, :], 1.0, None, ALU.mult))
                            link(dve.memset(one_row[0:1, :], 1.0))
                            for k in range(EP // CH):
                                dve.wait_ge(setup_dma.sem, d0 + 64 + 32 * k + 16)
                                link(dve.tensor_tensor_scan(length[0:1, 1:CH + 1], run[0:1, :], one_row[0:1, :],
                                                            length[0:1, CH:CH + 1] if k else 0.0, ALU.mult, ALU.add))
                                link(dve.reciprocal(run[0:1, :], length[0:1, 1:CH + 1]))
                        else:
                            link(dve.tensor_scalar(start[:, :], start[:, :], -NEG, NEG, ALU.mult, ALU.add))
                        step_total[0] = step[0]

                    setup_step.base = step_total[0]
                    setup_dma.base = d0 + 64 + (32 * (EP // CH) if with_inverse else 0)

        step_total = [0]
        KP = EP // P
        full, rest = E // KP, E % KP
        with ExitStack() as c:
            keys_in = sb("keys_in", [P, 2, KP], i32, c)
            edge_marks = sb("edge_marks", [1, J], i32, c)
            key_big = sb("key_big", [P, 1024], i32, c)
            zero_rows = sb("zero_rows", [P, J * D], f32, c)
            NPOS = N // 125 if N % 125 == 0 else 0
            with nc.Block() as block:
                d0, s0 = setup_dma.base, setup_step.base
                n_fill = -(-N // (P * 512))

                @block.vector
                def _(dve):
                    dve.memset(keys_in[:, :, :], N).then_inc(setup_step.sem, 1)
                    dve.memset(edge_marks[:, :], -1).then_inc(setup_step.sem, 1)
                    dve.memset(key_big[:, :], BIG).then_inc(setup_step.sem, 1)
                    dve.memset(zero_rows[:, :], 0.0).then_inc(setup_step.sem, 1)

                @block.sync
                def _(sp):
                    sp.wait_ge(setup_step.sem, s0 + 4)
                    n = 0
                    for k, key in enumerate(("src", "dst")):
                        sp.dma_start(keys_in[0:full, k, :], t[key][0:full * KP].rearrange("(p k) -> p k", k=KP)).then_inc(setup_dma.sem, 16)
                        n += 1
                        if rest:
                            sp.dma_start(keys_in[full:full + 1, k, 0:rest], t[key][full * KP:E].rearrange("(p k) -> p k", p=1)).then_inc(setup_dma.sem, 16)
                            n += 1
                    sp.wait_ge(setup_dma.sem, d0 + 16 * n)
                    sp.dma_start(src_pad.rearrange("(p k) -> p k", k=KP), keys_in[:, 0, :]).then_inc(setup_dma.sem, 16)
                    sp.dma_start(dst_pad[J:J + EP].rearrange("(p k) -> p k", k=KP), keys_in[:, 1, :]).then_inc(setup_dma.sem, 16)
                    n += 2
                    for table in (dst_pad, key_pad):
                        for at in (0, J + EP):
                            sp.dma_start(table[at:at + J].rearrange("(o j) -> o j", o=1), edge_marks[:, :]).then_inc(setup_dma.sem, 16)
                            n += 1
                    for k in range(-(-N // (P * 512))):
                        lo, hi = k * P * 512, min(N, (k + 1) * P * 512)
                        w = (hi - lo) // P
                        if w:
                            sp.dma_start(pos_nodes[lo:lo + w * P, :].rearrange("(p w) o -> p (w o)", p=P), key_big[:, 0:w]).then_inc(setup_dma.sem, 16)
                            n += 1
                        r = (hi - lo) - w * P
                        if r:
                            sp.dma_start(pos_nodes[hi - r:hi, :].rearrange("(o w) u -> o (w u)", o=1), key_big[0:1, 0:r]).then_inc(setup_dma.sem, 16)
                            n += 1
                    with sp.Fori(0, NB - 1) as b:
                        sp.dma_start(rows(attn_nodes, b), zero_rows[:, :].rearrange("p (j d) -> p j d", j=J)).then_inc(attn_zeroed.sem, 16)
                    sp.dma_start(attn_nodes[(NB - 1) * BLK:N, :].rearrange("(p j) d -> p j d", j=J),
                                 zero_rows[OVER:P, :].rearrange("p (j d) -> p j d", j=J)).then_inc(attn_zeroed.sem, 16)
                    sp.wait_ge(attn_zeroed.sem, 16 * NB)
                    sp.wait_ge(setup_dma.sem, d0 + 16 * n)
                    step_total[0] = d0 + 16 * n

            setup_step.base += 4
            setup_dma.base = step_total[0]

        segment_phase(dst_pad, "dst", True, last_dst_idx[:, :], rep_mask[:, :], same_dst)

        with ExitStack() as c:
            iota_edge = sb("iota_edge", [P, ET], i32, c)
            src_i = sb("src_i", [P, EB, J], i32, c)
            dst_i = sb("dst_i", [P, EB, J], i32, c)
            slot_i = sb("slot_i", [P, ET], i32, c)
            slot_f = sb("slot_f", [P, ET], f32, c)
            home_i = sb("home_i", [P, ET], i32, c)
            home_f = sb("home_f", [P, ET], f32, c)
            pos_i = sb("pos_i", [P, NB, J], i32, c)
            val_stage = [sb(f"val_stage{k}", [P, J], i32, c) for k in range(2)]
            slots_written = counted("slots_written")
            slots_read = counted("slots_read")
            with nc.Block() as block:
                d0, s0, g0, k0 = setup_dma.base, setup_step.base, [g.base for g in gathered], staged.base

                @block.sync
                def _(sp):
                    sp.dma_start(src_i[:, :, :], cols_bj(src_pad[:])).then_inc(setup_dma.sem, 16)
                    sp.dma_start(dst_i[:, :, :], cols_bj(dst_pad[J:J + EP])).then_inc(setup_dma.sem, 16)
                    sp.wait_ge(slots_written.sem, 1)
                    sp.dma_start(pos_i[:, 0:NB - 1, :], pos_nodes[0:(NB - 1) * BLK, :].rearrange("(b p j) o -> p b (j o)", p=P, j=J)).then_inc(setup_dma.sem, 16)
                    sp.dma_start(pos_i[:, NB - 1, :], pos_nodes[N - BLK:N, :].rearrange("(p j) o -> p (j o)", j=J)).then_inc(setup_dma.sem, 16)

                @block.vector
                def _(dve):
                    dve.wait_ge(setup_dma.sem, d0 + 32)
                    dve.tensor_scalar(src_clamped[:, :], src_i[:, :, :].rearrange("p b j -> p (b j)"), float(N - 1), None, ALU.min).then_inc(setup_step.sem, 1)
                    dve.tensor_scalar(dst_clamped[:, :], dst_i[:, :, :].rearrange("p b j -> p (b j)"), float(N - 1), None, ALU.min).then_inc(setup_step.sem, 1)
                    dve.wait_ge(setup_dma.sem, d0 + 64)
                    dve.tensor_scalar(node_mask[:, :], pos_i[:, :, :].rearrange("p b j -> p (b j)"), float(BIG), None, ALU.is_equal).then_inc(setup_step.sem, 1)
                    dve.wait_ge(setup_step.sem, s0 + 4)
                    dve.memset(node_mask[0:max(OVER, 1), (NB - 1) * J:NB * J], 0.0).then_inc(setup_step.sem, 1)
                    dve.wait_ge(slots_read.sem, 1)
                    dve.tensor_scalar(slot_f[:, :], slot_i[:, :], 2.0, 1.0, ALU.mult, ALU.add).then_inc(setup_step.sem, 1)
                    dve.wait_ge(setup_step.sem, s0 + 6)
                    dve.tensor_copy(link_idx[:, :], slot_f[:, :]).then_inc(setup_step.sem, 1)
                    dve.tensor_scalar(home_f[:, :], home_i[:, :], 2.0, 1.0, ALU.mult, ALU.add).then_inc(setup_step.sem, 1)
                    dve.wait_ge(setup_step.sem, s0 + 8)
                    dve.tensor_copy(home_idx[:, :], home_f[:, :]).then_inc(setup_step.sem, 1)
                    dve.wait_ge(setup_step.sem, s0 + 9)

                @block.gpsimd
                def _(pool):
                    pool.iota(iota_edge[:, :], pattern=[[BLK, EB], [1, J]], base=0, channel_multiplier=J).then_inc(setup_step.sem, 1)
                    pool.wait_ge(setup_step.sem, s0 + 3)
                    with pool.Fori(0, EB) as b:
                        pool.tensor_copy(idx_stage[0][:, 0:J], last_dst_idx[:, ds(b * J, J)]).then_inc(staged.sem, 1)
                        pool.tensor_copy(val_stage[0][:, :], iota_edge[:, ds(b * J, J)]).then_inc(staged.sem, 1)
                        hold(pool, waits_passed, staged.sem, b * 2 + (k0 + 2))
                        for j in range(J):
                            pool.indirect_dma_start(pos_nodes[:, :], bass.IndirectOffsetOnAxis(idx_stage[0][:, j:j + 1], 0),
                                                    val_stage[0][:, j:j + 1], None, bounds_check=N - 1,
                                                    oob_is_err=False).then_inc(gathered[0].sem, 16)
                        hold(pool, waits_passed, gathered[0].sem, b * (16 * J) + (g0[0] + 16 * J))
                    pool.wait_ge(gathered[0].sem, g0[0] + 16 * J * EB)
                    pool.nop().then_inc(slots_written.sem, 1)
                    for n, (table, found) in enumerate(((src_clamped, slot_i), (dst_clamped, home_i))):
                        k1 = k0 + 2 * EB * (n + 1)
                        g1 = g0[1] + 16 * J * EB * n
                        with pool.Fori(0, EB) as b:
                            pool.tensor_copy(idx_stage[0][:, 0:J], table[:, ds(b * J, J)]).then_inc(staged.sem, 1)
                            hold(pool, waits_passed, staged.sem, b * 2 + (k1 + 1))
                            for j in range(J):
                                pool.indirect_dma_start(val_stage[1][:, j:j + 1], None, pos_nodes[:, :],
                                                        bass.IndirectOffsetOnAxis(idx_stage[0][:, j:j + 1], 0),
                                                        bounds_check=N - 1, oob_is_err=False).then_inc(gathered[1].sem, 16)
                            hold(pool, waits_passed, gathered[1].sem, b * (16 * J) + (g1 + 16 * J))
                            pool.tensor_copy(found[:, ds(b * J, J)], val_stage[1][:, :]).then_inc(staged.sem, 1)
                            hold(pool, waits_passed, staged.sem, b * 2 + (k1 + 2))
                    pool.nop().then_inc(slots_read.sem, 1)
            setup_dma.base += 64
            setup_step.base += 9
            staged.base += 6 * EB
            gathered[0].base += 16 * J * EB
            gathered[1].base += 2 * 16 * J * EB

        with ExitStack() as c:
            rec_i = sb("rec_i", [P, EB, J, 2], i32, c)
            tile_major = [sb(f"sort_keys{k}", [P, ET], i32, c) for k in range(2)]
            digit_i = sb("digit_i", [P, ET], i32, c)
            digit = sb("digit", [P, ET], bf16, c)
            digit_iota = sb("digit_iota", [P, RADIX], bf16, c)
            onehot = sb("onehot", [P, ET * RADIX], bf16, c)
            earlier = sb("earlier", [P, P], bf16, c)
            ones_bf = sb("ones_bf", [P, P], bf16, c)
            counts = sb("counts", [P, RADIX * ET], f32, c)
            place = sb("place", [P, ET * RADIX], f32, c)
            rank = sb("rank", [P, ET], f32, c)
            rank_i = [sb(f"rank_i{k}", [P, ET], i32, c) for k in range(4)]
            rec_stage = sb("rec_stage", [P, J, 2], i32, c)
            rank_made = counted("rank_made")
            src_i_again = sb("src_i_again", [P, EB, J], i32, c)
            iota_again = sb("iota_again", [P, ET], i32, c)
            setup_edge = counted("sort_constants")
            setup_edge0 = counted("sort_zeros")
            TPC = 512 // RADIX
            NCH = ET // TPC
            for n_pass in range(PASSES):
                last_pass = n_pass == PASSES - 1
                with nc.Block() as block:
                    d0, s0, g0, k0 = setup_dma.base, setup_step.base, gathered[0].base, staged.base
                    c0, r0 = chain[0].base, chain[1].base
                    m0 = rank_made.base

                    @block.sync
                    def _(sp):
                        if n_pass:
                            sp.dma_start(rec_i[:, :, :, :], sorting[(n_pass - 1) % 2].rearrange("(b p j) t -> p b (j t)", p=P, j=J)).then_inc(setup_dma.sem, 16)
                        else:
                            sp.dma_start(src_i_again[:, :, :], cols_bj(src_pad[:])).then_inc(setup_dma.sem, 16)

                    @block.vector
                    def _(dve):
                        step = [s0]

                        def link(op):
                            step[0] += 1
                            op.then_inc(setup_step.sem, 1)
                            dve.wait_ge(setup_step.sem, step[0])

                        dve.wait_ge(setup_dma.sem, d0 + 16)
                        if n_pass == 0:
                            dve.wait_ge(setup_edge.sem, 4)
                            link(dve.tensor_copy(rec_i[:, :, :, 0], src_i_again[:, :, :]))
                            link(dve.tensor_copy(rec_i[:, :, :, 1], iota_again[:, :].rearrange("p (b j) -> p b j", j=J)))
                        keys = rec_i[:, :, :, 0].rearrange("p b j -> p (b j)")
                        link(dve.tensor_copy(tile_major[0][:, :], keys))
                        link(dve.tensor_scalar(digit_i[:, :], tile_major[0][:, :], DIGIT * n_pass, RADIX - 1,
                                               ALU.logical_shift_right, ALU.bitwise_and))
                        link(dve.tensor_copy(digit[:, :], digit_i[:, :]))
                        link(dve.tensor_tensor(onehot[:, :].rearrange("p (t r) -> p t r", r=RADIX),
                                               digit[:, :].unsqueeze(2).broadcast_to([P, ET, RADIX]),
                                               digit_iota[:, :].unsqueeze(1).broadcast_to([P, ET, RADIX]), ALU.is_equal))
                        dve.wait_ge(chain[1].sem, r0 + NCH)
                        link(dve.tensor_tensor_scan(counts[:, :], counts[:, :], counts[:, :], 0.0, ALU.add, ALU.bypass))
                        for k in range(NCH):
                            dve.wait_ge(chain[2].sem, chain[2].base + k + 1)
                            bank = work[:, (3 + k % 3) * 512:(4 + k % 3) * 512]
                            dve.tensor_tensor(place[:, k * 512:(k + 1) * 512].rearrange("p (t r) -> p t r", r=RADIX),
                                              bank.rearrange("p (t r) -> p t r", r=RADIX),
                                              counts[:, :].rearrange("p (r t) -> p t r", r=RADIX)[:, k * TPC:(k + 1) * TPC, :],
                                              ALU.add).then_inc(rank_made.sem, 1)
                        dve.wait_ge(rank_made.sem, m0 + NCH)
                        link(dve.tensor_tensor(place[:, :], place[:, :], onehot[:, :], ALU.mult))
                        link(dve.tensor_reduce(rank[:, :], place[:, :].rearrange("p (t r) -> p t r", r=RADIX), AX, ALU.add))
                        link(dve.tensor_copy(rank_i[0][:, :], rank[:, :]))
                        if last_pass:
                            link(dve.tensor_copy(rank_i[3][:, :], rank_i[0][:, :]))
                        else:
                            link(dve.tensor_scalar(rank_i[1][:, :], rank_i[0][:, :], P - 1, J.bit_length() - 1, ALU.bitwise_and, ALU.logical_shift_left))
                            link(dve.tensor_scalar(rank_i[2][:, :], rank_i[0][:, :], P.bit_length() - 1, J - 1, ALU.logical_shift_right, ALU.bitwise_and))
                            link(dve.tensor_tensor(rank_i[1][:, :], rank_i[1][:, :], rank_i[2][:, :], ALU.bitwise_or))
                            link(dve.tensor_scalar(rank_i[2][:, :], rank_i[0][:, :], BLK.bit_length() - 1, BLK.bit_length() - 1, ALU.logical_shift_right, ALU.logical_shift_left))
                            link(dve.tensor_tensor(rank_i[3][:, :], rank_i[1][:, :], rank_i[2][:, :], ALU.bitwise_or))
                        step_total[0] = step[0]

                    onehot_step = s0 + (6 if n_pass == 0 else 4)

                    @block.tensor
                    def _(pe):
                        pe.wait_ge(setup_step.sem, onehot_step)
                        for k in range(NCH):
                            if k >= 3:
                                pe.wait_ge(chain[1].sem, r0 + k - 2)
                            pe.matmul(work[:, (k % 3) * 512:(k % 3 + 1) * 512], ones_bf[:, :], onehot[:, k * 512:(k + 1) * 512],
                                      start=True, stop=True).then_inc(chain[0].sem, 1)
                        for k in range(NCH):
                            if k >= 3:
                                pe.wait_ge(rank_made.sem, m0 + k - 2)
                            pe.matmul(work[:, (3 + k % 3) * 512:(4 + k % 3) * 512], earlier[:, :], onehot[:, k * 512:(k + 1) * 512],
                                      start=True, stop=True).then_inc(chain[2].sem, 1)

                    @block.scalar
                    def _(act):
                        for k in range(NCH):
                            act.wait_ge(chain[0].sem, c0 + k + 1)
                            act.activation(counts[:, :].rearrange("p (r t) -> p t r", r=RADIX)[:, k * TPC:(k + 1) * TPC, :],
                                           work[:, (k % 3) * 512:(k % 3 + 1) * 512].rearrange("p (t r) -> p t r", r=RADIX),
                                           ACT.Copy).then_inc(chain[1].sem, 1)

                    n_links = 7 + (2 if n_pass == 0 else 0) + 2 + (1 if last_pass else 5)
                    rank_step = s0 + (6 if n_pass == 0 else 4) + 1 + 3 + (1 if last_pass else 5)

                    @block.gpsimd
                    def _(pool):
                        if n_pass == 0:
                            pool.iota(iota_again[:, :], pattern=[[BLK, EB], [1, J]], base=0, channel_multiplier=J).then_inc(setup_edge.sem, 1)
                            pool.iota(digit_iota[:, :], pattern=[[1, RADIX]], base=0, channel_multiplier=0,
                                      allow_small_or_imprecise_dtypes=True).then_inc(setup_edge.sem, 1)
                            pool.memset(ones_bf[:, :], 1.0).then_inc(setup_edge.sem, 1)
                            pool.memset(earlier[:, :], 0.0).then_inc(setup_edge0.sem, 1)
                            pool.wait_ge(setup_edge0.sem, 1)
                            pool.affine_select(out=earlier[:, :], in_=earlier[:, :], compare_op=ALU.is_gt, fill=-1.0,
                                               base=0, pattern=[[1, P]], channel_multiplier=-1).then_inc(setup_edge.sem, 1)
                        pool.wait_ge(setup_step.sem, rank_step)
                        with pool.Fori(0, EB) as b:
                            pool.tensor_copy(idx_stage[0][:, 0:J], rank_i[3][:, ds(b * J, J)]).then_inc(staged.sem, 1)
                            pool.tensor_copy(rec_stage[:, :, :].rearrange("p j t -> p (j t)"),
                                             rec_i[:, :, :, :].rearrange("p b j t -> p (b j t)")[:, ds(b * (2 * J), 2 * J)]).then_inc(staged.sem, 1)
                            hold(pool, waits_passed, staged.sem, b * 2 + (k0 + 2))
                            for j in range(J):
                                pool.indirect_dma_start(sorting[n_pass % 2][:, :], bass.IndirectOffsetOnAxis(idx_stage[0][:, j:j + 1], 0),
                                                        rec_stage[:, j, :], None, bounds_check=EP - 1,
                                                        oob_is_err=False).then_inc(gathered[0].sem, 16)
                            hold(pool, waits_passed, gathered[0].sem, b * (16 * J) + (g0 + 16 * J))
                        pool.wait_ge(gathered[0].sem, g0 + 16 * J * EB)
                assert step_total[0] == rank_step, (step_total[0], rank_step)
                setup_step.base = step_total[0]
                setup_dma.base += 16
                chain[0].base += NCH
                chain[1].base += NCH
                chain[2].base += NCH
                rank_made.base += NCH
                staged.base += 2 * EB
                gathered[0].base += 16 * J * EB

            key_lin = sb("key_lin", [P, EB, J], i32, c)
            with nc.Block() as block:
                d0, s0 = setup_dma.base, setup_step.base

                @block.sync
                def _(sp):
                    sp.dma_start(rec_i[:, :, :, :], sorting[(PASSES - 1) % 2].rearrange("(b p j) t -> p b (j t)", p=P, j=J)).then_inc(setup_dma.sem, 16)
                    sp.wait_ge(setup_step.sem, s0 + 2)
                    sp.dma_start(cols_bj(key_pad[J:J + EP]), key_lin[:, :, :]).then_inc(setup_dma.sem, 16)
                    sp.wait_ge(setup_dma.sem, d0 + 32)

                @block.vector
                def _(dve):
                    dve.wait_ge(setup_dma.sem, d0 + 16)
                    dve.tensor_copy(key_lin[:, :, :], rec_i[:, :, :, 0]).then_inc(setup_step.sem, 1)
                    dve.tensor_copy(sorted_edge[:, :], rec_i[:, :, :, 1].rearrange("p b j -> p (b j)")).then_inc(setup_step.sem, 1)
            setup_dma.base += 32
            setup_step.base += 2
        with ExitStack() as c:
            rep_src = sb("rep_src", [P, ET], f32, c)
            segment_phase(key_pad, "key", False, attn_out_idx[:, :], rep_src[:, :], neg_start)
        def lane_tiles(name, lanes, width=BLK):
            return [sb(f"{name}{k}", [P, width]) for k in range(lanes)]

        rows_in = lane_tiles("rows_in", DL)
        centered = lane_tiles("centered", DL)
        squares = lane_tiles("squares", DL)
        feat = lane_tiles("feat", DL)
        feat_out = lane_tiles("feat_out", DL)
        rows_out = lane_tiles("rows_out", DL)
        resid = lane_tiles("resid", DL)
        masked = lane_tiles("masked", DL, J * (D + 1))
        stats = lane_tiles("stats", DL, 4 * 2 * J)
        agg = lane_tiles("agg", EL)
        mean_agg = lane_tiles("mean_agg", EL)
        flags = lane_tiles("flags", EL)
        inverse = lane_tiles("inverse", EL)
        edge_in = lane_tiles("edge_in", EL)
        edge_rows = lane_tiles("edge_rows", EL)
        running_max = lane_tiles("running_max", EL, BLK + 1)
        record_rows = lane_tiles("record_rows", EL, J * REC)
        moments = sb("moments", [D, D + 1])
        moments_edges = sb("moments_edges", [D, D + 1])
        w1_moments = sb("w1_moments", [D, H])
        coef = sb("coef", [P, 8])
        zeros = sb("zeros", [P, 2 * D])

        class Steps:

            def __init__(self, names, lanes, blocks, loads=0, more=0, stores=1, gathers=0):
                self.names, self.K, self.lanes = names, len(names), lanes
                self.rounds, self.rest = blocks // lanes, blocks % lanes
                self.per = dict(loaded=16 * loads, more=16 * more, stored=16 * stores, gathered=16 * gathers)
                self.base = [s.base for s in chain]
                self.at = {k: [s.base for s in sems] for k, sems in lane_sems.items()}

            def after(self, lane, i, name):
                return i * self.K + (self.base[lane] + self.names.index(name) + 1)

            def start(self, lane, i):
                return i * self.K + self.base[lane]

            def dma(self, what, lane, i, rounds=1):
                return i * self.per[what] + (self.at[what][lane] + rounds * self.per[what])

            def run(self, engine, body):
                if self.rounds:
                    with engine.Fori(0, self.rounds) as i:
                        body(i, range(self.lanes))
                if self.rest:
                    body(self.rounds, range(self.rest))

            def close(self):
                for k in range(self.lanes):
                    n = self.rounds + (k < self.rest)
                    chain[k].base += n * self.K
                    for what, sems in lane_sems.items():
                        sems[k].base += n * self.per[what]

        more_loaded = [counted(f"lane{k}_more_loaded") for k in range(DL)]
        lane_sems = dict(loaded=loaded, more=more_loaded, stored=stored, gathered=gathered)
        gather_ready = [counted(f"lane{k}_gather_indices") for k in range(DL)]
        scattered = [counted(f"lane{k}_scattered") for k in range(EL)]
        scatter_done = [counted(f"lane{k}_scatter_done") for k in range(EL)]
        resid_saved = [counted(f"lane{k}_residual_saved") for k in range(DL)]

        LN = ["ln_sum", "ln_center", "ln_square", "ln_var", "ln_root", "ln_inverse", "ln_out"]

        def ln_vector(dve, S, lane, i, pre, first, src, T, tag=""):
            x = src[:, 0:T * D].rearrange("p (t d) -> p t d", d=D)
            c = centered[lane][:, 0:T * D].rearrange("p (t d) -> p t d", d=D)
            q = squares[lane][:, 0:T * D].rearrange("p (t d) -> p t d", d=D)
            st = stats[lane]
            total, var, inv = st[:, 0:T], st[:, 16:16 + T], st[:, 32:32 + T]
            first()
            dve.tensor_reduce(total, x, AX, ALU.add).then_inc(chain[lane].sem, 1)
            dve.wait_ge(chain[lane].sem, S.after(lane, i, tag + "ln_sum"))
            dve.scalar_tensor_tensor(c, total.unsqueeze(2).broadcast_to([P, T, D]), -1.0 / D, x, ALU.mult,
                                     ALU.add).then_inc(chain[lane].sem, 1)
            dve.wait_ge(chain[lane].sem, S.after(lane, i, tag + "ln_square"))
            dve.tensor_reduce(var, q, AX, ALU.add).then_inc(chain[lane].sem, 1)
            dve.wait_ge(chain[lane].sem, S.after(lane, i, tag + "ln_root"))
            dve.reciprocal(inv, st[:, 48:48 + T]).then_inc(chain[lane].sem, 1)
            dve.wait_ge(chain[lane].sem, S.after(lane, i, tag + "ln_inverse"))
            dve.scalar_tensor_tensor(c, c, 0.0, inv.unsqueeze(2).broadcast_to([P, T, D]), ALU.max,
                                     ALU.mult).then_inc(chain[lane].sem, 1)

        def ln_scalar(act, S, lane, i, T, tag=""):
            st = stats[lane]
            act.wait_ge(chain[lane].sem, S.after(lane, i, tag + "ln_center"))
            act.activation(squares[lane][:, 0:T * D], centered[lane][:, 0:T * D], ACT.Square).then_inc(chain[lane].sem, 1)
            act.wait_ge(chain[lane].sem, S.after(lane, i, tag + "ln_var"))
            act.activation(st[:, 48:48 + T], st[:, 16:16 + T], ACT.Sqrt, bias=eps_ln[:, :],
                           scale=1.0 / D).then_inc(chain[lane].sem, 1)

        def edge_psum(lane):
            return work[:, lane * 1536:lane * 1536 + 1024], work[:, lane * 1536 + 1024:(lane + 1) * 1536]

        def node_psum(lane):
            return work[:, lane * 1024:lane * 1024 + 512], work[:, lane * 1024 + 512:(lane + 1) * 1024]

        def tiles_of(tile, j):
            return tile.rearrange("f (p j) -> f j p", j=J)[:, j, :]

        def in_order(tile):
            return tile.rearrange("f (p j) -> f p j", j=J)

        def by_tile(bank):
            return bank.rearrange("f (j p) -> f p j", p=P)

        cleared = agg + mean_agg + feat_out + running_max + record_rows + masked + edge_rows + edge_in + [zeros]
        lane_counts = chain + loaded + more_loaded + stored + scatter_done + gather_ready + resid_saved
        with nc.Block() as block:
            @block.vector
            def _(dve):
                for tile in cleared:
                    dve.memset(tile[:, :], 0.0).then_inc(setup_step.sem, 1)
                dve.wait_ge(setup_step.sem, setup_step.base + len(cleared))

            @block.gpsimd
            def _(pool):
                for c in lane_counts:
                    pool.sem_inc(c.sem, 64)
        setup_step.base += len(cleared)
        for c in lane_counts:
            c.base += 64

        def edge_phase(kind, l, source, tin, tout, ln=False, add_resid=False):
            names = list(LN) if ln else []
            names += ["t_in", "feat"]
            if kind == "gnn":
                names += ["edge_mm", "edge_act"] if l > 0 else ["edge_t", "edge_feat"]
                names += ["edge_pair", "msg_mm", "msg_act"]
            if kind in ("sage", "gnn"):
                names += ["scan", "mean"]
            if kind in ("sage", "gnn", "proj"):
                names += ["mm", "act", "t_out"]
                if kind == "gnn":
                    names += ["l2_square", "l2_sum", "l2_root", "l2_floor", "l2_inverse"]
                names += ["rows"]
                if kind == "gnn" and add_resid:
                    names += ["add_resid"]
            if kind == "gin":
                names += ["scan", "z", "z_rows", "z_masked", "z_mask", "gram"]
            if kind == "qkv":
                names += ["qkv", "q_bias", "k_bias", "v_bias", "q_times_k", "dot", "score", "max_score"]
            last = names[-1]
            scans = kind in ("sage", "gnn", "gin")
            homes = source == "links" and kind in ("qkv", "gnn")
            gathers = {"nodes": 2 * J, "attention": 2 * J, "links": J * (1 + homes), "rows": 0}[source]
            save_resid = ln
            n_more = 2 * (kind in ("sage", "gnn")) + (kind == "gin") + add_resid + (kind == "gnn")
            n_load = int(source in ("links", "rows"))
            n_store = {"sage": 1, "proj": 1, "qkv": 1, "gin": 2, "gnn": 1 + (l < 2)}[kind]
            S = Steps(names, EL, EB, loads=n_load, more=n_more, stores=n_store, gathers=gathers)
            stage0 = [g.base for g in gather_ready]
            saved0 = [g.base for g in resid_saved]
            nodes = {"nodes": t["x"], "attention": attn_nodes, "links": None, "rows": None}[source]
            slots = tin.rearrange("e (h d) -> (e h) d", h=2) if source == "links" else None
            reads_rows = "ln_center" if ln else "t_in"
            relu = ACT.Relu if kind != "proj" else ACT.Identity
            w = {"sage": sage, "gnn": gnn, "proj": [dict(own=w_o, agg=None, bias=b_o)], "gin": gin, "qkv": [None] * 3}[kind]
            w = w[0] if kind == "proj" else w[l]

            with nc.Block() as block:
                @block.sync
                def _(sp):
                    if kind == "gnn" and l == 0:
                        pass

                    def body(i, lanes):
                        for lane in lanes:
                            b = i * EL + lane
                            if n_load:
                                hold(sp, waits_passed_sp, chain[lane].sem, S.after(lane, i - 1, reads_rows))
                                if save_resid:
                                    hold(sp, waits_passed_sp, resid_saved[lane].sem, i * 16 + saved0[lane])
                                sp.dma_start(rows_in[lane][:, :].rearrange("p (j d) -> p j d", j=J), rows(tin, b)).then_inc(loaded[lane].sem, 16)
                        for lane in lanes:
                            b = i * EL + lane
                            hold(sp, waits_passed_sp, chain[lane].sem, S.start(lane, i))
                            if kind == "gnn" and l > 0:
                                hold(sp, waits_passed_sp, stored[lane].sem, S.dma("stored", lane, i, rounds=0))
                            if kind in ("sage", "gnn", "gin"):
                                sp.dma_start(flags[lane][0:D, :], same_dst[ds(b * BLK, BLK)].partition_broadcast(D)).then_inc(more_loaded[lane].sem, 16)
                            if kind in ("sage", "gnn"):
                                sp.dma_start(inverse[lane][0:D, :], inv_deg[ds(b * BLK, BLK)].partition_broadcast(D)).then_inc(more_loaded[lane].sem, 16)
                            if add_resid:
                                sp.dma_start(resid[lane][:, :].rearrange("p (j d) -> p j d", j=J), rows(sd_resid, b)).then_inc(more_loaded[lane].sem, 16)
                            if kind == "gnn":
                                if l > 0:
                                    sp.dma_start(edge_in[lane][D:P, :], edge_state[ds(b, 1), :, :].rearrange("o f e -> (o f) e")).then_inc(more_loaded[lane].sem, 16)
                                elif isinstance(i, int) and i * EL + lane == EB - 1:
                                    n_last = (E - (EB - 1) * BLK) // J
                                    sp.dma_start(edge_rows[lane][0:n_last, :].rearrange("p (j d) -> p j d", j=J)[:, :, D:P],
                                                 t["edge_attr_64"][(EB - 1) * BLK:E, :].rearrange("(p j) d -> p j d", j=J)).then_inc(more_loaded[lane].sem, 16)
                                else:
                                    sp.dma_start(edge_rows[lane][:, :].rearrange("p (j d) -> p j d", j=J)[:, :, D:P],
                                                 rows(t["edge_attr_64"], b)).then_inc(more_loaded[lane].sem, 16)
                    S.run(sp, body)

                @block.gpsimd
                def _(pool):
                    def body(i, lanes):
                        for lane in lanes:
                            b = i * EL + lane
                            if source == "rows":
                                continue
                            if source == "links":
                                tables = [(link_idx, 0)] + [(home_idx, D)] * homes
                                hold(pool, waits_passed, loaded[lane].sem, S.dma("loaded", lane, i))
                            else:
                                tables = [(src_clamped, 0), (dst_clamped, D)]
                                hold(pool, waits_passed, chain[lane].sem, S.after(lane, i - 1, reads_rows))
                                if save_resid:
                                    hold(pool, waits_passed, resid_saved[lane].sem, i * 16 + saved0[lane])
                            hold(pool, waits_passed, gathered[lane].sem, S.dma("gathered", lane, i, rounds=0))
                            for k, (table, _) in enumerate(tables):
                                pool.tensor_copy(idx_stage[lane][:, k * J:(k + 1) * J], table[:, ds(b * J, J)]).then_inc(gather_ready[lane].sem, 1)
                            hold(pool, waits_passed, gather_ready[lane].sem, i * len(tables) + (stage0[lane] + len(tables)))
                            for k, (_, at) in enumerate(tables):
                                for j in range(J):
                                    pool.indirect_dma_start(
                                        rows_in[lane][:, j * P + at:j * P + at + D], None, slots if source == "links" else nodes[:, :],
                                        bass.IndirectOffsetOnAxis(idx_stage[lane][:, k * J + j:k * J + j + 1], 0),
                                        bounds_check=(2 * EP - 1) if source == "links" else N - 1,
                                        oob_is_err=False).then_inc(gathered[lane].sem, 16)
                    S.run(pool, body)

                def rows_ready(engine, lane, i):
                    if gathers:
                        engine.wait_ge(gathered[lane].sem, S.dma("gathered", lane, i))
                    else:
                        engine.wait_ge(loaded[lane].sem, S.dma("loaded", lane, i))

                @block.tensor
                def _(pe):
                    if kind == "gin":
                        pe.matmul(gram_edges[0:D, 0:D + 1], zeros[:, 0:D], zeros[:, 0:D + 1], start=True, stop=True)

                    def body(i, lanes):
                        for lane in lanes:
                            A, B = edge_psum(lane)
                            if ln:
                                pe.wait_ge(chain[lane].sem, S.after(lane, i, "ln_out"))
                            else:
                                pe.wait_ge(chain[lane].sem, S.start(lane, i))
                                rows_ready(pe, lane, i)
                            src = centered[lane] if ln else rows_in[lane]
                            for j in range(J):
                                op = pe.transpose(A[:, j * P:(j + 1) * P], src[:, j * P:(j + 1) * P], ident[:, :])
                            op.then_inc(chain[lane].sem, 1)
                        if kind == "gnn":
                            for lane in lanes:
                                A, B = edge_psum(lane)
                                pe.wait_ge(chain[lane].sem, S.after(lane, i, "feat"))
                                pe.wait_ge(more_loaded[lane].sem, S.dma("more", lane, i))
                                if l == 0:
                                    for j in range(J):
                                        op = pe.transpose(A[:, j * P:(j + 1) * P], edge_rows[lane][:, j * P:(j + 1) * P], ident[:, :])
                                else:
                                    for h in range(2):
                                        c = slice(h * 512, (h + 1) * 512)
                                        pe.matmul(A[:, c], w["edge_nodes"][:, :], feat[lane][:, c], start=True, stop=False)
                                        op = pe.matmul(A[:, c], w["edge_own"][:, :], edge_in[lane][:, c], start=False, stop=True)
                                op.then_inc(chain[lane].sem, 1)
                            for lane in lanes:
                                A, B = edge_psum(lane)
                                pe.wait_ge(chain[lane].sem, S.after(lane, i, "edge_pair"))
                                for h in range(2):
                                    c = slice(h * 512, (h + 1) * 512)
                                    op = pe.matmul(A[0:D, c], w["msg"][:, :], edge_in[lane][:, c], start=True, stop=True)
                                op.then_inc(chain[lane].sem, 1)
                        if kind in ("sage", "gnn", "proj"):
                            for lane in lanes:
                                A, B = edge_psum(lane)
                                pe.wait_ge(chain[lane].sem, S.after(lane, i, "feat" if kind == "proj" else "mean"))
                                for h in range(2):
                                    c = slice(h * 512, (h + 1) * 512)
                                    op = pe.matmul(A[:, c], w["own"][:, :], feat[lane][:, c], start=True, stop=kind == "proj")
                                    if kind != "proj":
                                        op = pe.matmul(A[:, c], w["agg"][0:D, :], mean_agg[lane][0:D, c], start=False, stop=True)
                                op.then_inc(chain[lane].sem, 1)
                            for lane in lanes:
                                A, B = edge_psum(lane)
                                pe.wait_ge(chain[lane].sem, S.after(lane, i, "act"))
                                for j in range(J):
                                    op = pe.transpose(A[:, j * P:(j + 1) * P], tiles_of(feat_out[lane][:, :], j), ident[:, :])
                                op.then_inc(chain[lane].sem, 1)
                        if kind == "gin":
                            for lane in lanes:
                                A, B = edge_psum(lane)
                                pe.wait_ge(chain[lane].sem, S.after(lane, i, "scan"))
                                for j in range(J):
                                    c = slice(j * D, (j + 1) * D)
                                    pe.matmul(B[:, c], tiles_of(feat[lane][:, :], j), w["keep_ident"][:, :], start=True, stop=False)
                                    op = pe.matmul(B[:, c], tiles_of(agg[lane][0:D, :], j), ident[0:D, 0:D], start=False, stop=True)
                                op.then_inc(chain[lane].sem, 1)
                            for lane in lanes:
                                pe.wait_ge(chain[lane].sem, S.after(lane, i, "z_mask"))
                                zm = masked[lane][:, :].rearrange("p (j d) -> p j d", j=J)
                                for j in range(J):
                                    op = pe.matmul(gram_edges[0:D, 0:D + 1], squares[lane][:, j * D:(j + 1) * D], zm[:, j, :],
                                                   start=False, stop=False, skip_group_check=True)
                                op.then_inc(chain[lane].sem, 1)
                        if kind == "qkv":
                            for lane in lanes:
                                A, B = edge_psum(lane)
                                pe.wait_ge(chain[lane].sem, S.after(lane, i, "feat"))
                                for j in range(J):
                                    c = slice(j * D, (j + 1) * D)
                                    pe.matmul(B[:, c], tiles_of(feat[lane][0:D, :], j), w_qkv[0:D, 0:D], start=True, stop=True)
                                    pe.matmul(A[:, j * D:(j + 1) * D], tiles_of(feat[lane][D:P, :], j), w_qkv[D:P, 0:D], start=True, stop=True)
                                    op = pe.matmul(A[:, 512 + j * D:512 + (j + 1) * D], tiles_of(feat[lane][D:P, :], j), w_qkv[D:P, D:2 * D], start=True, stop=True)
                                op.then_inc(chain[lane].sem, 1)
                    S.run(pe, body)

                @block.scalar
                def _(act):
                    def body(i, lanes):
                        if save_resid:
                            for lane in lanes:
                                b = i * EL + lane
                                rows_ready(act, lane, i)
                                act.dma_start(rows(sd_resid, b), rows_in[lane][:, :].rearrange("p (j d) -> p j d", j=J)).then_inc(resid_saved[lane].sem, 16)
                        if ln:
                            for lane in lanes:
                                ln_scalar(act, S, lane, i, 2 * J)
                        for lane in lanes:
                            A, B = edge_psum(lane)
                            act.wait_ge(chain[lane].sem, S.after(lane, i, "t_in"))
                            if kind == "gin":
                                act.wait_ge(stored[lane].sem, S.dma("stored", lane, i, rounds=0))
                            act.activation(in_order(feat[lane][:, :]), by_tile(A), ACT.Copy).then_inc(chain[lane].sem, 1)
                        if kind == "gnn":
                            for lane in lanes:
                                A, B = edge_psum(lane)
                                if l == 0:
                                    act.wait_ge(chain[lane].sem, S.after(lane, i, "edge_t"))
                                    act.wait_ge(stored[lane].sem, S.dma("stored", lane, i, rounds=0))
                                    act.activation(in_order(edge_in[lane][D:P, :]), by_tile(A)[D:P], ACT.Copy).then_inc(chain[lane].sem, 1)
                                else:
                                    act.wait_ge(chain[lane].sem, S.after(lane, i, "edge_mm"))
                                    act.activation(edge_in[lane][D:P, :], A[D:P, :], ACT.Relu, bias=w["edge_b"][D:P, :]).then_inc(chain[lane].sem, 1)
                            for lane in lanes:
                                act.wait_ge(chain[lane].sem, S.after(lane, i, "edge_act" if l else "edge_feat"))
                                act.activation(edge_in[lane][0:D, :], feat[lane][0:D, :], ACT.Copy).then_inc(chain[lane].sem, 1)
                            for lane in lanes:
                                b = i * EL + lane
                                if l < 2:
                                    act.dma_start(edge_state[ds(b, 1), :, :].rearrange("o f e -> (o f) e"), edge_in[lane][D:P, :]).then_inc(stored[lane].sem, 16)
                            for lane in lanes:
                                A, B = edge_psum(lane)
                                act.wait_ge(chain[lane].sem, S.after(lane, i, "msg_mm"))
                                act.activation(running_max[lane][0:D, 0:BLK], A[0:D, :], ACT.Relu, bias=w["msg_b"][0:D, :]).then_inc(chain[lane].sem, 1)
                        if kind in ("sage", "gnn", "proj"):
                            for lane in lanes:
                                A, B = edge_psum(lane)
                                act.wait_ge(chain[lane].sem, S.after(lane, i, "mm"))
                                act.activation(feat_out[lane][:, :], A, relu, bias=w["bias"][:, :]).then_inc(chain[lane].sem, 1)
                            if kind == "gnn":
                                for lane in lanes:
                                    A, B = edge_psum(lane)
                                    act.wait_ge(chain[lane].sem, S.after(lane, i, "t_out"))
                                    act.activation(squares[lane][:, :], A, ACT.Square).then_inc(chain[lane].sem, 1)
                                for lane in lanes:
                                    act.wait_ge(chain[lane].sem, S.after(lane, i, "l2_sum"))
                                    act.activation(stats[lane][:, 16:32], stats[lane][:, 0:16], ACT.Sqrt).then_inc(chain[lane].sem, 1)
                            for lane in lanes:
                                b = i * EL + lane
                                act.wait_ge(chain[lane].sem, S.after(lane, i, last))
                                act.dma_start(rows(tout, b), rows_out[lane][:, :].rearrange("p (j d) -> p j d", j=J)).then_inc(stored[lane].sem, 16)
                        if kind == "gin":
                            for lane in lanes:
                                b = i * EL + lane
                                act.wait_ge(chain[lane].sem, S.after(lane, i, "scan"))
                                act.dma_start(gin_x[ds(b, 1), :, :].rearrange("o f e -> (o f) e"), feat[lane][:, :]).then_inc(stored[lane].sem, 16)
                                act.dma_start(gin_agg[ds(b, 1), :, :].rearrange("o f e -> (o f) e"), agg[lane][0:D, :]).then_inc(stored[lane].sem, 16)
                        if kind == "qkv":
                            for lane in lanes:
                                b = i * EL + lane
                                act.wait_ge(chain[lane].sem, S.after(lane, i, last))
                                act.dma_start(rows(records, b), record_rows[lane][:, :].rearrange("p (j d) -> p j d", j=J)).then_inc(stored[lane].sem, 16)
                    S.run(act, body)
                    for lane in range(EL):
                        n = S.rounds + (lane < S.rest)
                        act.wait_ge(stored[lane].sem, S.at["stored"][lane] + n * S.per["stored"])
                        if save_resid:
                            act.wait_ge(resid_saved[lane].sem, saved0[lane] + 16 * n)

                @block.vector
                def _(dve):
                    def body(i, lanes):
                        if ln:
                            for lane in lanes:
                                def first():
                                    dve.wait_ge(chain[lane].sem, S.start(lane, i))
                                    rows_ready(dve, lane, i)
                                ln_vector(dve, S, lane, i, None, first, rows_in[lane], 2 * J)
                        if scans:
                            for lane in lanes:
                                msg = running_max[lane][0:D, 0:BLK] if kind == "gnn" else feat[lane][0:D, :]
                                dve.wait_ge(chain[lane].sem, S.after(lane, i, "msg_act" if kind == "gnn" else "feat"))
                                dve.wait_ge(more_loaded[lane].sem, S.dma("more", lane, i))
                                if kind == "gin":
                                    dve.wait_ge(stored[lane].sem, S.dma("stored", lane, i, rounds=0))
                                if lane == 0:
                                    dve.wait_ge(chain[EL - 1].sem, S.after(EL - 1, i - 1, "scan"))
                                else:
                                    dve.wait_ge(chain[lane - 1].sem, S.after(lane - 1, i, "scan"))
                                before = agg[(lane - 1) % EL]
                                dve.tensor_tensor_scan(agg[lane][0:D, :], flags[lane][0:D, :], msg, before[0:D, BLK - 1:BLK],
                                                       ALU.mult, ALU.add).then_inc(chain[lane].sem, 1)
                        if kind in ("sage", "gnn"):
                            for lane in lanes:
                                dve.wait_ge(chain[lane].sem, S.after(lane, i, "scan"))
                                dve.tensor_tensor(mean_agg[lane][0:D, :], agg[lane][0:D, :], inverse[lane][0:D, :], ALU.mult).then_inc(chain[lane].sem, 1)
                        if kind in ("sage", "proj"):
                            for lane in lanes:
                                A, B = edge_psum(lane)
                                dve.wait_ge(chain[lane].sem, S.after(lane, i, "t_out"))
                                dve.wait_ge(stored[lane].sem, S.dma("stored", lane, i, rounds=0))
                                if add_resid:
                                    dve.wait_ge(more_loaded[lane].sem, S.dma("more", lane, i))
                                    dve.tensor_tensor(rows_out[lane][:, :], A, resid[lane][:, :], ALU.add).then_inc(chain[lane].sem, 1)
                                else:
                                    dve.tensor_copy(rows_out[lane][:, :], A).then_inc(chain[lane].sem, 1)
                        if kind == "gnn":
                            for lane in lanes:
                                A, B = edge_psum(lane)
                                st = stats[lane]
                                dve.wait_ge(chain[lane].sem, S.after(lane, i, "l2_square"))
                                dve.tensor_reduce(st[:, 0:16], squares[lane][:, :].rearrange("p (t d) -> p t d", d=D), AX, ALU.add).then_inc(chain[lane].sem, 1)
                            for lane in lanes:
                                A, B = edge_psum(lane)
                                st = stats[lane]
                                dve.wait_ge(chain[lane].sem, S.after(lane, i, "l2_root"))
                                dve.tensor_scalar(st[:, 32:48], st[:, 16:32], L2_EPS, None, ALU.max).then_inc(chain[lane].sem, 1)
                                dve.wait_ge(chain[lane].sem, S.after(lane, i, "l2_floor"))
                                dve.reciprocal(st[:, 48:64], st[:, 32:48]).then_inc(chain[lane].sem, 1)
                                dve.wait_ge(chain[lane].sem, S.after(lane, i, "l2_inverse"))
                                dve.wait_ge(stored[lane].sem, S.dma("stored", lane, i, rounds=0) + 16 * (l < 2))
                                dve.tensor_tensor(rows_out[lane][:, :].rearrange("p (t d) -> p t d", d=D), A.rearrange("p (t d) -> p t d", d=D),
                                                  st[:, 48:64].unsqueeze(2).broadcast_to([P, 2 * J, D]), ALU.mult).then_inc(chain[lane].sem, 1)
                                if add_resid:
                                    dve.wait_ge(chain[lane].sem, S.after(lane, i, "rows"))
                                    dve.tensor_tensor(rows_out[lane][:, :], rows_out[lane][:, :], resid[lane][:, :], ALU.add).then_inc(chain[lane].sem, 1)
                        if kind == "gin":
                            for lane in lanes:
                                A, B = edge_psum(lane)
                                b = i * EL + lane
                                zm = masked[lane][:, :].rearrange("p (j d) -> p j d", j=J)
                                z = squares[lane][:, 0:J * D]
                                mask = rep_mask[:, ds(b * J, J)]
                                dve.wait_ge(chain[lane].sem, S.after(lane, i, "z"))
                                dve.tensor_copy(z, B).then_inc(chain[lane].sem, 1)
                                dve.wait_ge(chain[lane].sem, S.after(lane, i, "z_rows"))
                                dve.tensor_tensor(zm[:, :, 0:D], z.rearrange("p (j d) -> p j d", j=J), mask.unsqueeze(2).broadcast_to([P, J, D]),
                                                  ALU.mult).then_inc(chain[lane].sem, 1)
                                dve.tensor_copy(zm[:, :, D], mask).then_inc(chain[lane].sem, 1)
                        if kind == "qkv":
                            for lane in lanes:
                                A, B = edge_psum(lane)
                                rec = record_rows[lane][:, :].rearrange("p (j d) -> p j d", j=J)
                                q, k = squares[lane][:, 0:J * D], squares[lane][:, J * D:2 * J * D]
                                dots = stats[lane][:, 0:J * HEADS]

                                def as_rows(v):
                                    return v.rearrange("p (j d) -> p j d", j=J)

                                def bias_of(n):
                                    return b_qkv[:, n, :].unsqueeze(1).broadcast_to([P, J, D])

                                dve.wait_ge(chain[lane].sem, S.after(lane, i, "qkv"))
                                dve.tensor_tensor(as_rows(q), as_rows(B), bias_of(0), ALU.add).then_inc(chain[lane].sem, 1)
                                dve.tensor_tensor(as_rows(k), as_rows(A[:, 0:512]), bias_of(1), ALU.add).then_inc(chain[lane].sem, 1)
                                dve.wait_ge(stored[lane].sem, S.dma("stored", lane, i, rounds=0))
                                dve.tensor_tensor(rec[:, :, 0:D], as_rows(A[:, 512:1024]), bias_of(2), ALU.add).then_inc(chain[lane].sem, 1)
                                dve.wait_ge(chain[lane].sem, S.after(lane, i, "v_bias"))
                                dve.tensor_tensor(centered[lane][:, 0:J * D], q, k, ALU.mult).then_inc(chain[lane].sem, 1)
                                dve.wait_ge(chain[lane].sem, S.after(lane, i, "q_times_k"))
                                dve.tensor_reduce(dots, centered[lane][:, 0:J * D].rearrange("p (t d) -> p t d", d=HD), AX, ALU.add).then_inc(chain[lane].sem, 1)
                                dve.wait_ge(chain[lane].sem, S.after(lane, i, "dot"))
                                dve.tensor_scalar(rec[:, :, D:D + HEADS], dots.rearrange("p (j h) -> p j h", h=HEADS),
                                                  1.0 / float(np.sqrt(HD)), None, ALU.mult).then_inc(chain[lane].sem, 1)
                                dve.wait_ge(chain[lane].sem, S.after(lane, i, "score"))
                                dve.tensor_reduce(rec[:, :, D + HEADS], rec[:, :, D:D + HEADS], AX, ALU.max).then_inc(chain[lane].sem, 1)
                    S.run(dve, body)
            S.close()
            for lane in range(EL):
                n = S.rounds + (lane < S.rest)
                if source != "rows":
                    gather_ready[lane].base += n * (1 if source == "links" and not homes else 2)
                if save_resid:
                    resid_saved[lane].base += 16 * n

        def gin_edge_phase(l, tout, add_resid):
            w = gin[l]
            S = Steps(["s_mm", "s_act", "d_mm", "d_act", "y_mm", "y_act", "t_out", "rows"], EL, EB,
                      loads=2 + add_resid, stores=1)
            with nc.Block() as block:
                @block.sync
                def _(sp):
                    def body(i, lanes):
                        for lane in lanes:
                            b = i * EL + lane
                            hold(sp, waits_passed_sp, chain[lane].sem, S.start(lane, i))
                            sp.dma_start(rows_in[lane][:, :], gin_x[ds(b, 1), :, :].rearrange("o f e -> (o f) e")).then_inc(loaded[lane].sem, 16)
                            sp.dma_start(flags[lane][0:D, :], gin_agg[ds(b, 1), :, :].rearrange("o f e -> (o f) e")).then_inc(loaded[lane].sem, 16)
                            if add_resid:
                                sp.dma_start(resid[lane][:, :].rearrange("p (j d) -> p j d", j=J), rows(sd_resid, b)).then_inc(loaded[lane].sem, 16)
                    S.run(sp, body)

                @block.tensor
                def _(pe):
                    def body(i, lanes):
                        for lane in lanes:
                            A, B = edge_psum(lane)
                            pe.wait_ge(chain[lane].sem, S.start(lane, i))
                            pe.wait_ge(loaded[lane].sem, S.dma("loaded", lane, i))
                            for h in range(2):
                                c = slice(h * 512, (h + 1) * 512)
                                op = pe.matmul(A[:, c], w["w1_own"][0:D, :], rows_in[lane][0:D, c], start=True, stop=True)
                            op.then_inc(chain[lane].sem, 1)
                        for lane in lanes:
                            A, B = edge_psum(lane)
                            pe.wait_ge(chain[lane].sem, S.after(lane, i, "s_act"))
                            for h in range(2):
                                c = slice(h * 512, (h + 1) * 512)
                                pe.matmul(A[:, c], w["w1_dst"][:, :], rows_in[lane][:, c], start=True, stop=False)
                                op = pe.matmul(A[:, c], w["w1"][0:D, :], flags[lane][0:D, c], start=False, stop=True)
                            op.then_inc(chain[lane].sem, 1)
                        for lane in lanes:
                            A, B = edge_psum(lane)
                            pe.wait_ge(chain[lane].sem, S.after(lane, i, "d_act"))
                            for h in range(2):
                                c = slice(h * 512, (h + 1) * 512)
                                pe.matmul(A[:, c], w["w2_src"][:, :], centered[lane][:, c], start=True, stop=False)
                                op = pe.matmul(A[:, c], w["w2_dst"][:, :], squares[lane][:, c], start=False, stop=True)
                            op.then_inc(chain[lane].sem, 1)
                        for lane in lanes:
                            A, B = edge_psum(lane)
                            pe.wait_ge(chain[lane].sem, S.after(lane, i, "y_act"))
                            for j in range(J):
                                op = pe.transpose(A[:, j * P:(j + 1) * P], tiles_of(feat_out[lane][:, :], j), ident[:, :])
                            op.then_inc(chain[lane].sem, 1)
                    S.run(pe, body)

                @block.scalar
                def _(act):
                    def body(i, lanes):
                        for mm, dest in (("s_mm", centered), ("d_mm", squares)):
                            for lane in lanes:
                                A, B = edge_psum(lane)
                                act.wait_ge(chain[lane].sem, S.after(lane, i, mm))
                                act.activation(dest[lane][:, :], A, ACT.Relu, bias=w["shift"][:, :], scale=w["scale"][:, :]).then_inc(chain[lane].sem, 1)
                        for lane in lanes:
                            A, B = edge_psum(lane)
                            act.wait_ge(chain[lane].sem, S.after(lane, i, "y_mm"))
                            act.activation(feat_out[lane][:, :], A, ACT.Identity, bias=w["b2"][:, :]).then_inc(chain[lane].sem, 1)
                        for lane in lanes:
                            b = i * EL + lane
                            act.wait_ge(chain[lane].sem, S.after(lane, i, "rows"))
                            act.dma_start(rows(tout, b), rows_out[lane][:, :].rearrange("p (j d) -> p j d", j=J)).then_inc(stored[lane].sem, 16)
                    S.run(act, body)
                    for lane in range(EL):
                        act.wait_ge(stored[lane].sem, S.at["stored"][lane] + (S.rounds + (lane < S.rest)) * 16)

                @block.vector
                def _(dve):
                    def body(i, lanes):
                        for lane in lanes:
                            A, B = edge_psum(lane)
                            dve.wait_ge(chain[lane].sem, S.after(lane, i, "t_out"))
                            dve.wait_ge(stored[lane].sem, S.dma("stored", lane, i, rounds=0))
                            if add_resid:
                                dve.tensor_tensor(rows_out[lane][:, :], A, resid[lane][:, :], ALU.add).then_inc(chain[lane].sem, 1)
                            else:
                                dve.tensor_copy(rows_out[lane][:, :], A).then_inc(chain[lane].sem, 1)
                    S.run(dve, body)
            S.close()

        def attention_phase():
            R72 = D + HEADS
            S = Steps(["t_in", "feat", "max_mm", "carry", "run_max", "score_mm", "unit", "below_max", "max_step",
                       "max_step_neg", "weight", "rescale", "weighted", "sums", "t_out", "guard", "inverse", "rows"],
                      EL, EB, loads=0, more=1, stores=0, gathers=J)
            n0, done0 = [c.base for c in scattered], [c.base for c in scatter_done]
            stage0 = [g.base for g in gather_ready]
            with nc.Block() as block:
                @block.sync
                def _(sp):
                    def body(i, lanes):
                        for lane in lanes:
                            b = i * EL + lane
                            hold(sp, waits_passed_sp, chain[lane].sem, S.start(lane, i))
                            sp.dma_start(flags[lane][0:R72, :], neg_start[ds(b * BLK, BLK)].partition_broadcast(R72)).then_inc(more_loaded[lane].sem, 16)
                    S.run(sp, body)

                @block.gpsimd
                def _(pool):
                    def body(i, lanes):
                        for lane in lanes:
                            b = i * EL + lane
                            hold(pool, waits_passed, chain[lane].sem, S.after(lane, i - 1, "t_in"))
                            pool.tensor_copy(idx_stage[lane][:, 0:J], sorted_edge[:, ds(b * J, J)]).then_inc(gather_ready[lane].sem, 1)
                            pool.tensor_copy(idx_stage[lane][:, J:2 * J], attn_out_idx[:, ds(b * J, J)]).then_inc(gather_ready[lane].sem, 1)
                            hold(pool, waits_passed, gather_ready[lane].sem, i * 2 + (stage0[lane] + 2))
                            for j in range(J):
                                pool.indirect_dma_start(rows_in[lane][:, j * REC:(j + 1) * REC], None, records[:, :],
                                                        bass.IndirectOffsetOnAxis(idx_stage[lane][:, j:j + 1], 0),
                                                        bounds_check=EP - 1, oob_is_err=False).then_inc(gathered[lane].sem, 16)
                        for lane in lanes:
                            hold(pool, waits_passed, chain[lane].sem, S.after(lane, i, "rows"))
                            for j in range(J):
                                pool.indirect_dma_start(attn_nodes[:, :], bass.IndirectOffsetOnAxis(idx_stage[lane][:, J + j:J + j + 1], 0),
                                                        rows_out[lane][:, j * D:(j + 1) * D], None,
                                                        bounds_check=N - 1, oob_is_err=False).then_inc(scattered[lane].sem, 16)
                        for lane in lanes:
                            hold(pool, waits_passed, scattered[lane].sem, i * (16 * J) + (n0[lane] + 16 * J))
                            pool.sem_inc(scatter_done[lane].sem, 1)
                    S.run(pool, body)

                @block.tensor
                def _(pe):
                    def body(i, lanes):
                        for lane in lanes:
                            A, B = edge_psum(lane)
                            pe.wait_ge(chain[lane].sem, S.start(lane, i))
                            pe.wait_ge(gathered[lane].sem, S.dma("gathered", lane, i))
                            for j in range(J):
                                op = pe.transpose(A[0:REC, j * P:(j + 1) * P], rows_in[lane][:, j * REC:(j + 1) * REC], ident[:, :])
                            op.then_inc(chain[lane].sem, 1)
                        for step, before, pick in (("max_mm", "feat", pick_max), ("score_mm", "run_max", pick_score)):
                            for lane in lanes:
                                A, B = edge_psum(lane)
                                pe.wait_ge(chain[lane].sem, S.after(lane, i, before))
                                for h in range(2):
                                    c = slice(h * 512, (h + 1) * 512)
                                    op = pe.matmul(A[0:R72, c], pick[0:REC, :], feat[lane][0:REC, c], start=True, stop=True)
                                op.then_inc(chain[lane].sem, 1)
                        for lane in lanes:
                            A, B = edge_psum(lane)
                            pe.wait_ge(chain[lane].sem, S.after(lane, i, "sums"))
                            for j in range(J):
                                op = pe.transpose(A[:, j * P:j * P + R72], tiles_of(feat_out[lane][0:R72, :], j), ident[0:R72, 0:R72])
                            op.then_inc(chain[lane].sem, 1)
                    S.run(pe, body)

                @block.scalar
                def _(act):
                    def body(i, lanes):
                        for lane in lanes:
                            A, B = edge_psum(lane)
                            act.wait_ge(chain[lane].sem, S.after(lane, i, "t_in"))
                            act.activation(in_order(feat[lane][0:REC, :]), by_tile(A)[0:REC], ACT.Copy).then_inc(chain[lane].sem, 1)
                        for lane in lanes:
                            act.wait_ge(chain[lane].sem, S.after(lane, i, "max_step_neg"))
                            act.activation(centered[lane][0:R72, :], centered[lane][0:R72, :], ACT.Exp).then_inc(chain[lane].sem, 1)
                            act.activation(squares[lane][0:R72, :], squares[lane][0:R72, :], ACT.Exp).then_inc(chain[lane].sem, 1)
                    S.run(act, body)

                @block.vector
                def _(dve):
                    def body(i, lanes):
                        for lane in lanes:
                            A, B = edge_psum(lane)
                            other = (lane - 1) % EL
                            m = running_max[lane]
                            dve.wait_ge(chain[lane].sem, S.after(lane, i, "max_mm"))
                            dve.wait_ge(more_loaded[lane].sem, S.dma("more", lane, i))
                            if lane == 0:
                                dve.wait_ge(chain[other].sem, S.after(other, i - 1, "run_max"))
                            else:
                                dve.wait_ge(chain[other].sem, S.after(other, i, "run_max"))
                            dve.tensor_copy(m[0:R72, 0:1], running_max[other][0:R72, BLK:BLK + 1]).then_inc(chain[lane].sem, 1)
                            dve.wait_ge(chain[lane].sem, S.after(lane, i, "carry"))
                            dve.tensor_tensor_scan(m[0:R72, 1:BLK + 1], flags[lane][0:R72, :], A[0:R72, :], m[0:R72, 0:1],
                                                   ALU.add, ALU.max).then_inc(chain[lane].sem, 1)
                        for lane in lanes:
                            A, B = edge_psum(lane)
                            m = running_max[lane]
                            d, r = centered[lane][0:R72, :], squares[lane][0:R72, :]
                            dve.wait_ge(chain[lane].sem, S.after(lane, i, "score_mm"))
                            dve.memset(feat[lane][D:R72, :], 1.0).then_inc(chain[lane].sem, 1)
                            dve.tensor_tensor(d, A[0:R72, :], m[0:R72, 1:BLK + 1], ALU.subtract).then_inc(chain[lane].sem, 1)
                            dve.tensor_tensor(r, m[0:R72, 0:BLK], m[0:R72, 1:BLK + 1], ALU.subtract).then_inc(chain[lane].sem, 1)
                            dve.wait_ge(chain[lane].sem, S.after(lane, i, "max_step"))
                            dve.tensor_tensor(r, r, flags[lane][0:R72, :], ALU.add).then_inc(chain[lane].sem, 1)
                        for lane in lanes:
                            other = (lane - 1) % EL
                            d, r = centered[lane][0:R72, :], squares[lane][0:R72, :]
                            dve.wait_ge(chain[lane].sem, S.after(lane, i, "rescale"))
                            dve.tensor_tensor(d, d, feat[lane][0:R72, :], ALU.mult).then_inc(chain[lane].sem, 1)
                            dve.wait_ge(chain[lane].sem, S.after(lane, i, "weighted"))
                            if lane == 0:
                                dve.wait_ge(chain[other].sem, S.after(other, i - 1, "sums"))
                            else:
                                dve.wait_ge(chain[other].sem, S.after(other, i, "sums"))
                            dve.tensor_tensor_scan(feat_out[lane][0:R72, :], r, d, feat_out[other][0:R72, BLK - 1:BLK],
                                                   ALU.mult, ALU.add).then_inc(chain[lane].sem, 1)
                        for lane in lanes:
                            A, B = edge_psum(lane)
                            a = A.rearrange("p (j f) -> p j f", j=J)
                            g, inv = stats[lane][:, 0:J * HEADS], masked[lane][:, 0:J * HEADS]
                            dve.wait_ge(chain[lane].sem, S.after(lane, i, "t_out"))
                            dve.tensor_scalar(g.rearrange("p (j h) -> p j h", h=HEADS), a[:, :, D:R72], SM_EPS, None, ALU.add).then_inc(chain[lane].sem, 1)
                            dve.wait_ge(chain[lane].sem, S.after(lane, i, "guard"))
                            dve.reciprocal(inv, g).then_inc(chain[lane].sem, 1)
                            dve.wait_ge(chain[lane].sem, S.after(lane, i, "inverse"))
                            dve.wait_ge(scatter_done[lane].sem, i + done0[lane])
                            dve.tensor_tensor(rows_out[lane][:, 0:J * D].rearrange("p (j h d) -> p j h d", h=HEADS, d=HD),
                                              a[:, :, 0:D].rearrange("p j (h d) -> p j h d", d=HD),
                                              inv.rearrange("p (j h) -> p j h", h=HEADS).unsqueeze(3).broadcast_to([P, J, HEADS, HD]),
                                              ALU.mult).then_inc(chain[lane].sem, 1)
                    S.run(dve, body)
            S.close()
            for lane in range(EL):
                n = S.rounds + (lane < S.rest)
                gather_ready[lane].base += 2 * n
                scattered[lane].base += 16 * J * n
                scatter_done[lane].base += n

        def scatter_phase(tin):
            S = Steps(["none"], EL, EB, loads=1, stores=0, gathers=J)
            stage0 = [g.base for g in gather_ready]
            with nc.Block() as block:
                @block.sync
                def _(sp):
                    def body(i, lanes):
                        for lane in lanes:
                            hold(sp, waits_passed_sp, gathered[lane].sem, S.dma("gathered", lane, i, rounds=0))
                            sp.dma_start(rows_in[lane][:, :].rearrange("p (j d) -> p j d", j=J), rows(tin, i * EL + lane)).then_inc(loaded[lane].sem, 16)
                    S.run(sp, body)

                @block.gpsimd
                def _(pool):
                    def body(i, lanes):
                        for lane in lanes:
                            b = i * EL + lane
                            hold(pool, waits_passed, gathered[lane].sem, S.dma("gathered", lane, i, rounds=0))
                            pool.tensor_copy(idx_stage[lane][:, 0:J], last_dst_idx[:, ds(b * J, J)]).then_inc(gather_ready[lane].sem, 1)
                            hold(pool, waits_passed, gather_ready[lane].sem, i + (stage0[lane] + 1))
                            hold(pool, waits_passed, loaded[lane].sem, S.dma("loaded", lane, i))
                            for j in range(J):
                                pool.indirect_dma_start(out[:, :], bass.IndirectOffsetOnAxis(idx_stage[lane][:, j:j + 1], 0),
                                                        rows_in[lane][:, j * P + D:(j + 1) * P], None,
                                                        bounds_check=N - 1, oob_is_err=False).then_inc(gathered[lane].sem, 16)
                    S.run(pool, body)
                    for lane in range(EL):
                        pool.wait_ge(gathered[lane].sem, S.at["gathered"][lane] + (S.rounds + (lane < S.rest)) * 16 * J)

        def node_rows(table, i, lane):
            if isinstance(i, int) and i * DL + lane == NB - 1:
                return table[N - BLK:N, :].rearrange("(p j) d -> p j d", j=J)
            return rows(table, i * DL + lane)

        def as3(tile):
            return tile.rearrange("p (j d) -> p j d", j=J)

        def node_store(act, S, i, lane, table, tile, sem):
            first = OVER if isinstance(i, int) and i * DL + lane == NB - 1 else 0
            act.dma_start(node_rows(table, i, lane)[first:P, :, :], as3(tile)[first:P, :, :]).then_inc(sem, 16)

        def node_sums_vector(dve, S, lane, i, h):
            hm = as3(masked[lane][:, :])
            mask = node_mask[:, ds((i * DL + lane) * J, J)] if not isinstance(i, int) else \
                node_mask[:, (i * DL + lane) * J:(i * DL + lane + 1) * J]
            dve.tensor_tensor(hm[:, :, 0:D], as3(h), mask.unsqueeze(2).broadcast_to([P, J, D]), ALU.mult).then_inc(chain[lane].sem, 1)
            dve.tensor_copy(hm[:, :, D], mask).then_inc(chain[lane].sem, 1)

        def node_sums_tensor(pe, S, lane, i, h):
            hm = as3(masked[lane][:, :])
            for j in range(J):
                op = pe.matmul(gram_nodes[0:D, 0:D + 1], h[:, j * D:(j + 1) * D], hm[:, j, :],
                               start=False, stop=False, skip_group_check=True)
            op.then_inc(chain[lane].sem, 1)

        W = J * D

        def transpose4(pe, bank, src):
            for q in range(4):
                op = pe.transpose(bank[:, q * P:(q + 1) * P], src[:, q * P:(q + 1) * P], ident[:, :])
            return op

        def node_sage_phase():
            names = LN + ["t_in", "feat"] + [s + str(k) for k in range(3) for s in ("mm", "act")] + ["t_out", "x1"] \
                + ["again_" + s for s in LN] + ["masked", "mask", "gram"]
            S = Steps(names, DL, NB, loads=1, stores=2)
            with nc.Block() as block:
                @block.sync
                def _(sp):
                    def body(i, lanes):
                        for lane in lanes:
                            hold(sp, waits_passed_sp, chain[lane].sem, S.after(lane, i - 1, "x1"))
                            sp.dma_start(as3(rows_in[lane][:, 0:W]), node_rows(t["x"], i, lane)).then_inc(loaded[lane].sem, 16)
                    S.run(sp, body)

                @block.tensor
                def _(pe):
                    pe.matmul(gram_nodes[0:D, 0:D + 1], zeros[:, 0:D], zeros[:, 0:D + 1], start=True, stop=True)

                    def body(i, lanes):
                        for lane in lanes:
                            A, B = node_psum(lane)
                            pe.wait_ge(chain[lane].sem, S.after(lane, i, "ln_out"))
                            transpose4(pe, A, centered[lane]).then_inc(chain[lane].sem, 1)
                        for k in range(3):
                            for lane in lanes:
                                A, B = node_psum(lane)
                                pe.wait_ge(chain[lane].sem, S.after(lane, i, f"act{k - 1}" if k else "feat"))
                                pe.matmul(B, sage[k]["own"][:, :], feat[lane][:, 0:W], start=True, stop=True).then_inc(chain[lane].sem, 1)
                        for lane in lanes:
                            A, B = node_psum(lane)
                            pe.wait_ge(chain[lane].sem, S.after(lane, i, "act2"))
                            transpose4(pe, A, feat[lane]).then_inc(chain[lane].sem, 1)
                        for lane in lanes:
                            pe.wait_ge(chain[lane].sem, S.after(lane, i, "mask"))
                            node_sums_tensor(pe, S, lane, i, centered[lane][:, 0:W])
                    S.run(pe, body)

                @block.scalar
                def _(act):
                    def body(i, lanes):
                        for lane in lanes:
                            ln_scalar(act, S, lane, i, J)
                        for lane in lanes:
                            A, B = node_psum(lane)
                            act.wait_ge(chain[lane].sem, S.after(lane, i, "t_in"))
                            act.activation(feat[lane][:, 0:W], A, ACT.Copy).then_inc(chain[lane].sem, 1)
                        for k in range(3):
                            for lane in lanes:
                                A, B = node_psum(lane)
                                act.wait_ge(chain[lane].sem, S.after(lane, i, f"mm{k}"))
                                act.activation(feat[lane][:, 0:W], B, ACT.Relu, bias=sage[k]["bias"][:, :]).then_inc(chain[lane].sem, 1)
                        for lane in lanes:
                            act.wait_ge(chain[lane].sem, S.after(lane, i, "x1"))
                            node_store(act, S, i, lane, x1_nodes, rows_out[lane][:, 0:W], stored[lane].sem)
                        for lane in lanes:
                            ln_scalar(act, S, lane, i, J, "again_")
                        for lane in lanes:
                            act.wait_ge(chain[lane].sem, S.after(lane, i, "again_ln_out"))
                            node_store(act, S, i, lane, h_nodes[0], centered[lane][:, 0:W], stored[lane].sem)
                    S.run(act, body)
                    for lane in range(DL):
                        act.wait_ge(stored[lane].sem, S.at["stored"][lane] + (S.rounds + (lane < S.rest)) * 32)

                @block.vector
                def _(dve):
                    def body(i, lanes):
                        for lane in lanes:
                            def first():
                                dve.wait_ge(chain[lane].sem, S.start(lane, i))
                                dve.wait_ge(stored[lane].sem, S.dma("stored", lane, i, rounds=0))
                                dve.wait_ge(loaded[lane].sem, S.dma("loaded", lane, i))
                            ln_vector(dve, S, lane, i, None, first, rows_in[lane], J)
                        for lane in lanes:
                            A, B = node_psum(lane)
                            dve.wait_ge(chain[lane].sem, S.after(lane, i, "t_out"))
                            dve.tensor_tensor(rows_out[lane][:, 0:W], A, rows_in[lane][:, 0:W], ALU.add).then_inc(chain[lane].sem, 1)
                        for lane in lanes:
                            def first():
                                dve.wait_ge(chain[lane].sem, S.after(lane, i, "x1"))
                            ln_vector(dve, S, lane, i, None, first, rows_out[lane], J, "again_")
                        for lane in lanes:
                            dve.wait_ge(chain[lane].sem, S.after(lane, i, "again_ln_out"))
                            node_sums_vector(dve, S, lane, i, centered[lane][:, 0:W])
                    S.run(dve, body)
            S.close()

        def node_gin_phase(l):
            w = gin[l]
            final = l == 2
            tin, tout = h_nodes[l % 2], x2_nodes if final else h_nodes[(l + 1) % 2]
            names = ["t_in", "feat", "w1", "norm", "w2", "y", "t_out", "rows"] + ([] if final else ["masked", "mask", "gram"])
            S = Steps(names, DL, NB, loads=1, more=int(final), stores=1)
            with nc.Block() as block:
                @block.sync
                def _(sp):
                    def body(i, lanes):
                        for lane in lanes:
                            hold(sp, waits_passed_sp, chain[lane].sem, S.after(lane, i - 1, "t_in"))
                            sp.dma_start(as3(rows_in[lane][:, 0:W]), node_rows(tin, i, lane)).then_inc(loaded[lane].sem, 16)
                        for lane in lanes:
                            if final:
                                hold(sp, waits_passed_sp, chain[lane].sem, S.start(lane, i))
                                sp.dma_start(as3(resid[lane][:, 0:W]), node_rows(x1_nodes, i, lane)).then_inc(more_loaded[lane].sem, 16)
                    S.run(sp, body)

                @block.tensor
                def _(pe):
                    if not final:
                        pe.matmul(gram_nodes[0:D, 0:D + 1], zeros[:, 0:D], zeros[:, 0:D + 1], start=True, stop=True)

                    def body(i, lanes):
                        for lane in lanes:
                            A, B = node_psum(lane)
                            pe.wait_ge(chain[lane].sem, S.start(lane, i))
                            pe.wait_ge(loaded[lane].sem, S.dma("loaded", lane, i))
                            transpose4(pe, A, rows_in[lane]).then_inc(chain[lane].sem, 1)
                        for lane in lanes:
                            A, B = node_psum(lane)
                            pe.wait_ge(chain[lane].sem, S.after(lane, i, "feat"))
                            pe.matmul(A, w["w1_own"][0:D, :], feat[lane][0:D, 0:W], start=True, stop=True)
                            pe.matmul(B, w["w1_own"][D:P, :], feat[lane][D:P, 0:W], start=True, stop=True).then_inc(chain[lane].sem, 1)
                        for lane in lanes:
                            A, B = node_psum(lane)
                            pe.wait_ge(chain[lane].sem, S.after(lane, i, "norm"))
                            pe.matmul(A, w["w2_src"][:, :], centered[lane][:, 0:W], start=True, stop=False)
                            pe.matmul(A, w["w2_dst"][:, :], centered[lane][:, W:2 * W], start=False, stop=True).then_inc(chain[lane].sem, 1)
                        for lane in lanes:
                            A, B = node_psum(lane)
                            pe.wait_ge(chain[lane].sem, S.after(lane, i, "y"))
                            transpose4(pe, B, feat_out[lane]).then_inc(chain[lane].sem, 1)
                        if not final:
                            for lane in lanes:
                                pe.wait_ge(chain[lane].sem, S.after(lane, i, "mask"))
                                node_sums_tensor(pe, S, lane, i, rows_out[lane][:, 0:W])
                    S.run(pe, body)

                @block.scalar
                def _(act):
                    def body(i, lanes):
                        for lane in lanes:
                            A, B = node_psum(lane)
                            act.wait_ge(chain[lane].sem, S.after(lane, i, "t_in"))
                            act.activation(feat[lane][:, 0:W], A, ACT.Copy).then_inc(chain[lane].sem, 1)
                        for lane in lanes:
                            act.wait_ge(chain[lane].sem, S.after(lane, i, "w1"))
                            act.activation(centered[lane][:, :], work[:, lane * 1024:(lane + 1) * 1024], ACT.Relu,
                                           bias=w["shift"][:, :], scale=w["scale"][:, :]).then_inc(chain[lane].sem, 1)
                        for lane in lanes:
                            A, B = node_psum(lane)
                            act.wait_ge(chain[lane].sem, S.after(lane, i, "w2"))
                            act.activation(feat_out[lane][:, 0:W], A, ACT.Identity, bias=w["b2"][:, :]).then_inc(chain[lane].sem, 1)
                        for lane in lanes:
                            act.wait_ge(chain[lane].sem, S.after(lane, i, "rows"))
                            node_store(act, S, i, lane, tout, rows_out[lane][:, 0:W], stored[lane].sem)
                    S.run(act, body)
                    for lane in range(DL):
                        act.wait_ge(stored[lane].sem, S.at["stored"][lane] + (S.rounds + (lane < S.rest)) * 16)

                @block.vector
                def _(dve):
                    def body(i, lanes):
                        for lane in lanes:
                            A, B = node_psum(lane)
                            dve.wait_ge(chain[lane].sem, S.after(lane, i, "t_out"))
                            dve.wait_ge(stored[lane].sem, S.dma("stored", lane, i, rounds=0))
                            if final:
                                dve.wait_ge(more_loaded[lane].sem, S.dma("more", lane, i))
                                dve.tensor_tensor(rows_out[lane][:, 0:W], B, resid[lane][:, 0:W], ALU.add).then_inc(chain[lane].sem, 1)
                            else:
                                dve.tensor_copy(rows_out[lane][:, 0:W], B).then_inc(chain[lane].sem, 1)
                        if not final:
                            for lane in lanes:
                                dve.wait_ge(chain[lane].sem, S.after(lane, i, "rows"))
                                node_sums_vector(dve, S, lane, i, rows_out[lane][:, 0:W])
                    S.run(dve, body)
            S.close()

        def node_final_phase():
            layer = ["t", "feat", "mm", "act", "back", "l2_square", "l2_sum", "l2_root", "l2_floor", "l2_inverse", "rows"]
            names = ["t_in", "feat", "mm", "act", "t_out", "x3"] + LN + [s + str(k) for k in range(3) for s in layer] + ["out"]
            S = Steps(names, DL, NB, loads=1, more=1, stores=1)
            with nc.Block() as block:
                @block.sync
                def _(sp):
                    def body(i, lanes):
                        for lane in lanes:
                            hold(sp, waits_passed_sp, chain[lane].sem, S.after(lane, i - 1, "t_in"))
                            sp.dma_start(as3(rows_in[lane][:, 0:W]), node_rows(attn_nodes, i, lane)).then_inc(loaded[lane].sem, 16)
                        for lane in lanes:
                            hold(sp, waits_passed_sp, chain[lane].sem, S.after(lane, i - 1, "x3"))
                            sp.dma_start(as3(resid[lane][:, 0:W]), node_rows(x2_nodes, i, lane)).then_inc(more_loaded[lane].sem, 16)
                    S.run(sp, body)

                @block.tensor
                def _(pe):
                    def body(i, lanes):
                        for lane in lanes:
                            A, B = node_psum(lane)
                            pe.wait_ge(chain[lane].sem, S.start(lane, i))
                            pe.wait_ge(loaded[lane].sem, S.dma("loaded", lane, i))
                            transpose4(pe, A, rows_in[lane]).then_inc(chain[lane].sem, 1)
                        for lane in lanes:
                            A, B = node_psum(lane)
                            pe.wait_ge(chain[lane].sem, S.after(lane, i, "feat"))
                            pe.matmul(B, w_o[:, :], feat[lane][:, 0:W], start=True, stop=True).then_inc(chain[lane].sem, 1)
                        for lane in lanes:
                            A, B = node_psum(lane)
                            pe.wait_ge(chain[lane].sem, S.after(lane, i, "act"))
                            transpose4(pe, A, feat_out[lane]).then_inc(chain[lane].sem, 1)
                        for k in range(3):
                            for lane in lanes:
                                A, B = node_psum(lane)
                                pe.wait_ge(chain[lane].sem, S.after(lane, i, f"rows{k - 1}" if k else "ln_out"))
                                transpose4(pe, A, centered[lane]).then_inc(chain[lane].sem, 1)
                            for lane in lanes:
                                A, B = node_psum(lane)
                                pe.wait_ge(chain[lane].sem, S.after(lane, i, f"feat{k}"))
                                pe.matmul(B, gnn[k]["own"][:, :], feat[lane][:, 0:W], start=True, stop=True).then_inc(chain[lane].sem, 1)
                            for lane in lanes:
                                A, B = node_psum(lane)
                                pe.wait_ge(chain[lane].sem, S.after(lane, i, f"act{k}"))
                                transpose4(pe, A, feat_out[lane]).then_inc(chain[lane].sem, 1)
                    S.run(pe, body)

                @block.scalar
                def _(act):
                    def body(i, lanes):
                        for lane in lanes:
                            A, B = node_psum(lane)
                            act.wait_ge(chain[lane].sem, S.after(lane, i, "t_in"))
                            act.activation(feat[lane][:, 0:W], A, ACT.Copy).then_inc(chain[lane].sem, 1)
                        for lane in lanes:
                            A, B = node_psum(lane)
                            act.wait_ge(chain[lane].sem, S.after(lane, i, "mm"))
                            act.activation(feat_out[lane][:, 0:W], B, ACT.Identity, bias=b_o[:, :]).then_inc(chain[lane].sem, 1)
                        for lane in lanes:
                            ln_scalar(act, S, lane, i, J)
                        for k in range(3):
                            for lane in lanes:
                                A, B = node_psum(lane)
                                act.wait_ge(chain[lane].sem, S.after(lane, i, f"t{k}"))
                                act.activation(feat[lane][:, 0:W], A, ACT.Copy).then_inc(chain[lane].sem, 1)
                            for lane in lanes:
                                A, B = node_psum(lane)
                                act.wait_ge(chain[lane].sem, S.after(lane, i, f"mm{k}"))
                                act.activation(feat_out[lane][:, 0:W], B, ACT.Relu, bias=gnn[k]["bias"][:, :]).then_inc(chain[lane].sem, 1)
                            for lane in lanes:
                                A, B = node_psum(lane)
                                act.wait_ge(chain[lane].sem, S.after(lane, i, f"back{k}"))
                                act.activation(squares[lane][:, 0:W], A, ACT.Square).then_inc(chain[lane].sem, 1)
                            for lane in lanes:
                                act.wait_ge(chain[lane].sem, S.after(lane, i, f"l2_sum{k}"))
                                act.activation(stats[lane][:, 16:16 + J], stats[lane][:, 0:J], ACT.Sqrt).then_inc(chain[lane].sem, 1)
                        for lane in lanes:
                            act.wait_ge(chain[lane].sem, S.after(lane, i, "out"))
                            node_store(act, S, i, lane, out, rows_out[lane][:, 0:W], stored[lane].sem)
                    S.run(act, body)
                    for lane in range(DL):
                        act.wait_ge(stored[lane].sem, S.at["stored"][lane] + (S.rounds + (lane < S.rest)) * 16)

                @block.vector
                def _(dve):
                    def body(i, lanes):
                        for lane in lanes:
                            A, B = node_psum(lane)
                            dve.wait_ge(chain[lane].sem, S.after(lane, i, "t_out"))
                            dve.wait_ge(stored[lane].sem, S.dma("stored", lane, i, rounds=0))
                            dve.wait_ge(more_loaded[lane].sem, S.dma("more", lane, i))
                            dve.tensor_tensor(rows_out[lane][:, 0:W], A, resid[lane][:, 0:W], ALU.add).then_inc(chain[lane].sem, 1)
                        for lane in lanes:
                            def first():
                                dve.wait_ge(chain[lane].sem, S.after(lane, i, "x3"))
                            ln_vector(dve, S, lane, i, None, first, rows_out[lane], J)
                        for k in range(3):
                            for lane in lanes:
                                dve.wait_ge(chain[lane].sem, S.after(lane, i, f"l2_square{k}"))
                                dve.tensor_reduce(stats[lane][:, 0:J], as3(squares[lane][:, 0:W]), AX, ALU.add).then_inc(chain[lane].sem, 1)
                            for lane in lanes:
                                A, B = node_psum(lane)
                                st = stats[lane]
                                dve.wait_ge(chain[lane].sem, S.after(lane, i, f"l2_root{k}"))
                                dve.tensor_scalar(st[:, 32:32 + J], st[:, 16:16 + J], L2_EPS, None, ALU.max).then_inc(chain[lane].sem, 1)
                                dve.wait_ge(chain[lane].sem, S.after(lane, i, f"l2_floor{k}"))
                                dve.reciprocal(st[:, 48:48 + J], st[:, 32:32 + J]).then_inc(chain[lane].sem, 1)
                                dve.wait_ge(chain[lane].sem, S.after(lane, i, f"l2_inverse{k}"))
                                dve.tensor_tensor(as3(centered[lane][:, 0:W]), as3(A), st[:, 48:48 + J].unsqueeze(2).broadcast_to([P, J, D]),
                                                  ALU.mult).then_inc(chain[lane].sem, 1)
                        for lane in lanes:
                            dve.wait_ge(chain[lane].sem, S.after(lane, i, "rows2"))
                            dve.tensor_tensor(rows_out[lane][:, 0:W], rows_out[lane][:, 0:W], centered[lane][:, 0:W], ALU.add).then_inc(chain[lane].sem, 1)
                    S.run(dve, body)
            S.close()

        def coefficients_phase(l):
            w = gin[l]
            s0 = setup_step.base
            with nc.Block() as block:
                @block.vector
                def _(dve):
                    step = [s0]

                    def link(op):
                        step[0] += 1
                        op.then_inc(setup_step.sem, 1)
                        dve.wait_ge(setup_step.sem, step[0])

                    k = w["keep"][0:D, :]
                    link(dve.tensor_copy(moments_edges[:, :], gram_edges[0:D, 0:D + 1]))
                    link(dve.tensor_scalar(moments[:, :], gram_nodes[0:D, 0:D + 1], k, None, ALU.mult))
                    link(dve.tensor_scalar(moments[:, 0:D], moments[:, 0:D], k, None, ALU.mult))
                    link(dve.tensor_tensor(moments[:, :], moments[:, :], moments_edges[:, :], ALU.add))
                    link(dve.tensor_scalar(moments[:, :], moments[:, :], 1.0 / N, None, ALU.mult))
                    step[0] += 1
                    dve.wait_ge(setup_step.sem, step[0])
                    link(dve.tensor_tensor(w1_moments[:, :], work[0:D, 0:H], w["w1"][0:D, :], ALU.mult))
                    link(dve.tensor_copy(coef[:, 0:1], work[:, 512:513]))
                    link(dve.tensor_tensor(coef[:, 1:2], coef[:, 0:1], coef[:, 0:1], ALU.mult))
                    step[0] += 1
                    dve.wait_ge(setup_step.sem, step[0])
                    link(dve.tensor_tensor(coef[:, 2:3], work[:, 1024:1025], coef[:, 1:2], ALU.subtract))
                    link(dve.tensor_scalar(coef[:, 2:3], coef[:, 2:3], 0.0, None, ALU.max))
                    step[0] += 1
                    dve.wait_ge(setup_step.sem, step[0])
                    link(dve.reciprocal(coef[:, 4:5], coef[:, 3:4]))
                    link(dve.tensor_tensor(w["scale"][:, :], coef[:, 4:5], w["gamma"][:, :], ALU.mult))
                    link(dve.tensor_tensor(coef[:, 5:6], coef[:, 0:1], w["b1"][:, :], ALU.add))
                    link(dve.tensor_tensor(coef[:, 6:7], w["b1"][:, :], coef[:, 5:6], ALU.subtract))
                    link(dve.tensor_tensor(coef[:, 7:8], coef[:, 6:7], w["scale"][:, :], ALU.mult))
                    link(dve.tensor_tensor(w["shift"][:, :], coef[:, 7:8], w["beta"][:, :], ALU.add))

                @block.tensor
                def _(pe):
                    pe.wait_ge(setup_step.sem, s0 + 5)
                    pe.matmul(work[0:D, 0:H], moments[0:D, 0:D], w["w1"][0:D, :], start=True, stop=True)
                    pe.matmul(work[:, 512:513], w["w1"][0:D, :], moments[0:D, D:D + 1], start=True, stop=True).then_inc(setup_step.sem, 1)
                    pe.wait_ge(setup_step.sem, s0 + 9)
                    pe.matmul(work[:, 1024:1025], w1_moments[0:D, :], ones[0:D, 0:1], start=True, stop=True).then_inc(setup_step.sem, 1)

                @block.scalar
                def _(act):
                    act.wait_ge(setup_step.sem, s0 + 12)
                    act.activation(coef[:, 3:4], coef[:, 2:3], ACT.Sqrt, bias=eps_bn[:, :]).then_inc(setup_step.sem, 1)
            setup_step.base += 19

        node_sage_phase()
        edge_phase("sage", 0, "nodes", None, sd[0], ln=True)
        edge_phase("sage", 1, "links", sd[0], sd[1])
        edge_phase("sage", 2, "links", sd[1], sd[0], add_resid=True)
        edge_phase("gin", 0, "links", sd[0], None, ln=True)
        coefficients_phase(0)
        node_gin_phase(0)
        gin_edge_phase(0, sd[1], False)
        edge_phase("gin", 1, "links", sd[1], None)
        coefficients_phase(1)
        node_gin_phase(1)
        gin_edge_phase(1, sd[0], False)
        edge_phase("gin", 2, "links", sd[0], None)
        coefficients_phase(2)
        node_gin_phase(2)
        gin_edge_phase(2, sd[1], True)
        edge_phase("qkv", 0, "links", sd[1], None, ln=True)
        attention_phase()
        edge_phase("proj", 0, "attention", None, sd[0], add_resid=True)
        node_final_phase()
        edge_phase("gnn", 0, "rows", sd[0], sd[1], ln=True)
        edge_phase("gnn", 1, "links", sd[1], sd[0])
        edge_phase("gnn", 2, "links", sd[0], sd[1], add_resid=True)
        scatter_phase(sd[1])


_CONST = None


def kernel(**inputs):
    import numpy as _np
    import concourse.bacc as _bacc
    from concourse import mybir as _mybir
    from concourse.bass_utils import run_bass_kernel_spmd as _run

    nc = _bacc.Bacc("TRN2", target_bir_lowering=False, num_devices=1)
    arrays, tensors = {}, {}
    for name, value in inputs.items():
        a = _np.asarray(value)
        if name.startswith("L0_gnn_w"):
            a = a.T
        a = _np.ascontiguousarray(a)
        arrays[f"in_{name}"] = a
        tensors[name] = nc.dram_tensor(f"in_{name}", a.shape, _mybir.dt.from_np(a.dtype), kind="ExternalInput").ap()
    shape = tuple(int(n) for n in inputs["x"].shape)
    out = nc.dram_tensor("out", shape, _mybir.dt.float32, kind="ExternalOutput").ap()
    build_program(nc, tensors, out)
    r = _run(nc, [arrays], core_ids=[0])
    return r.results[0]["out"]
```

```python
class Counted:

    def __init__(self, sem):
        self.sem, self.base = sem, 0


def build_program(nc, t, out):
    import concourse.bass as bass
    from concourse import mybir
    from contextlib import ExitStack
    import numpy as np

    f32, i32, bf16 = mybir.dt.float32, mybir.dt.int32, mybir.dt.bfloat16
    ALU = mybir.AluOpType
    ACT = mybir.ActivationFunctionType
    AX = mybir.AxisListType.X
    ds = bass.ds

    P = 128
    N, D = t["x"].shape
    E = t["src"].shape[0]
    J = 8
    BLK = P * J
    H = t["L1_gnn_W1"].shape[2]
    HEADS = 8
    HD = D // HEADS
    EB = -(-E // BLK)
    EP = EB * BLK
    ET = EB * J
    NB = -(-N // BLK)
    OVER = (NB * BLK - N) // J
    assert NB * BLK - N == OVER * J and E % J == 0
    BIG = 1 << 22
    NEG = -1.0e30
    LN_EPS, BN_EPS, L2_EPS, SM_EPS = 1e-5, 1e-5, 1e-12, 1e-8
    DL, EL = 6, 3
    REC = 80
    DIGIT = 6
    RADIX = 1 << DIGIT
    PASSES = -(-int(N).bit_length() // DIGIT)

    ctx = ExitStack()
    with ctx:
        def dram(name, shape, dt=f32):
            return nc.dram_tensor(name, shape, dt).ap()

        def sb(name, shape, dt=f32, c=ctx):
            return c.enter_context(nc.sbuf_tensor(name, shape, dt))

        def counted(name):
            return Counted(ctx.enter_context(nc.semaphore(name)))

        x1_nodes = dram("x1_nodes", (N, D))
        x2_nodes = dram("x2_nodes", (N, D))
        h_nodes = [dram(f"h_nodes{k}", (N, D)) for k in range(2)]
        attn_nodes = dram("attn_nodes", (N, D))
        pos_nodes = dram("pos_nodes", (N, 1), i32)
        sd = [dram(f"sd{k}", (EP, 2 * D)) for k in range(2)]
        sd_resid = dram("sd_resid", (EP, 2 * D))
        gin_x = dram("gin_x", (EB, P, BLK))
        gin_agg = dram("gin_agg", (EB, D, BLK))
        edge_state = dram("edge_state", (EB, D, BLK))
        records = dram("records", (EP, REC))
        src_pad = dram("src_pad", (EP,), i32)
        dst_pad = dram("dst_pad", (EP + 2 * J,), i32)
        key_pad = dram("key_pad", (EP + 2 * J,), i32)
        same_dst = dram("same_dst", (EP,))
        inv_deg = dram("inv_deg", (EP,))
        neg_start = dram("neg_start", (EP,))
        sorting = [dram(f"sorting{k}", (EP, 2), i32) for k in range(2)]

        def rows(table, b, width=None):
            return table[ds(b * BLK, BLK), :].rearrange("(p j) d -> p j d", j=J)

        def cols_bj(vec):
            return vec.rearrange("(b p j) -> p b j", p=P, j=J)

        chain = [counted(f"lane{k}_steps_done") for k in range(DL)]
        loaded = [counted(f"lane{k}_loaded") for k in range(DL)]
        stored = [counted(f"lane{k}_stored") for k in range(DL)]
        gathered = [counted(f"lane{k}_gathered") for k in range(EL)]
        held = {nc.gpsimd.engine: counted("gpsimd_waits_passed"), nc.sync.engine: counted("sync_waits_passed")}
        staged = [counted(f"indices_staged{k}") for k in range(EL)]
        setup_dma = counted("setup_dma")
        setup_step = counted("setup_step")
        weights_in = counted("weights_in")
        zeroed = counted("weights_zeroed")
        attn_zeroed = counted("attention_table_zeroed")

        ident = sb("ident", [P, P])
        src_clamped = sb("src_clamped", [P, ET], i32)
        dst_clamped = sb("dst_clamped", [P, ET], i32)
        link_idx = sb("link_idx", [P, ET], i32)
        home_idx = sb("home_idx", [P, ET], i32)
        last_dst_idx = sb("last_dst_idx", [P, ET], i32)
        rep_mask = sb("rep_mask", [P, ET])
        node_mask = sb("node_mask", [P, NB * J])
        sorted_edge = sb("sorted_edge", [P, ET], i32)
        attn_out_idx = sb("attn_out_idx", [P, ET], i32)
        idx_stage = [sb(f"idx_stage{k}", [P, 2 * J], i32) for k in range(EL)]
        zeros = sb("zeros", [P, J * D])
        eps_ln = sb("eps_ln", [P, 1])
        eps_bn = sb("eps_bn", [P, 1])
        ones = sb("ones", [P, P])

        work = ctx.enter_context(nc.psum_tensor("work", [P, 6 * 512], f32))
        gram_nodes = ctx.enter_context(nc.psum_tensor("gram_nodes", [P, 512], f32))
        gram_edges = ctx.enter_context(nc.psum_tensor("gram_edges", [P, 512], f32))

        zero_tiles, weight_loads = [], []

        def weight(name, shape, parts, zero=False):
            tile = sb(name, shape)
            if zero:
                zero_tiles.append(tile)
            for where, src in parts(tile):
                weight_loads.append((where, src))
            return tile

        def column(name, vec, copies):
            n = vec.shape[0]
            return weight(name, [P, 1], lambda w: [
                (w[k * n:(k + 1) * n, :], vec.rearrange("(n o) -> n o", o=1)) for k in range(copies)])

        def block_diag(name, m):
            return weight(name, [P, P], lambda w: [(w[0:D, 0:D], m), (w[D:P, D:P], m)], zero=True)

        def to_dst(name, m, at=0):
            return weight(name, [P, P], lambda w: [(w[at:at + m.shape[0], D:P], m)], zero=True)

        sage = []
        for l in range(3):
            sage.append(dict(own=block_diag(f"sage_own{l}", t[f"L0_gnn_wr{l}"]),
                             agg=to_dst(f"sage_agg{l}", t[f"L0_gnn_wl{l}"]),
                             bias=column(f"sage_bias{l}", t[f"L0_gnn_bl{l}"], 2)))
        gin = []
        for l in range(3):
            w1, w2 = t["L1_gnn_W1"][l], t["L1_gnn_W2"][l]
            eps_all = t["L1_gnn_eps"]
            gin.append(dict(
                w1=weight(f"gin_w1_{l}", [P, H], lambda w: [(w[0:D, :], w1), (w[D:P, :], w1)]),
                w1_own=sb(f"gin_w1_own{l}", [P, H]),
                w1_dst=sb(f"gin_w1_dst{l}", [P, H]),
                keep=weight(f"gin_keep{l}", [P, 1], lambda w: [(w[:, :], eps_all[l:l + 1].partition_broadcast(P))]),
                keep_ident=sb(f"gin_keep_ident{l}", [P, D]),
                w2_src=weight(f"gin_w2_src{l}", [P, P], lambda w: [(w[:, 0:D], w2)], zero=True),
                w2_dst=weight(f"gin_w2_dst{l}", [P, P], lambda w: [(w[:, D:P], w2)], zero=True),
                b1=column(f"gin_b1_{l}", t["L1_gnn_b1"][l], 1),
                gamma=column(f"gin_gamma{l}", t["L1_gnn_gamma"][l], 1),
                beta=column(f"gin_beta{l}", t["L1_gnn_beta"][l], 1),
                b2=column(f"gin_b2_{l}", t["L1_gnn_b2"][l], 2),
                scale=sb(f"gin_scale{l}", [P, 1]), shift=sb(f"gin_shift{l}", [P, 1])))
        w_qkv = weight("w_qkv", [P, 2 * D], lambda w: [
            (w[0:D, 0:D], t["L2_gnn_Wq"]), (w[D:P, 0:D], t["L2_gnn_Wk"]), (w[D:P, D:P], t["L2_gnn_Wv"])], zero=True)
        b_qkv = weight("b_qkv", [P, 3, D], lambda w: [
            (w[:, k, :], t[f"L2_gnn_b{c}"].partition_broadcast(P)) for k, c in enumerate("qkv")])
        w_o = block_diag("w_o", t["L2_gnn_Wo"])
        b_o = column("b_o", t["L2_gnn_bo"], 2)
        gnn = []
        for l in range(3):
            aw = t["L3_gnn_agg_W"][l]
            g = dict(msg=weight(f"gnn_msg{l}", [P, D], lambda w: [(w[:, :], t["L3_gnn_msg_W"][l])]),
                     msg_b=column(f"gnn_msg_b{l}", t["L3_gnn_msg_b"][l], 1),
                     own=block_diag(f"gnn_own{l}", aw[D:2 * D, :]),
                     agg=to_dst(f"gnn_agg{l}", aw[0:D, :]),
                     bias=column(f"gnn_bias{l}", t["L3_gnn_agg_b"][l], 2))
            if l > 0:
                ew, eb = t["L3_gnn_edge_W"][l - 1], t["L3_gnn_edge_b"][l - 1]
                g.update(edge_nodes=to_dst(f"gnn_edge_nodes{l}", ew[0:2 * D, :]),
                         edge_own=to_dst(f"gnn_edge_own{l}", ew[2 * D:3 * D, :], at=D),
                         edge_b=column(f"gnn_edge_b{l}", eb, 2))
            gnn.append(g)
        pick_max = sb("pick_max", [P, 72])
        pick_score = sb("pick_score", [P, 72])

        def engine_setup_counts(n):
            setup_step.base += n

        with nc.Block() as block:
            @block.gpsimd
            def _(pool):
                for tile in zero_tiles:
                    pool.memset(tile[:, :], 0.0).then_inc(zeroed.sem, 1)
                pool.memset(ones[:, :], 1.0).then_inc(setup_step.sem, 1)
                pool.memset(eps_ln[:, :], LN_EPS).then_inc(setup_step.sem, 1)
                pool.memset(eps_bn[:, :], BN_EPS).then_inc(setup_step.sem, 1)
                pool.memset(ident[:, :], 0.0).then_inc(setup_step.sem, 1)
                pool.memset(pick_max[:, :], 0.0).then_inc(setup_step.sem, 1)
                pool.memset(pick_score[:, :], 0.0).then_inc(setup_step.sem, 1)
                pool.wait_ge(setup_step.sem, 6)
                pool.affine_select(out=ident[:, :], in_=ident[:, :], compare_op=ALU.not_equal, fill=1.0,
                                   base=0, pattern=[[-1, P]], channel_multiplier=1).then_inc(setup_step.sem, 1)
                pool.affine_select(out=pick_max[:, :], in_=pick_max[:, :], compare_op=ALU.not_equal, fill=1.0,
                                   base=-72, pattern=[[0, 72]], channel_multiplier=1).then_inc(setup_step.sem, 1)
                pool.affine_select(out=pick_score[:, 0:D].rearrange("p (h d) -> p h d", d=HD),
                                   in_=pick_score[:, 0:D].rearrange("p (h d) -> p h d", d=HD),
                                   compare_op=ALU.not_equal, fill=1.0, base=-D,
                                   pattern=[[-1, HEADS], [0, HD]], channel_multiplier=1).then_inc(setup_step.sem, 1)
                pool.affine_select(out=pick_score[:, D:72], in_=pick_score[:, D:72],
                                   compare_op=ALU.not_equal, fill=1.0, base=-D,
                                   pattern=[[-1, HEADS]], channel_multiplier=1).then_inc(setup_step.sem, 1)
                pool.wait_ge(setup_step.sem, 10)

            @block.sync
            def _(sp):
                sp.wait_ge(zeroed.sem, len(zero_tiles))
                for where, src in weight_loads:
                    sp.dma_start(where, src).then_inc(weights_in.sem, 16)

            @block.vector
            def _(dve):
                dve.wait_ge(weights_in.sem, 16 * len(weight_loads))
                dve.wait_ge(setup_step.sem, 10)
                for g in gin:
                    dve.tensor_scalar(g["keep"][:, :], g["keep"][:, :], 1.0, None, ALU.add).then_inc(setup_step.sem, 1)
                dve.wait_ge(setup_step.sem, 13)
                for g in gin:
                    dve.tensor_scalar(g["w1_own"][:, :], g["w1"][:, :], g["keep"][:, :], None, ALU.mult)
                    dve.memset(g["w1_dst"][0:D, :], 0.0)
                    dve.tensor_scalar(g["w1_dst"][D:P, :], g["w1"][D:P, :], g["keep"][D:P, :], None, ALU.mult)
                    dve.memset(g["keep_ident"][0:D, :], 0.0)
                    dve.tensor_scalar(g["keep_ident"][D:P, :], ident[D:P, D:P], g["keep"][D:P, :], None,
                                      ALU.mult).then_inc(setup_step.sem, 1)
                dve.wait_ge(setup_step.sem, 16)
        setup_step.base = 16

        def segment_phase(key_table, first_name, as_flags, out_idx, rep, start_table):
            with ExitStack() as c:
                keys = sb(first_name + "_keys", [P, 3, EB, J], i32, c)
                keysf = sb(first_name + "_keysf", [P, 3, ET], f32, c)
                start = sb(first_name + "_start", [P, ET], f32, c)
                last = sb(first_name + "_last", [P, ET], f32, c)
                valid = sb(first_name + "_valid", [P, ET], f32, c)
                idxf = sb(first_name + "_idxf", [P, ET], f32, c)
                with nc.Block() as block:
                    d0, s0 = setup_dma.base, setup_step.base

                    @block.sync
                    def _(sp):
                        for k, shift in enumerate((J - 1, J, J + 1)):
                            sp.dma_start(keys[:, k, :, :], cols_bj(key_table[shift:shift + EP])).then_inc(setup_dma.sem, 16)
                        sp.wait_ge(setup_step.sem, s0 + 7)
                        sp.dma_start(cols_bj(start_table[:]), start[:, :].rearrange("p (b j) -> p b j", j=J)).then_inc(setup_dma.sem, 16)
                        sp.wait_ge(setup_dma.sem, d0 + 64)

                    @block.vector
                    def _(dve):
                        step = [s0]

                        def link(op):
                            step[0] += 1
                            op.then_inc(setup_step.sem, 1)
                            dve.wait_ge(setup_step.sem, step[0])

                        dve.wait_ge(setup_dma.sem, d0 + 48)
                        link(dve.tensor_copy(keysf[:, :, :], keys[:, :, :, :].rearrange("p k b j -> p k (b j)")))
                        link(dve.tensor_tensor(start[:, :], keysf[:, 1, :], keysf[:, 0, :], ALU.is_equal))
                        link(dve.tensor_tensor(last[:, :], keysf[:, 1, :], keysf[:, 2, :], ALU.not_equal))
                        link(dve.scalar_tensor_tensor(rep, keysf[:, 1, :], float(N), last[:, :], ALU.is_lt, ALU.mult))
                        link(dve.scalar_tensor_tensor(idxf[:, :], keysf[:, 1, :], -float(BIG), rep, ALU.add, ALU.mult))
                        link(dve.tensor_scalar(out_idx, idxf[:, :], float(BIG), None, ALU.add))
                        if as_flags:
                            link(dve.tensor_scalar(start[:, :], start[:, :], 1.0, None, ALU.mult))
                        else:
                            link(dve.tensor_scalar(start[:, :], start[:, :], -NEG, NEG, ALU.mult, ALU.add))
                        step_total[0] = step[0]

                    setup_step.base = step_total[0]
                    setup_dma.base = d0 + 64

        step_total = [0]
        KP = EP // P
        full, rest = E // KP, E % KP
        with ExitStack() as c:
            keys_in = sb("keys_in", [P, 2, KP], i32, c)
            edge_marks = sb("edge_marks", [1, J], i32, c)
            key_big = sb("key_big", [P, 1024], i32, c)
            with nc.Block() as block:
                d0, s0 = setup_dma.base, setup_step.base

                @block.vector
                def _(dve):
                    dve.memset(keys_in[:, :, :], N).then_inc(setup_step.sem, 1)
                    dve.memset(edge_marks[:, :], -1).then_inc(setup_step.sem, 1)
                    dve.memset(key_big[:, :], BIG).then_inc(setup_step.sem, 1)
                    dve.memset(zeros[:, :], 0.0).then_inc(setup_step.sem, 1)

                @block.sync
                def _(sp):
                    sp.wait_ge(setup_step.sem, s0 + 4)
                    n = 0
                    for k, key in enumerate(("src", "dst")):
                        sp.dma_start(keys_in[0:full, k, :], t[key][0:full * KP].rearrange("(p k) -> p k", k=KP)).then_inc(setup_dma.sem, 16)
                        n += 1
                        if rest:
                            sp.dma_start(keys_in[full:full + 1, k, 0:rest], t[key][full * KP:E].rearrange("(p k) -> p k", p=1)).then_inc(setup_dma.sem, 16)
                            n += 1
                    sp.wait_ge(setup_dma.sem, d0 + 16 * n)
                    sp.dma_start(src_pad.rearrange("(p k) -> p k", k=KP), keys_in[:, 0, :]).then_inc(setup_dma.sem, 16)
                    sp.dma_start(dst_pad[J:J + EP].rearrange("(p k) -> p k", k=KP), keys_in[:, 1, :]).then_inc(setup_dma.sem, 16)
                    n += 2
                    for table in (dst_pad, key_pad):
                        for at in (0, J + EP):
                            sp.dma_start(table[at:at + J].rearrange("(o j) -> o j", o=1), edge_marks[:, :]).then_inc(setup_dma.sem, 16)
                            n += 1
                    for k in range(-(-N // (P * 512))):
                        lo, hi = k * P * 512, min(N, (k + 1) * P * 512)
                        w = (hi - lo) // P
                        if w:
                            sp.dma_start(pos_nodes[lo:lo + w * P, :].rearrange("(p w) o -> p (w o)", p=P), key_big[:, 0:w]).then_inc(setup_dma.sem, 16)
                            n += 1
                        r = (hi - lo) - w * P
                        if r:
                            sp.dma_start(pos_nodes[hi - r:hi, :].rearrange("(o w) u -> o (w u)", o=1), key_big[0:1, 0:r]).then_inc(setup_dma.sem, 16)
                            n += 1
                    with sp.Fori(0, NB - 1) as b:
                        sp.dma_start(rows(attn_nodes, b), zeros[:, :].rearrange("p (j d) -> p j d", j=J)).then_inc(attn_zeroed.sem, 16)
                    sp.dma_start(attn_nodes[(NB - 1) * BLK:N, :].rearrange("(p j) d -> p j d", j=J),
                                 zeros[OVER:P, :].rearrange("p (j d) -> p j d", j=J)).then_inc(attn_zeroed.sem, 16)
                    sp.wait_ge(setup_dma.sem, d0 + 16 * n)
                    step_total[0] = d0 + 16 * n

            setup_step.base += 4
            setup_dma.base = step_total[0]

        segment_phase(dst_pad, "dst", True, last_dst_idx[:, :], rep_mask[:, :], same_dst)

        def hold(engine, sem, value):
            engine.wait_ge(sem, value)
            engine.sem_inc(held[engine.engine].sem, 1)

        def in_turns(pool, slots, issue, finish):
            turns, rest = EB // slots, EB % slots
            for slot in range(min(slots, EB)):
                issue(slot, 0, slot)
            if turns > 1:
                with pool.Fori(1, turns) as n:
                    for slot in range(slots):
                        finish(slot, n - 1, (n - 1) * slots + slot)
                        issue(slot, n, n * slots + slot)
            for slot in range(rest if turns else 0):
                finish(slot, turns - 1, (turns - 1) * slots + slot)
                issue(slot, turns, turns * slots + slot)
            for slot in range(min(slots, EB)):
                last = turns if slot < rest else turns - 1
                if turns == 0:
                    last = 0
                finish(slot, last, last * slots + slot)

        def turns_of(slot, slots):
            return EB // slots + (slot < EB % slots)

        with ExitStack() as c:
            iota_edge = sb("iota_edge", [P, ET], i32, c)
            src_i = sb("src_i", [P, EB, J], i32, c)
            dst_i = sb("dst_i", [P, EB, J], i32, c)
            slot_i = sb("slot_i", [P, ET], i32, c)
            slot_f = sb("slot_f", [P, ET], f32, c)
            home_i = sb("home_i", [P, ET], i32, c)
            home_f = sb("home_f", [P, ET], f32, c)
            pos_i = sb("pos_i", [P, NB, J], i32, c)
            val_stage = [sb(f"val_stage{k}", [P, J], i32, c) for k in range(EL)]
            slots_written = counted("slots_written")
            slots_read = counted("slots_read")
            length_dma = counted("length_dma")
            length_step = counted("length_step")
            CH = EP // 4 if EP % (4 * J) == 0 else EP
            run = sb("run", [1, CH], f32, c)
            length = sb("length", [1, CH + 1], f32, c)
            one_row = sb("one_row", [1, CH], f32, c)
            with nc.Block() as block:
                d0, s0, g0 = setup_dma.base, setup_step.base, [g.base for g in gathered]

                @block.sync
                def _(sp):
                    sp.dma_start(src_i[:, :, :], cols_bj(src_pad[:])).then_inc(setup_dma.sem, 16)
                    sp.dma_start(dst_i[:, :, :], cols_bj(dst_pad[J:J + EP])).then_inc(setup_dma.sem, 16)
                    for k in range(EP // CH):
                        if k:
                            sp.wait_ge(length_step.sem, 1 + 2 * k)
                        sp.dma_start(run[0:1, :], same_dst[k * CH:(k + 1) * CH].rearrange("(o n) -> o n", o=1)).then_inc(length_dma.sem, 16)
                        sp.wait_ge(length_step.sem, 1 + 2 * (k + 1))
                        sp.dma_start(inv_deg[k * CH:(k + 1) * CH].rearrange("(o n) -> o n", o=1), run[0:1, :]).then_inc(length_dma.sem, 16)
                        sp.wait_ge(length_dma.sem, 32 * (k + 1))
                    sp.wait_ge(slots_written.sem, 1)
                    sp.dma_start(pos_i[:, 0:NB - 1, :], pos_nodes[0:(NB - 1) * BLK, :].rearrange("(b p j) o -> p b (j o)", p=P, j=J)).then_inc(setup_dma.sem, 16)
                    sp.dma_start(pos_i[:, NB - 1, :], pos_nodes[N - BLK:N, :].rearrange("(p j) o -> p (j o)", j=J)).then_inc(setup_dma.sem, 16)

                @block.vector
                def _(dve):
                    dve.wait_ge(setup_dma.sem, d0 + 32)
                    dve.tensor_scalar(src_clamped[:, :], src_i[:, :, :].rearrange("p b j -> p (b j)"), float(N - 1), None, ALU.min).then_inc(setup_step.sem, 1)
                    dve.tensor_scalar(dst_clamped[:, :], dst_i[:, :, :].rearrange("p b j -> p (b j)"), float(N - 1), None, ALU.min).then_inc(setup_step.sem, 1)
                    dve.memset(one_row[0:1, :], 1.0).then_inc(length_step.sem, 1)
                    for k in range(EP // CH):
                        dve.wait_ge(length_step.sem, 1 + 2 * k)
                        dve.wait_ge(length_dma.sem, 32 * k + 16)
                        dve.tensor_tensor_scan(length[0:1, 1:CH + 1], run[0:1, :], one_row[0:1, :],
                                               length[0:1, CH:CH + 1] if k else 0.0, ALU.mult, ALU.add).then_inc(length_step.sem, 1)
                        dve.wait_ge(length_step.sem, 2 + 2 * k)
                        dve.reciprocal(run[0:1, :], length[0:1, 1:CH + 1]).then_inc(length_step.sem, 1)
                    dve.wait_ge(setup_dma.sem, d0 + 64)
                    dve.tensor_scalar(node_mask[:, :], pos_i[:, :, :].rearrange("p b j -> p (b j)"), float(BIG), None, ALU.is_equal).then_inc(setup_step.sem, 1)
                    dve.wait_ge(setup_step.sem, s0 + 4)
                    dve.memset(node_mask[0:max(OVER, 1), (NB - 1) * J:NB * J], 0.0).then_inc(setup_step.sem, 1)
                    dve.wait_ge(slots_read.sem, 1)
                    dve.tensor_scalar(slot_f[:, :], slot_i[:, :], 2.0, 1.0, ALU.mult, ALU.add).then_inc(setup_step.sem, 1)
                    dve.tensor_scalar(home_f[:, :], home_i[:, :], 2.0, 1.0, ALU.mult, ALU.add).then_inc(setup_step.sem, 1)
                    dve.wait_ge(setup_step.sem, s0 + 7)
                    dve.tensor_copy(link_idx[:, :], slot_f[:, :]).then_inc(setup_step.sem, 1)
                    dve.tensor_copy(home_idx[:, :], home_f[:, :]).then_inc(setup_step.sem, 1)
                    dve.wait_ge(setup_step.sem, s0 + 9)

                @block.gpsimd
                def _(pool):
                    def write_slots(slot, n, b):
                        pool.tensor_copy(idx_stage[slot][:, 0:J], last_dst_idx[:, ds(b * J, J)]).then_inc(staged[slot].sem, 1)
                        pool.tensor_copy(val_stage[slot][:, :], iota_edge[:, ds(b * J, J)]).then_inc(staged[slot].sem, 1)
                        hold(pool, staged[slot].sem, n * 2 + (staged[slot].base + 2))
                        for j in range(J):
                            pool.indirect_dma_start(pos_nodes[:, :], bass.IndirectOffsetOnAxis(idx_stage[slot][:, j:j + 1], 0),
                                                    val_stage[slot][:, j:j + 1], None, bounds_check=N - 1,
                                                    oob_is_err=False).then_inc(gathered[slot].sem, 16)

                    def written(slot, n, b):
                        hold(pool, gathered[slot].sem, n * (16 * J) + (gathered[slot].base + 16 * J))

                    pool.iota(iota_edge[:, :], pattern=[[BLK, EB], [1, J]], base=0, channel_multiplier=J).then_inc(setup_step.sem, 1)
                    pool.wait_ge(setup_step.sem, s0 + 3)
                    in_turns(pool, EL, write_slots, written)
                    pool.nop().then_inc(slots_written.sem, 1)
                    for slot in range(EL):
                        staged[slot].base += 2 * turns_of(slot, EL)
                        gathered[slot].base += 16 * J * turns_of(slot, EL)
                    for table, found in ((src_clamped, slot_i), (dst_clamped, home_i)):
                        def read_slots(slot, n, b):
                            pool.tensor_copy(idx_stage[slot][:, 0:J], table[:, ds(b * J, J)]).then_inc(staged[slot].sem, 1)
                            hold(pool, staged[slot].sem, n * 2 + (staged[slot].base + 1))
                            for j in range(J):
                                pool.indirect_dma_start(val_stage[slot][:, j:j + 1], None, pos_nodes[:, :],
                                                        bass.IndirectOffsetOnAxis(idx_stage[slot][:, j:j + 1], 0),
                                                        bounds_check=N - 1, oob_is_err=False).then_inc(gathered[slot].sem, 16)

                        def keep_slots(slot, n, b):
                            hold(pool, gathered[slot].sem, n * (16 * J) + (gathered[slot].base + 16 * J))
                            pool.tensor_copy(found[:, ds(b * J, J)], val_stage[slot][:, :]).then_inc(staged[slot].sem, 1)
                            hold(pool, staged[slot].sem, n * 2 + (staged[slot].base + 2))

                        in_turns(pool, EL, read_slots, keep_slots)
                        for slot in range(EL):
                            staged[slot].base += 2 * turns_of(slot, EL)
                            gathered[slot].base += 16 * J * turns_of(slot, EL)
                    pool.nop().then_inc(slots_read.sem, 1)
            setup_dma.base += 64
            setup_step.base += 9

        with ExitStack() as c:
            rec_i = sb("rec_i", [P, EB, J, 2], i32, c)
            tile_major = [sb(f"sort_keys{k}", [P, ET], i32, c) for k in range(2)]
            digit_i = sb("digit_i", [P, ET], i32, c)
            digit = sb("digit", [P, ET], bf16, c)
            digit_iota = sb("digit_iota", [P, RADIX], bf16, c)
            onehot = sb("onehot", [P, ET * RADIX], bf16, c)
            earlier = sb("earlier", [P, P], bf16, c)
            ones_bf = sb("ones_bf", [P, P], bf16, c)
            counts = sb("counts", [P, RADIX * ET], f32, c)
            place = sb("place", [P, ET * RADIX], f32, c)
            rank = sb("rank", [P, ET], f32, c)
            rank_i = [sb(f"rank_i{k}", [P, ET], i32, c) for k in range(4)]
            rec_stage = [sb(f"rec_stage{k}", [P, J, 2], i32, c) for k in range(EL)]
            rank_made = counted("rank_made")
            src_i_again = sb("src_i_again", [P, EB, J], i32, c)
            iota_again = sb("iota_again", [P, ET], i32, c)
            setup_edge = counted("sort_constants")
            setup_edge0 = counted("sort_zeros")
            TPC = 512 // RADIX
            NCH = ET // TPC
            for n_pass in range(PASSES):
                last_pass = n_pass == PASSES - 1
                with nc.Block() as block:
                    d0, s0 = setup_dma.base, setup_step.base
                    c0, r0 = chain[0].base, chain[1].base
                    m0 = rank_made.base

                    @block.sync
                    def _(sp):
                        if n_pass:
                            sp.dma_start(rec_i[:, :, :, :], sorting[(n_pass - 1) % 2].rearrange("(b p j) t -> p b (j t)", p=P, j=J)).then_inc(setup_dma.sem, 16)
                        else:
                            sp.dma_start(src_i_again[:, :, :], cols_bj(src_pad[:])).then_inc(setup_dma.sem, 16)

                    @block.vector
                    def _(dve):
                        step = [s0]

                        def link(op):
                            step[0] += 1
                            op.then_inc(setup_step.sem, 1)
                            dve.wait_ge(setup_step.sem, step[0])

                        dve.wait_ge(setup_dma.sem, d0 + 16)
                        if n_pass == 0:
                            dve.wait_ge(setup_edge.sem, 4)
                            link(dve.tensor_copy(rec_i[:, :, :, 0], src_i_again[:, :, :]))
                            link(dve.tensor_copy(rec_i[:, :, :, 1], iota_again[:, :].rearrange("p (b j) -> p b j", j=J)))
                        keys = rec_i[:, :, :, 0].rearrange("p b j -> p (b j)")
                        link(dve.tensor_copy(tile_major[0][:, :], keys))
                        link(dve.tensor_scalar(digit_i[:, :], tile_major[0][:, :], DIGIT * n_pass, RADIX - 1,
                                               ALU.logical_shift_right, ALU.bitwise_and))
                        link(dve.tensor_copy(digit[:, :], digit_i[:, :]))
                        link(dve.tensor_tensor(onehot[:, :].rearrange("p (t r) -> p t r", r=RADIX),
                                               digit[:, :].unsqueeze(2).broadcast_to([P, ET, RADIX]),
                                               digit_iota[:, :].unsqueeze(1).broadcast_to([P, ET, RADIX]), ALU.is_equal))
                        dve.wait_ge(chain[1].sem, r0 + NCH)
                        link(dve.tensor_tensor_scan(counts[:, :], counts[:, :], counts[:, :], 0.0, ALU.add, ALU.bypass))
                        for k in range(NCH):
                            dve.wait_ge(chain[2].sem, chain[2].base + k + 1)
                            bank = work[:, (3 + k % 3) * 512:(4 + k % 3) * 512]
                            dve.tensor_tensor(place[:, k * 512:(k + 1) * 512].rearrange("p (t r) -> p t r", r=RADIX),
                                              bank.rearrange("p (t r) -> p t r", r=RADIX),
                                              counts[:, :].rearrange("p (r t) -> p t r", r=RADIX)[:, k * TPC:(k + 1) * TPC, :],
                                              ALU.add).then_inc(rank_made.sem, 1)
                        dve.wait_ge(rank_made.sem, m0 + NCH)
                        link(dve.tensor_tensor(place[:, :], place[:, :], onehot[:, :], ALU.mult))
                        link(dve.tensor_reduce(rank[:, :], place[:, :].rearrange("p (t r) -> p t r", r=RADIX), AX, ALU.add))
                        link(dve.tensor_copy(rank_i[0][:, :], rank[:, :]))
                        if last_pass:
                            link(dve.tensor_copy(rank_i[3][:, :], rank_i[0][:, :]))
                        else:
                            link(dve.tensor_scalar(rank_i[1][:, :], rank_i[0][:, :], P - 1, J.bit_length() - 1, ALU.bitwise_and, ALU.logical_shift_left))
                            link(dve.tensor_scalar(rank_i[2][:, :], rank_i[0][:, :], P.bit_length() - 1, J - 1, ALU.logical_shift_right, ALU.bitwise_and))
                            link(dve.tensor_tensor(rank_i[1][:, :], rank_i[1][:, :], rank_i[2][:, :], ALU.bitwise_or))
                            link(dve.tensor_scalar(rank_i[2][:, :], rank_i[0][:, :], BLK.bit_length() - 1, BLK.bit_length() - 1, ALU.logical_shift_right, ALU.logical_shift_left))
                            link(dve.tensor_tensor(rank_i[3][:, :], rank_i[1][:, :], rank_i[2][:, :], ALU.bitwise_or))
                        step_total[0] = step[0]

                    onehot_step = s0 + (6 if n_pass == 0 else 4)

                    @block.tensor
                    def _(pe):
                        pe.wait_ge(setup_step.sem, onehot_step)
                        for k in range(NCH):
                            if k >= 3:
                                pe.wait_ge(chain[1].sem, r0 + k - 2)
                            pe.matmul(work[:, (k % 3) * 512:(k % 3 + 1) * 512], ones_bf[:, :], onehot[:, k * 512:(k + 1) * 512],
                                      start=True, stop=True).then_inc(chain[0].sem, 1)
                        for k in range(NCH):
                            if k >= 3:
                                pe.wait_ge(rank_made.sem, m0 + k - 2)
                            pe.matmul(work[:, (3 + k % 3) * 512:(4 + k % 3) * 512], earlier[:, :], onehot[:, k * 512:(k + 1) * 512],
                                      start=True, stop=True).then_inc(chain[2].sem, 1)

                    @block.scalar
                    def _(act):
                        for k in range(NCH):
                            act.wait_ge(chain[0].sem, c0 + k + 1)
                            act.activation(counts[:, :].rearrange("p (r t) -> p t r", r=RADIX)[:, k * TPC:(k + 1) * TPC, :],
                                           work[:, (k % 3) * 512:(k % 3 + 1) * 512].rearrange("p (t r) -> p t r", r=RADIX),
                                           ACT.Copy).then_inc(chain[1].sem, 1)

                    n_links = 7 + (2 if n_pass == 0 else 0) + 2 + (1 if last_pass else 5)
                    rank_step = s0 + (6 if n_pass == 0 else 4) + 1 + 3 + (1 if last_pass else 5)

                    @block.gpsimd
                    def _(pool):
                        if n_pass == 0:
                            pool.iota(iota_again[:, :], pattern=[[BLK, EB], [1, J]], base=0, channel_multiplier=J).then_inc(setup_edge.sem, 1)
                            pool.iota(digit_iota[:, :], pattern=[[1, RADIX]], base=0, channel_multiplier=0,
                                      allow_small_or_imprecise_dtypes=True).then_inc(setup_edge.sem, 1)
                            pool.memset(ones_bf[:, :], 1.0).then_inc(setup_edge.sem, 1)
                            pool.memset(earlier[:, :], 0.0).then_inc(setup_edge0.sem, 1)
                            pool.wait_ge(setup_edge0.sem, 1)
                            pool.affine_select(out=earlier[:, :], in_=earlier[:, :], compare_op=ALU.is_gt, fill=-1.0,
                                               base=0, pattern=[[1, P]], channel_multiplier=-1).then_inc(setup_edge.sem, 1)
                        pool.wait_ge(setup_step.sem, rank_step)
                        def scatter(slot, n, b):
                            pool.tensor_copy(idx_stage[slot][:, 0:J], rank_i[3][:, ds(b * J, J)]).then_inc(staged[slot].sem, 1)
                            pool.tensor_copy(rec_stage[slot][:, :, :].rearrange("p j t -> p (j t)"),
                                             rec_i[:, :, :, :].rearrange("p b j t -> p (b j t)")[:, ds(b * (2 * J), 2 * J)]).then_inc(staged[slot].sem, 1)
                            hold(pool, staged[slot].sem, n * 2 + (staged[slot].base + 2))
                            for j in range(J):
                                pool.indirect_dma_start(sorting[n_pass % 2][:, :], bass.IndirectOffsetOnAxis(idx_stage[slot][:, j:j + 1], 0),
                                                        rec_stage[slot][:, j, :], None, bounds_check=EP - 1,
                                                        oob_is_err=False).then_inc(gathered[slot].sem, 16)

                        def scattered_to_rank(slot, n, b):
                            hold(pool, gathered[slot].sem, n * (16 * J) + (gathered[slot].base + 16 * J))

                        in_turns(pool, EL, scatter, scattered_to_rank)
                        for slot in range(EL):
                            staged[slot].base += 2 * turns_of(slot, EL)
                            gathered[slot].base += 16 * J * turns_of(slot, EL)
                assert step_total[0] == rank_step, (step_total[0], rank_step)
                setup_step.base = step_total[0]
                setup_dma.base += 16
                chain[0].base += NCH
                chain[1].base += NCH
                chain[2].base += NCH
                rank_made.base += NCH

            key_lin = sb("key_lin", [P, EB, J], i32, c)
            with nc.Block() as block:
                d0, s0 = setup_dma.base, setup_step.base

                @block.sync
                def _(sp):
                    sp.dma_start(rec_i[:, :, :, :], sorting[(PASSES - 1) % 2].rearrange("(b p j) t -> p b (j t)", p=P, j=J)).then_inc(setup_dma.sem, 16)
                    sp.wait_ge(setup_step.sem, s0 + 2)
                    sp.dma_start(cols_bj(key_pad[J:J + EP]), key_lin[:, :, :]).then_inc(setup_dma.sem, 16)
                    sp.wait_ge(setup_dma.sem, d0 + 32)

                @block.vector
                def _(dve):
                    dve.wait_ge(setup_dma.sem, d0 + 16)
                    dve.tensor_copy(key_lin[:, :, :], rec_i[:, :, :, 0]).then_inc(setup_step.sem, 1)
                    dve.tensor_copy(sorted_edge[:, :], rec_i[:, :, :, 1].rearrange("p b j -> p (b j)")).then_inc(setup_step.sem, 1)
            setup_dma.base += 32
            setup_step.base += 2
        with ExitStack() as c:
            rep_src = sb("rep_src", [P, ET], f32, c)
            segment_phase(key_pad, "key", False, attn_out_idx[:, :], rep_src[:, :], neg_start)
        def lane_tiles(name, lanes, width=BLK):
            return [sb(f"{name}{k}", [P, width]) for k in range(lanes)]

        W = J * D
        rows_in = lane_tiles("rows_in", EL)
        centered = lane_tiles("centered", EL)
        squares = lane_tiles("squares", EL)
        feat = lane_tiles("feat", EL)
        feat_out = lane_tiles("feat_out", EL)
        rows_out = lane_tiles("rows_out", EL)
        resid = lane_tiles("resid", EL)
        masked = lane_tiles("masked", DL, J * (D + 1))
        stats = lane_tiles("stats", DL, 4 * 2 * J)
        agg = lane_tiles("agg", EL, BLK + 1)
        mean_agg = lane_tiles("mean_agg", EL)
        flags = lane_tiles("flags", EL)
        inverse = lane_tiles("inverse", EL)
        edge_in = lane_tiles("edge_in", EL)
        edge_rows = resid
        record_rows = mean_agg
        running_max = agg
        messages = centered

        def node_lanes(tiles):
            return [tiles[k // 2][:, (k % 2) * W:(k % 2 + 1) * W] for k in range(DL)]

        assert DL == 2 * EL
        n_rows_in, n_centered, n_squares, n_feat, n_feat_out, n_rows_out, n_resid = (
            node_lanes(tiles) for tiles in (rows_in, centered, squares, feat, feat_out, rows_out, resid))
        moments = sb("moments", [D, D + 1])
        moments_edges = sb("moments_edges", [D, D + 1])
        w1_moments = sb("w1_moments", [D, H])
        coef = sb("coef", [P, 8])

        class Steps:

            def __init__(self, names, lanes, blocks, loads=0, more=0, stores=1, gathers=0):
                self.names, self.K, self.lanes = names, len(names), lanes
                self.rounds = (blocks - 1) // lanes
                self.rest = blocks - self.rounds * lanes
                self.per = dict(loaded=16 * loads, more=16 * more, stored=16 * stores, gathered=16 * gathers)
                self.base = [s.base for s in chain]
                self.at = {k: [s.base for s in sems] for k, sems in lane_sems.items()}

            def after(self, lane, i, name):
                return i * self.K + (self.base[lane] + self.names.index(name) + 1)

            def start(self, lane, i):
                return i * self.K + self.base[lane]

            def dma(self, what, lane, i, rounds=1):
                return i * self.per[what] + (self.at[what][lane] + rounds * self.per[what])

            def run_in_order(self, engine, body):
                if self.rounds:
                    with engine.Fori(0, self.rounds) as i:
                        body(i, range(self.lanes))
                body(self.rounds, range(self.rest))

            def run(self, engine, body):
                slots = self.names + ["end"]
                T = len(slots)

                def pass_through(i):
                    for slot in range(T):
                        def at(step):
                            due = []
                            for lane in range(self.lanes):
                                late = lane * T // self.lanes
                                if (slots.index(step) + late) % T == slot:
                                    k = i if slot >= late else i - 1
                                    if not isinstance(k, int) or 0 <= k < self.rounds + (lane < self.rest):
                                        due.append((k, lane))
                            return due
                        body(at)

                pass_through(0)
                if self.rounds > 1:
                    with engine.Fori(1, self.rounds) as i:
                        pass_through(i)
                if self.rounds:
                    pass_through(self.rounds)
                pass_through(self.rounds + 1)

            def close(self):
                for k in range(self.lanes):
                    n = self.rounds + (k < self.rest)
                    chain[k].base += n * self.K
                    for what, sems in lane_sems.items():
                        if k < len(sems):
                            sems[k].base += n * self.per[what]

        more_loaded = [counted(f"lane{k}_more_loaded") for k in range(DL)]
        lane_sems = dict(loaded=loaded, more=more_loaded, stored=stored, gathered=gathered)
        gather_ready = [counted(f"lane{k}_gather_indices") for k in range(EL)]
        scattered = [counted(f"lane{k}_scattered") for k in range(EL)]
        scatter_ready = [counted(f"lane{k}_scatter_indices") for k in range(EL)]
        scatter_done = [counted(f"lane{k}_scatter_done") for k in range(EL)]
        resid_saved = [counted(f"lane{k}_residual_saved") for k in range(EL)]

        LN = ["ln_sum", "ln_center", "ln_square", "ln_var", "ln_root", "ln_inverse", "ln_out"]

        def ln_vector(dve, S, at, ready, src, centered, squares, T, tag=""):
            def x(lane):
                return src[lane][:, 0:T * D].rearrange("p (t d) -> p t d", d=D)

            def c(lane):
                return centered[lane][:, 0:T * D].rearrange("p (t d) -> p t d", d=D)

            for i, lane in at(tag + "ln_sum"):
                ready(i, lane)
                dve.tensor_reduce(stats[lane][:, 0:T], x(lane), AX, ALU.add).then_inc(chain[lane].sem, 1)
            for i, lane in at(tag + "ln_center"):
                dve.wait_ge(chain[lane].sem, S.after(lane, i, tag + "ln_sum"))
                dve.scalar_tensor_tensor(c(lane), stats[lane][:, 0:T].unsqueeze(2).broadcast_to([P, T, D]), -1.0 / D, x(lane),
                                         ALU.mult, ALU.add).then_inc(chain[lane].sem, 1)
            for i, lane in at(tag + "ln_var"):
                dve.wait_ge(chain[lane].sem, S.after(lane, i, tag + "ln_square"))
                dve.tensor_reduce(stats[lane][:, 16:16 + T], squares[lane][:, 0:T * D].rearrange("p (t d) -> p t d", d=D), AX,
                                  ALU.add).then_inc(chain[lane].sem, 1)
            for i, lane in at(tag + "ln_inverse"):
                dve.wait_ge(chain[lane].sem, S.after(lane, i, tag + "ln_root"))
                dve.reciprocal(stats[lane][:, 32:32 + T], stats[lane][:, 48:48 + T]).then_inc(chain[lane].sem, 1)
            for i, lane in at(tag + "ln_out"):
                dve.wait_ge(chain[lane].sem, S.after(lane, i, tag + "ln_inverse"))
                dve.scalar_tensor_tensor(c(lane), c(lane), 0.0, stats[lane][:, 32:32 + T].unsqueeze(2).broadcast_to([P, T, D]),
                                         ALU.max, ALU.mult).then_inc(chain[lane].sem, 1)

        def ln_scalar(act, S, at, centered, squares, T, tag=""):
            for i, lane in at(tag + "ln_square"):
                act.wait_ge(chain[lane].sem, S.after(lane, i, tag + "ln_center"))
                act.activation(squares[lane][:, 0:T * D], centered[lane][:, 0:T * D], ACT.Square).then_inc(chain[lane].sem, 1)
            for i, lane in at(tag + "ln_root"):
                act.wait_ge(chain[lane].sem, S.after(lane, i, tag + "ln_var"))
                act.activation(stats[lane][:, 48:48 + T], stats[lane][:, 16:16 + T], ACT.Sqrt, bias=eps_ln[:, :],
                               scale=1.0 / D).then_inc(chain[lane].sem, 1)

        def edge_psum(lane):
            return work[:, lane * 1024:(lane + 1) * 1024]

        def node_psum(lane):
            return work[:, lane * 512:(lane + 1) * 512]

        def tiles_of(tile, j):
            return tile.rearrange("f (p j) -> f j p", j=J)[:, j, :]

        def in_order(tile):
            return tile.rearrange("f (p j) -> f p j", j=J)

        def by_tile(bank):
            return bank.rearrange("f (j p) -> f p j", p=P)

        cleared = agg + mean_agg + feat_out + masked + resid + edge_in
        lane_counts = chain + loaded + more_loaded + stored + scatter_done + scatter_ready + gather_ready + resid_saved
        with nc.Block() as block:
            @block.vector
            def _(dve):
                for tile in cleared:
                    dve.memset(tile[:, :], 0.0).then_inc(setup_step.sem, 1)
                dve.wait_ge(setup_step.sem, setup_step.base + len(cleared))

            @block.gpsimd
            def _(pool):
                for c in lane_counts:
                    pool.sem_inc(c.sem, 64)
        setup_step.base += len(cleared)
        for c in lane_counts:
            c.base += 64

        def edge_phase(kind, l, source, tin, tout, ln=False, add_resid=False):
            names = list(LN) if ln else []
            names += ["t_in", "feat"]
            if kind == "gnn":
                names += ["edge_mm", "edge_act"] if l > 0 else ["edge_t", "edge_feat"]
                names += ["edge_pair", "msg_mm", "msg_act"]
            if kind in ("sage", "gnn"):
                names += ["scan", "mean"]
            if kind in ("sage", "gnn", "proj"):
                names += ["mm", "act", "t_out"]
                if kind == "gnn":
                    names += ["l2_square", "l2_sum", "l2_root", "l2_floor", "l2_inverse"]
                names += ["rows"]
                if kind == "gnn" and add_resid:
                    names += ["add_resid"]
            if kind == "gin":
                names += ["scan", "z", "z_rows", "z_masked", "z_mask", "gram"]
            if kind == "qkv":
                names += ["qk_mm", "q_bias", "k_bias", "v_mm", "v_bias", "q_times_k", "dot", "score", "max_score"]
            last = names[-1]
            scans = kind in ("sage", "gnn", "gin")
            homes = source == "links" and kind in ("qkv", "gnn")
            gathers = {"nodes": 2 * J, "attention": 2 * J, "links": J * (1 + homes), "rows": 0}[source]
            save_resid = ln
            n_more = 2 * (kind in ("sage", "gnn")) + (kind == "gin") + add_resid + (kind == "gnn")
            n_load = int(source in ("links", "rows"))
            n_store = {"sage": 1, "proj": 1, "qkv": 1, "gin": 2, "gnn": 1 + (l < 2)}[kind]
            S = Steps(names, EL, EB, loads=n_load, more=n_more, stores=n_store, gathers=gathers)
            stage0 = [g.base for g in gather_ready]
            saved0 = [g.base for g in resid_saved]
            nodes = {"nodes": t["x"], "attention": attn_nodes, "links": None, "rows": None}[source]
            slots = tin.rearrange("e (h d) -> (e h) d", h=2) if source == "links" else None
            reads_rows = "ln_center" if ln else "t_in"
            relu = ACT.Relu if kind != "proj" else ACT.Identity
            w = {"sage": sage, "gnn": gnn, "proj": [dict(own=w_o, agg=None, bias=b_o)], "gin": gin, "qkv": [None] * 3}[kind]
            w = w[0] if kind == "proj" else w[l]

            with nc.Block() as block:
                @block.sync
                def _(sp):
                    if kind == "gnn" and l == 0:
                        pass

                    def body(i, lanes):
                        for lane in lanes:
                            b = i * EL + lane
                            if n_load:
                                hold(sp, chain[lane].sem, S.after(lane, i - 1, reads_rows))
                                if save_resid:
                                    hold(sp, resid_saved[lane].sem, i * 16 + saved0[lane])
                                sp.dma_start(rows_in[lane][:, :].rearrange("p (j d) -> p j d", j=J), rows(tin, b)).then_inc(loaded[lane].sem, 16)
                        for lane in lanes:
                            b = i * EL + lane
                            if add_resid or kind == "gnn":
                                hold(sp, chain[lane].sem, S.start(lane, i))
                            elif scans:
                                hold(sp, chain[lane].sem, S.after(lane, i - 1, "mean" if kind == "sage" else "scan"))
                            if kind == "gnn" and l > 0:
                                hold(sp, stored[lane].sem, S.dma("stored", lane, i, rounds=0))
                            if kind in ("sage", "gnn", "gin"):
                                sp.dma_start(flags[lane][0:D, :], same_dst[ds(b * BLK, BLK)].partition_broadcast(D)).then_inc(more_loaded[lane].sem, 16)
                            if kind in ("sage", "gnn"):
                                sp.dma_start(inverse[lane][0:D, :], inv_deg[ds(b * BLK, BLK)].partition_broadcast(D)).then_inc(more_loaded[lane].sem, 16)
                            if add_resid:
                                sp.dma_start(resid[lane][:, :].rearrange("p (j d) -> p j d", j=J), rows(sd_resid, b)).then_inc(more_loaded[lane].sem, 16)
                            if kind == "gnn":
                                if l > 0:
                                    sp.dma_start(edge_in[lane][D:P, :], edge_state[ds(b, 1), :, :].rearrange("o f e -> (o f) e")).then_inc(more_loaded[lane].sem, 16)
                                elif isinstance(i, int) and i * EL + lane == EB - 1:
                                    n_last = (E - (EB - 1) * BLK) // J
                                    sp.dma_start(edge_rows[lane][0:n_last, :].rearrange("p (j d) -> p j d", j=J)[:, :, D:P],
                                                 t["edge_attr_64"][(EB - 1) * BLK:E, :].rearrange("(p j) d -> p j d", j=J)).then_inc(more_loaded[lane].sem, 16)
                                else:
                                    sp.dma_start(edge_rows[lane][:, :].rearrange("p (j d) -> p j d", j=J)[:, :, D:P],
                                                 rows(t["edge_attr_64"], b)).then_inc(more_loaded[lane].sem, 16)
                    S.run_in_order(sp, body)

                @block.gpsimd
                def _(pool):
                    def body(i, lanes):
                        for lane in lanes:
                            b = i * EL + lane
                            if source == "rows":
                                continue
                            if source == "links":
                                tables = [(link_idx, 0)] + [(home_idx, D)] * homes
                                hold(pool, loaded[lane].sem, S.dma("loaded", lane, i))
                            else:
                                tables = [(src_clamped, 0), (dst_clamped, D)]
                                hold(pool, chain[lane].sem, S.after(lane, i - 1, reads_rows))
                                if save_resid:
                                    hold(pool, resid_saved[lane].sem, i * 16 + saved0[lane])
                            hold(pool, gathered[lane].sem, S.dma("gathered", lane, i, rounds=0))
                            for k, (table, _) in enumerate(tables):
                                pool.tensor_copy(idx_stage[lane][:, k * J:(k + 1) * J], table[:, ds(b * J, J)]).then_inc(gather_ready[lane].sem, 1)
                            hold(pool, gather_ready[lane].sem, i * len(tables) + (stage0[lane] + len(tables)))
                            for k, (_, at) in enumerate(tables):
                                for j in range(J):
                                    pool.indirect_dma_start(
                                        rows_in[lane][:, j * P + at:j * P + at + D], None, slots if source == "links" else nodes[:, :],
                                        bass.IndirectOffsetOnAxis(idx_stage[lane][:, k * J + j:k * J + j + 1], 0),
                                        bounds_check=(2 * EP - 1) if source == "links" else N - 1,
                                        oob_is_err=False).then_inc(gathered[lane].sem, 16)
                    S.run_in_order(pool, body)

                def rows_ready(engine, lane, i):
                    if gathers:
                        engine.wait_ge(gathered[lane].sem, S.dma("gathered", lane, i))
                    else:
                        engine.wait_ge(loaded[lane].sem, S.dma("loaded", lane, i))

                @block.tensor
                def _(pe):
                    if kind == "gin":
                        pe.matmul(gram_edges[0:D, 0:D + 1], zeros[:, 0:D], zeros[:, 0:D + 1], start=True, stop=True)

                    def body(at):
                        for i, lane in at("t_in"):
                            A = edge_psum(lane)
                            if ln:
                                pe.wait_ge(chain[lane].sem, S.after(lane, i, "ln_out"))
                            else:
                                pe.wait_ge(chain[lane].sem, S.start(lane, i))
                                rows_ready(pe, lane, i)
                            src = centered[lane] if ln else rows_in[lane]
                            for j in range(J):
                                op = pe.transpose(A[:, j * P:(j + 1) * P], src[:, j * P:(j + 1) * P], ident[:, :])
                            op.then_inc(chain[lane].sem, 1)
                        if kind == "gnn":
                            for i, lane in at("edge_mm" if l else "edge_t"):
                                A = edge_psum(lane)
                                pe.wait_ge(chain[lane].sem, S.after(lane, i, "feat"))
                                pe.wait_ge(more_loaded[lane].sem, S.dma("more", lane, i))
                                if l == 0:
                                    for j in range(J):
                                        op = pe.transpose(A[:, j * P:(j + 1) * P], edge_rows[lane][:, j * P:(j + 1) * P], ident[:, :])
                                else:
                                    for h in range(2):
                                        c = slice(h * 512, (h + 1) * 512)
                                        pe.matmul(A[:, c], w["edge_nodes"][:, :], feat[lane][:, c], start=True, stop=False)
                                        op = pe.matmul(A[:, c], w["edge_own"][:, :], edge_in[lane][:, c], start=False, stop=True)
                                op.then_inc(chain[lane].sem, 1)
                            for i, lane in at("msg_mm"):
                                A = edge_psum(lane)
                                pe.wait_ge(chain[lane].sem, S.after(lane, i, "edge_pair"))
                                for h in range(2):
                                    c = slice(h * 512, (h + 1) * 512)
                                    op = pe.matmul(A[0:D, c], w["msg"][:, :], edge_in[lane][:, c], start=True, stop=True)
                                op.then_inc(chain[lane].sem, 1)
                        if kind in ("sage", "gnn", "proj"):
                            for i, lane in at("mm"):
                                A = edge_psum(lane)
                                pe.wait_ge(chain[lane].sem, S.after(lane, i, "feat" if kind == "proj" else "mean"))
                                for h in range(2):
                                    c = slice(h * 512, (h + 1) * 512)
                                    op = pe.matmul(A[:, c], w["own"][:, :], feat[lane][:, c], start=True, stop=kind == "proj")
                                    if kind != "proj":
                                        op = pe.matmul(A[:, c], w["agg"][0:D, :], mean_agg[lane][0:D, c], start=False, stop=True)
                                op.then_inc(chain[lane].sem, 1)
                            for i, lane in at("t_out"):
                                A = edge_psum(lane)
                                pe.wait_ge(chain[lane].sem, S.after(lane, i, "act"))
                                for j in range(J):
                                    op = pe.transpose(A[:, j * P:(j + 1) * P], tiles_of(feat_out[lane][:, :], j), ident[:, :])
                                op.then_inc(chain[lane].sem, 1)
                        if kind == "gin":
                            for i, lane in at("z"):
                                A = edge_psum(lane)
                                pe.wait_ge(chain[lane].sem, S.after(lane, i, "scan"))
                                for j in range(J):
                                    c = slice(j * D, (j + 1) * D)
                                    pe.matmul(A[:, c], tiles_of(feat[lane][:, :], j), w["keep_ident"][:, :], start=True, stop=False)
                                    op = pe.matmul(A[:, c], tiles_of(agg[lane][0:D, 0:BLK], j), ident[0:D, 0:D], start=False, stop=True)
                                op.then_inc(chain[lane].sem, 1)
                            for i, lane in at("gram"):
                                pe.wait_ge(chain[lane].sem, S.after(lane, i, "z_mask"))
                                zm = masked[lane][:, :].rearrange("p (j d) -> p j d", j=J)
                                for j in range(J):
                                    op = pe.matmul(gram_edges[0:D, 0:D + 1], squares[lane][:, j * D:(j + 1) * D], zm[:, j, :],
                                                   start=False, stop=False, skip_group_check=True)
                                op.then_inc(chain[lane].sem, 1)
                        if kind == "qkv":
                            for i, lane in at("qk_mm"):
                                A = edge_psum(lane)
                                pe.wait_ge(chain[lane].sem, S.after(lane, i, "feat"))
                                for j in range(J):
                                    pe.matmul(A[:, j * D:(j + 1) * D], tiles_of(feat[lane][0:D, :], j), w_qkv[0:D, 0:D], start=True, stop=True)
                                for j in range(J):
                                    op = pe.matmul(A[:, W + j * D:W + (j + 1) * D], tiles_of(feat[lane][D:P, :], j), w_qkv[D:P, 0:D], start=True, stop=True)
                                op.then_inc(chain[lane].sem, 1)
                            for i, lane in at("v_mm"):
                                A = edge_psum(lane)
                                pe.wait_ge(chain[lane].sem, S.after(lane, i, "k_bias"))
                                for j in range(J):
                                    op = pe.matmul(A[:, j * D:(j + 1) * D], tiles_of(feat[lane][D:P, :], j), w_qkv[D:P, D:2 * D], start=True, stop=True)
                                op.then_inc(chain[lane].sem, 1)
                    S.run(pe, body)

                @block.scalar
                def _(act):
                    def body(at):
                        if save_resid:
                            for i, lane in at("ln_sum"):
                                b = i * EL + lane
                                rows_ready(act, lane, i)
                                act.dma_start(rows(sd_resid, b), rows_in[lane][:, :].rearrange("p (j d) -> p j d", j=J)).then_inc(resid_saved[lane].sem, 16)
                        if ln:
                            ln_scalar(act, S, at, centered, squares, 2 * J)
                        for i, lane in at("feat"):
                            A = edge_psum(lane)
                            act.wait_ge(chain[lane].sem, S.after(lane, i, "t_in"))
                            if kind == "gin":
                                act.wait_ge(stored[lane].sem, S.dma("stored", lane, i, rounds=0))
                            act.activation(in_order(feat[lane][:, :]), by_tile(A), ACT.Copy).then_inc(chain[lane].sem, 1)
                        if kind == "gnn":
                            for i, lane in at("edge_act" if l else "edge_feat"):
                                A = edge_psum(lane)
                                if l == 0:
                                    act.wait_ge(chain[lane].sem, S.after(lane, i, "edge_t"))
                                    act.wait_ge(stored[lane].sem, S.dma("stored", lane, i, rounds=0))
                                    act.activation(in_order(edge_in[lane][D:P, :]), by_tile(A)[D:P], ACT.Copy).then_inc(chain[lane].sem, 1)
                                else:
                                    act.wait_ge(chain[lane].sem, S.after(lane, i, "edge_mm"))
                                    act.activation(edge_in[lane][D:P, :], A[D:P, :], ACT.Relu, bias=w["edge_b"][D:P, :]).then_inc(chain[lane].sem, 1)
                            for i, lane in at("edge_pair"):
                                act.wait_ge(chain[lane].sem, S.after(lane, i, "edge_act" if l else "edge_feat"))
                                act.activation(edge_in[lane][0:D, :], feat[lane][0:D, :], ACT.Copy).then_inc(chain[lane].sem, 1)
                            for i, lane in at("msg_mm"):
                                b = i * EL + lane
                                if l < 2:
                                    act.dma_start(edge_state[ds(b, 1), :, :].rearrange("o f e -> (o f) e"), edge_in[lane][D:P, :]).then_inc(stored[lane].sem, 16)
                            for i, lane in at("msg_act"):
                                A = edge_psum(lane)
                                act.wait_ge(chain[lane].sem, S.after(lane, i, "msg_mm"))
                                act.activation(messages[lane][0:D, :], A[0:D, :], ACT.Relu, bias=w["msg_b"][0:D, :]).then_inc(chain[lane].sem, 1)
                        if kind in ("sage", "gnn", "proj"):
                            for i, lane in at("act"):
                                A = edge_psum(lane)
                                act.wait_ge(chain[lane].sem, S.after(lane, i, "mm"))
                                act.activation(feat_out[lane][:, :], A, relu, bias=w["bias"][:, :]).then_inc(chain[lane].sem, 1)
                            if kind == "gnn":
                                for i, lane in at("l2_square"):
                                    A = edge_psum(lane)
                                    act.wait_ge(chain[lane].sem, S.after(lane, i, "t_out"))
                                    act.activation(squares[lane][:, :], A, ACT.Square).then_inc(chain[lane].sem, 1)
                                for i, lane in at("l2_root"):
                                    act.wait_ge(chain[lane].sem, S.after(lane, i, "l2_sum"))
                                    act.activation(stats[lane][:, 16:32], stats[lane][:, 0:16], ACT.Sqrt).then_inc(chain[lane].sem, 1)
                            for i, lane in at("end"):
                                b = i * EL + lane
                                act.wait_ge(chain[lane].sem, S.after(lane, i, last))
                                act.dma_start(rows(tout, b), rows_out[lane][:, :].rearrange("p (j d) -> p j d", j=J)).then_inc(stored[lane].sem, 16)
                        if kind == "gin":
                            for i, lane in at("z"):
                                b = i * EL + lane
                                act.wait_ge(chain[lane].sem, S.after(lane, i, "scan"))
                                act.dma_start(gin_x[ds(b, 1), :, :].rearrange("o f e -> (o f) e"), feat[lane][:, :]).then_inc(stored[lane].sem, 16)
                                act.dma_start(gin_agg[ds(b, 1), :, :].rearrange("o f e -> (o f) e"), agg[lane][0:D, 0:BLK]).then_inc(stored[lane].sem, 16)
                        if kind == "qkv":
                            for i, lane in at("end"):
                                b = i * EL + lane
                                act.wait_ge(chain[lane].sem, S.after(lane, i, last))
                                act.dma_start(rows(records, b), record_rows[lane][:, 0:J * REC].rearrange("p (j d) -> p j d", j=J)).then_inc(stored[lane].sem, 16)
                    S.run(act, body)
                    for lane in range(EL):
                        n = S.rounds + (lane < S.rest)
                        act.wait_ge(stored[lane].sem, S.at["stored"][lane] + n * S.per["stored"])
                        if save_resid:
                            act.wait_ge(resid_saved[lane].sem, saved0[lane] + 16 * n)

                @block.vector
                def _(dve):
                    def body(at):
                        if ln:
                            def ready(i, lane):
                                dve.wait_ge(chain[lane].sem, S.start(lane, i))
                                rows_ready(dve, lane, i)

                            ln_vector(dve, S, at, ready, rows_in, centered, squares, 2 * J)
                        if scans:
                            for i, lane in at("scan"):
                                msg = messages[lane][0:D, :] if kind == "gnn" else feat[lane][0:D, :]
                                dve.wait_ge(chain[lane].sem, S.after(lane, i, "msg_act" if kind == "gnn" else "feat"))
                                dve.wait_ge(more_loaded[lane].sem, S.dma("more", lane, i))
                                if kind == "gin":
                                    dve.wait_ge(stored[lane].sem, S.dma("stored", lane, i, rounds=0))
                                if lane == 0:
                                    dve.wait_ge(chain[EL - 1].sem, S.after(EL - 1, i - 1, "scan"))
                                else:
                                    dve.wait_ge(chain[lane - 1].sem, S.after(lane - 1, i, "scan"))
                                before = agg[(lane - 1) % EL]
                                dve.tensor_tensor_scan(agg[lane][0:D, 0:BLK], flags[lane][0:D, :], msg, before[0:D, BLK - 1:BLK],
                                                       ALU.mult, ALU.add).then_inc(chain[lane].sem, 1)
                        if kind in ("sage", "gnn"):
                            for i, lane in at("mean"):
                                dve.wait_ge(chain[lane].sem, S.after(lane, i, "scan"))
                                dve.tensor_tensor(mean_agg[lane][0:D, 0:BLK], agg[lane][0:D, 0:BLK], inverse[lane][0:D, :], ALU.mult).then_inc(chain[lane].sem, 1)
                        if kind in ("sage", "proj"):
                            for i, lane in at("rows"):
                                A = edge_psum(lane)
                                dve.wait_ge(chain[lane].sem, S.after(lane, i, "t_out"))
                                dve.wait_ge(stored[lane].sem, S.dma("stored", lane, i, rounds=0))
                                if add_resid:
                                    dve.wait_ge(more_loaded[lane].sem, S.dma("more", lane, i))
                                    dve.tensor_tensor(rows_out[lane][:, :], A, resid[lane][:, :], ALU.add).then_inc(chain[lane].sem, 1)
                                else:
                                    dve.tensor_copy(rows_out[lane][:, :], A).then_inc(chain[lane].sem, 1)
                        if kind == "gnn":
                            for i, lane in at("l2_sum"):
                                A = edge_psum(lane)
                                st = stats[lane]
                                dve.wait_ge(chain[lane].sem, S.after(lane, i, "l2_square"))
                                dve.tensor_reduce(st[:, 0:16], squares[lane][:, :].rearrange("p (t d) -> p t d", d=D), AX, ALU.add).then_inc(chain[lane].sem, 1)
                            for i, lane in at("l2_floor"):
                                dve.wait_ge(chain[lane].sem, S.after(lane, i, "l2_root"))
                                dve.tensor_scalar(stats[lane][:, 32:48], stats[lane][:, 16:32], L2_EPS, None, ALU.max).then_inc(chain[lane].sem, 1)
                            for i, lane in at("l2_inverse"):
                                dve.wait_ge(chain[lane].sem, S.after(lane, i, "l2_floor"))
                                dve.reciprocal(stats[lane][:, 48:64], stats[lane][:, 32:48]).then_inc(chain[lane].sem, 1)
                            for i, lane in at("rows"):
                                A = edge_psum(lane)
                                dve.wait_ge(chain[lane].sem, S.after(lane, i, "l2_inverse"))
                                dve.wait_ge(stored[lane].sem, S.dma("stored", lane, i, rounds=0) + 16 * (l < 2))
                                dve.tensor_tensor(rows_out[lane][:, :].rearrange("p (t d) -> p t d", d=D), A.rearrange("p (t d) -> p t d", d=D),
                                                  stats[lane][:, 48:64].unsqueeze(2).broadcast_to([P, 2 * J, D]), ALU.mult).then_inc(chain[lane].sem, 1)
                            if add_resid:
                                for i, lane in at("add_resid"):
                                    dve.wait_ge(chain[lane].sem, S.after(lane, i, "rows"))
                                    dve.tensor_tensor(rows_out[lane][:, :], rows_out[lane][:, :], resid[lane][:, :], ALU.add).then_inc(chain[lane].sem, 1)
                        if kind == "gin":
                            for i, lane in at("z_rows"):
                                dve.wait_ge(chain[lane].sem, S.after(lane, i, "z"))
                                dve.tensor_copy(squares[lane][:, 0:W], edge_psum(lane)[:, 0:W]).then_inc(chain[lane].sem, 1)
                            for i, lane in at("z_masked"):
                                zm = masked[lane][:, :].rearrange("p (j d) -> p j d", j=J)
                                mask = rep_mask[:, ds((i * EL + lane) * J, J)]
                                dve.wait_ge(chain[lane].sem, S.after(lane, i, "z_rows"))
                                dve.tensor_tensor(zm[:, :, 0:D], squares[lane][:, 0:W].rearrange("p (j d) -> p j d", j=J),
                                                  mask.unsqueeze(2).broadcast_to([P, J, D]), ALU.mult).then_inc(chain[lane].sem, 1)
                                dve.tensor_copy(zm[:, :, D], mask).then_inc(chain[lane].sem, 1)
                        if kind == "qkv":
                            def as_rows(v):
                                return v.rearrange("p (j d) -> p j d", j=J)

                            def bias_of(n):
                                return b_qkv[:, n, :].unsqueeze(1).broadcast_to([P, J, D])

                            def record(lane):
                                return record_rows[lane][:, 0:J * REC].rearrange("p (j d) -> p j d", j=J)

                            for i, lane in at("q_bias"):
                                A = edge_psum(lane)
                                q, k = squares[lane][:, 0:W], squares[lane][:, W:2 * W]
                                dve.wait_ge(chain[lane].sem, S.after(lane, i, "qk_mm"))
                                dve.tensor_tensor(as_rows(q), as_rows(A[:, 0:W]), bias_of(0), ALU.add).then_inc(chain[lane].sem, 1)
                                dve.tensor_tensor(as_rows(k), as_rows(A[:, W:2 * W]), bias_of(1), ALU.add).then_inc(chain[lane].sem, 1)
                            for i, lane in at("v_bias"):
                                dve.wait_ge(chain[lane].sem, S.after(lane, i, "v_mm"))
                                dve.wait_ge(stored[lane].sem, S.dma("stored", lane, i, rounds=0))
                                dve.tensor_tensor(record(lane)[:, :, 0:D], as_rows(edge_psum(lane)[:, 0:W]), bias_of(2), ALU.add).then_inc(chain[lane].sem, 1)
                            for i, lane in at("q_times_k"):
                                dve.wait_ge(chain[lane].sem, S.after(lane, i, "v_bias"))
                                dve.tensor_tensor(centered[lane][:, 0:W], squares[lane][:, 0:W], squares[lane][:, W:2 * W], ALU.mult).then_inc(chain[lane].sem, 1)
                            for i, lane in at("dot"):
                                dve.wait_ge(chain[lane].sem, S.after(lane, i, "q_times_k"))
                                dve.tensor_reduce(stats[lane][:, 0:J * HEADS], centered[lane][:, 0:W].rearrange("p (t d) -> p t d", d=HD), AX, ALU.add).then_inc(chain[lane].sem, 1)
                            for i, lane in at("score"):
                                dve.wait_ge(chain[lane].sem, S.after(lane, i, "dot"))
                                dve.tensor_scalar(record(lane)[:, :, D:D + HEADS], stats[lane][:, 0:J * HEADS].rearrange("p (j h) -> p j h", h=HEADS),
                                                  1.0 / float(np.sqrt(HD)), None, ALU.mult).then_inc(chain[lane].sem, 1)
                            for i, lane in at("max_score"):
                                dve.wait_ge(chain[lane].sem, S.after(lane, i, "score"))
                                dve.tensor_reduce(record(lane)[:, :, D + HEADS], record(lane)[:, :, D:D + HEADS], AX, ALU.max).then_inc(chain[lane].sem, 1)
                    S.run(dve, body)
            S.close()
            for lane in range(EL):
                n = S.rounds + (lane < S.rest)
                if source != "rows":
                    gather_ready[lane].base += n * (1 if source == "links" and not homes else 2)
                if save_resid:
                    resid_saved[lane].base += 16 * n

        def gin_edge_phase(l, tout, add_resid):
            w = gin[l]
            S = Steps(["s_mm", "s_act", "d_mm", "d_act", "y_mm", "y_act", "t_out", "rows"], EL, EB,
                      loads=2 + add_resid, stores=1)
            with nc.Block() as block:
                @block.sync
                def _(sp):
                    def body(i, lanes):
                        for lane in lanes:
                            b = i * EL + lane
                            hold(sp, chain[lane].sem, S.start(lane, i))
                            sp.dma_start(rows_in[lane][:, :], gin_x[ds(b, 1), :, :].rearrange("o f e -> (o f) e")).then_inc(loaded[lane].sem, 16)
                            sp.dma_start(flags[lane][0:D, :], gin_agg[ds(b, 1), :, :].rearrange("o f e -> (o f) e")).then_inc(loaded[lane].sem, 16)
                            if add_resid:
                                sp.dma_start(resid[lane][:, :].rearrange("p (j d) -> p j d", j=J), rows(sd_resid, b)).then_inc(loaded[lane].sem, 16)
                    S.run_in_order(sp, body)

                @block.tensor
                def _(pe):
                    def body(at):
                        for i, lane in at("s_mm"):
                            A = edge_psum(lane)
                            pe.wait_ge(chain[lane].sem, S.start(lane, i))
                            pe.wait_ge(loaded[lane].sem, S.dma("loaded", lane, i))
                            for h in range(2):
                                c = slice(h * 512, (h + 1) * 512)
                                op = pe.matmul(A[:, c], w["w1_own"][0:D, :], rows_in[lane][0:D, c], start=True, stop=True)
                            op.then_inc(chain[lane].sem, 1)
                        for i, lane in at("d_mm"):
                            A = edge_psum(lane)
                            pe.wait_ge(chain[lane].sem, S.after(lane, i, "s_act"))
                            for h in range(2):
                                c = slice(h * 512, (h + 1) * 512)
                                pe.matmul(A[:, c], w["w1_dst"][:, :], rows_in[lane][:, c], start=True, stop=False)
                                op = pe.matmul(A[:, c], w["w1"][0:D, :], flags[lane][0:D, c], start=False, stop=True)
                            op.then_inc(chain[lane].sem, 1)
                        for i, lane in at("y_mm"):
                            A = edge_psum(lane)
                            pe.wait_ge(chain[lane].sem, S.after(lane, i, "d_act"))
                            for h in range(2):
                                c = slice(h * 512, (h + 1) * 512)
                                pe.matmul(A[:, c], w["w2_src"][:, :], centered[lane][:, c], start=True, stop=False)
                                op = pe.matmul(A[:, c], w["w2_dst"][:, :], squares[lane][:, c], start=False, stop=True)
                            op.then_inc(chain[lane].sem, 1)
                        for i, lane in at("t_out"):
                            A = edge_psum(lane)
                            pe.wait_ge(chain[lane].sem, S.after(lane, i, "y_act"))
                            for j in range(J):
                                op = pe.transpose(A[:, j * P:(j + 1) * P], tiles_of(feat_out[lane][:, :], j), ident[:, :])
                            op.then_inc(chain[lane].sem, 1)
                    S.run(pe, body)

                @block.scalar
                def _(act):
                    def body(at):
                        for mm, dest in (("s_mm", centered), ("d_mm", squares)):
                            for i, lane in at(mm.replace("mm", "act")):
                                A = edge_psum(lane)
                                act.wait_ge(chain[lane].sem, S.after(lane, i, mm))
                                act.activation(dest[lane][:, :], A, ACT.Relu, bias=w["shift"][:, :], scale=w["scale"][:, :]).then_inc(chain[lane].sem, 1)
                        for i, lane in at("y_act"):
                            A = edge_psum(lane)
                            act.wait_ge(chain[lane].sem, S.after(lane, i, "y_mm"))
                            act.activation(feat_out[lane][:, :], A, ACT.Identity, bias=w["b2"][:, :]).then_inc(chain[lane].sem, 1)
                        for i, lane in at("end"):
                            b = i * EL + lane
                            act.wait_ge(chain[lane].sem, S.after(lane, i, "rows"))
                            act.dma_start(rows(tout, b), rows_out[lane][:, :].rearrange("p (j d) -> p j d", j=J)).then_inc(stored[lane].sem, 16)
                    S.run(act, body)
                    for lane in range(EL):
                        act.wait_ge(stored[lane].sem, S.at["stored"][lane] + (S.rounds + (lane < S.rest)) * 16)

                @block.vector
                def _(dve):
                    def body(at):
                        for i, lane in at("rows"):
                            A = edge_psum(lane)
                            dve.wait_ge(chain[lane].sem, S.after(lane, i, "t_out"))
                            dve.wait_ge(stored[lane].sem, S.dma("stored", lane, i, rounds=0))
                            if add_resid:
                                dve.tensor_tensor(rows_out[lane][:, :], A, resid[lane][:, :], ALU.add).then_inc(chain[lane].sem, 1)
                            else:
                                dve.tensor_copy(rows_out[lane][:, :], A).then_inc(chain[lane].sem, 1)
                    S.run(dve, body)
            S.close()

        def attention_phase():
            R72 = D + HEADS
            S = Steps(["t_in", "feat", "max_mm", "carry", "run_max", "score_mm", "unit", "below_max", "max_step",
                       "max_step_neg", "weight", "rescale", "weighted", "sums", "t_out", "guard", "inverse", "rows"],
                      EL, EB, loads=0, more=1, stores=0, gathers=J)
            n0, done0, ready0 = ([c.base for c in cs] for cs in (scattered, scatter_done, scatter_ready))
            stage0 = [g.base for g in gather_ready]
            with nc.Block() as block:
                @block.sync
                def _(sp):
                    def body(i, lanes):
                        for lane in lanes:
                            b = i * EL + lane
                            hold(sp, chain[lane].sem, S.start(lane, i))
                            sp.dma_start(flags[lane][0:R72, :], neg_start[ds(b * BLK, BLK)].partition_broadcast(R72)).then_inc(more_loaded[lane].sem, 16)
                    S.run_in_order(sp, body)

                @block.gpsimd
                def _(pool):
                    def gather(i, lanes):
                        for lane in lanes:
                            b = i * EL + lane
                            hold(pool, chain[lane].sem, S.after(lane, i - 1, "t_in"))
                            pool.tensor_copy(idx_stage[lane][:, 0:J], sorted_edge[:, ds(b * J, J)]).then_inc(gather_ready[lane].sem, 1)
                            hold(pool, gather_ready[lane].sem, i + (stage0[lane] + 1))
                            for j in range(J):
                                pool.indirect_dma_start(rows_in[lane][:, j * REC:(j + 1) * REC], None, records[:, :],
                                                        bass.IndirectOffsetOnAxis(idx_stage[lane][:, j:j + 1], 0),
                                                        bounds_check=EP - 1, oob_is_err=False).then_inc(gathered[lane].sem, 16)

                    def scatter(i, lanes):
                        for lane in lanes:
                            b = i * EL + lane
                            pool.tensor_copy(idx_stage[lane][:, J:2 * J], attn_out_idx[:, ds(b * J, J)]).then_inc(scatter_ready[lane].sem, 1)
                            hold(pool, scatter_ready[lane].sem, i + (ready0[lane] + 1))
                            hold(pool, chain[lane].sem, S.after(lane, i, "rows"))
                            for j in range(J):
                                pool.indirect_dma_start(attn_nodes[:, :], bass.IndirectOffsetOnAxis(idx_stage[lane][:, J + j:J + j + 1], 0),
                                                        rows_out[lane][:, j * D:(j + 1) * D], None,
                                                        bounds_check=N - 1, oob_is_err=False).then_inc(scattered[lane].sem, 16)
                        for lane in lanes:
                            hold(pool, scattered[lane].sem, i * (16 * J) + (n0[lane] + 16 * J))
                            pool.sem_inc(scatter_done[lane].sem, 1)

                    pool.wait_ge(attn_zeroed.sem, 16 * NB)
                    gather(0, range(min(EL, EB)))
                    if S.rounds > 1:
                        with pool.Fori(1, S.rounds) as i:
                            gather(i, range(EL))
                            scatter(i - 1, range(EL))
                    if S.rounds and S.rest:
                        gather(S.rounds, range(S.rest))
                    if S.rounds:
                        scatter(S.rounds - 1, range(EL))
                    if S.rest:
                        scatter(S.rounds, range(S.rest))

                @block.tensor
                def _(pe):
                    def body(at):
                        for i, lane in at("t_in"):
                            A = edge_psum(lane)
                            pe.wait_ge(chain[lane].sem, S.start(lane, i))
                            pe.wait_ge(gathered[lane].sem, S.dma("gathered", lane, i))
                            for j in range(J):
                                op = pe.transpose(A[0:REC, j * P:(j + 1) * P], rows_in[lane][:, j * REC:(j + 1) * REC], ident[:, :])
                            op.then_inc(chain[lane].sem, 1)
                        for step, before, pick in (("max_mm", "feat", pick_max), ("score_mm", "run_max", pick_score)):
                            for i, lane in at(step):
                                A = edge_psum(lane)
                                pe.wait_ge(chain[lane].sem, S.after(lane, i, before))
                                for h in range(2):
                                    c = slice(h * 512, (h + 1) * 512)
                                    op = pe.matmul(A[0:R72, c], pick[0:REC, :], feat[lane][0:REC, c], start=True, stop=True)
                                op.then_inc(chain[lane].sem, 1)
                        for i, lane in at("t_out"):
                            A = edge_psum(lane)
                            pe.wait_ge(chain[lane].sem, S.after(lane, i, "sums"))
                            for j in range(J):
                                op = pe.transpose(A[:, j * P:j * P + R72], tiles_of(feat_out[lane][0:R72, :], j), ident[0:R72, 0:R72])
                            op.then_inc(chain[lane].sem, 1)
                    S.run(pe, body)

                @block.scalar
                def _(act):
                    def body(at):
                        for i, lane in at("feat"):
                            A = edge_psum(lane)
                            act.wait_ge(chain[lane].sem, S.after(lane, i, "t_in"))
                            act.activation(in_order(feat[lane][0:REC, :]), by_tile(A)[0:REC], ACT.Copy).then_inc(chain[lane].sem, 1)
                        for i, lane in at("weight"):
                            act.wait_ge(chain[lane].sem, S.after(lane, i, "max_step_neg"))
                            act.activation(centered[lane][0:R72, :], centered[lane][0:R72, :], ACT.Exp).then_inc(chain[lane].sem, 1)
                            act.activation(squares[lane][0:R72, :], squares[lane][0:R72, :], ACT.Exp).then_inc(chain[lane].sem, 1)
                    S.run(act, body)

                @block.vector
                def _(dve):
                    def body(at):
                        def other_lane(i, lane):
                            return (EL - 1, i - 1) if lane == 0 else (lane - 1, i)

                        for i, lane in at("carry"):
                            other, round_of = other_lane(i, lane)
                            dve.wait_ge(chain[lane].sem, S.after(lane, i, "max_mm"))
                            dve.wait_ge(chain[other].sem, S.after(other, round_of, "run_max"))
                            dve.tensor_copy(running_max[lane][0:R72, 0:1], running_max[other][0:R72, BLK:BLK + 1]).then_inc(chain[lane].sem, 1)
                        for i, lane in at("run_max"):
                            m = running_max[lane]
                            dve.wait_ge(chain[lane].sem, S.after(lane, i, "carry"))
                            dve.wait_ge(more_loaded[lane].sem, S.dma("more", lane, i))
                            dve.tensor_tensor_scan(m[0:R72, 1:BLK + 1], flags[lane][0:R72, :], edge_psum(lane)[0:R72, :], m[0:R72, 0:1],
                                                   ALU.add, ALU.max).then_inc(chain[lane].sem, 1)
                        for i, lane in at("unit"):
                            m = running_max[lane]
                            dve.wait_ge(chain[lane].sem, S.after(lane, i, "score_mm"))
                            dve.memset(feat[lane][D:R72, :], 1.0).then_inc(chain[lane].sem, 1)
                            dve.tensor_tensor(centered[lane][0:R72, :], edge_psum(lane)[0:R72, :], m[0:R72, 1:BLK + 1], ALU.subtract).then_inc(chain[lane].sem, 1)
                            dve.tensor_tensor(squares[lane][0:R72, :], m[0:R72, 0:BLK], m[0:R72, 1:BLK + 1], ALU.subtract).then_inc(chain[lane].sem, 1)
                        for i, lane in at("max_step_neg"):
                            r = squares[lane][0:R72, :]
                            dve.wait_ge(chain[lane].sem, S.after(lane, i, "max_step"))
                            dve.tensor_tensor(r, r, flags[lane][0:R72, :], ALU.add).then_inc(chain[lane].sem, 1)
                        for i, lane in at("weighted"):
                            d = centered[lane][0:R72, :]
                            dve.wait_ge(chain[lane].sem, S.after(lane, i, "rescale"))
                            dve.tensor_tensor(d, d, feat[lane][0:R72, :], ALU.mult).then_inc(chain[lane].sem, 1)
                        for i, lane in at("sums"):
                            other, round_of = other_lane(i, lane)
                            dve.wait_ge(chain[lane].sem, S.after(lane, i, "weighted"))
                            dve.wait_ge(chain[other].sem, S.after(other, round_of, "sums"))
                            dve.tensor_tensor_scan(feat_out[lane][0:R72, :], squares[lane][0:R72, :], centered[lane][0:R72, :],
                                                   feat_out[other][0:R72, BLK - 1:BLK], ALU.mult, ALU.add).then_inc(chain[lane].sem, 1)
                        for i, lane in at("guard"):
                            a = edge_psum(lane).rearrange("p (j f) -> p j f", j=J)
                            dve.wait_ge(chain[lane].sem, S.after(lane, i, "t_out"))
                            dve.tensor_scalar(stats[lane][:, 0:J * HEADS].rearrange("p (j h) -> p j h", h=HEADS), a[:, :, D:R72],
                                              SM_EPS, None, ALU.add).then_inc(chain[lane].sem, 1)
                        for i, lane in at("inverse"):
                            dve.wait_ge(chain[lane].sem, S.after(lane, i, "guard"))
                            dve.reciprocal(masked[lane][:, 0:J * HEADS], stats[lane][:, 0:J * HEADS]).then_inc(chain[lane].sem, 1)
                        for i, lane in at("rows"):
                            a = edge_psum(lane).rearrange("p (j f) -> p j f", j=J)
                            inv = masked[lane][:, 0:J * HEADS]
                            dve.wait_ge(chain[lane].sem, S.after(lane, i, "inverse"))
                            dve.wait_ge(scatter_done[lane].sem, i + done0[lane])
                            dve.tensor_tensor(rows_out[lane][:, 0:J * D].rearrange("p (j h d) -> p j h d", h=HEADS, d=HD),
                                              a[:, :, 0:D].rearrange("p j (h d) -> p j h d", d=HD),
                                              inv.rearrange("p (j h) -> p j h", h=HEADS).unsqueeze(3).broadcast_to([P, J, HEADS, HD]),
                                              ALU.mult).then_inc(chain[lane].sem, 1)
                    S.run(dve, body)
            S.close()
            for lane in range(EL):
                n = S.rounds + (lane < S.rest)
                gather_ready[lane].base += n
                scatter_ready[lane].base += n
                scattered[lane].base += 16 * J * n
                scatter_done[lane].base += n

        def scatter_phase(tin):
            S = Steps(["none"], EL, EB, loads=1, stores=0, gathers=J)
            stage0 = [g.base for g in gather_ready]
            with nc.Block() as block:
                @block.sync
                def _(sp):
                    def body(i, lanes):
                        for lane in lanes:
                            hold(sp, gathered[lane].sem, S.dma("gathered", lane, i, rounds=0))
                            sp.dma_start(rows_in[lane][:, :].rearrange("p (j d) -> p j d", j=J), rows(tin, i * EL + lane)).then_inc(loaded[lane].sem, 16)
                    S.run_in_order(sp, body)

                @block.gpsimd
                def _(pool):
                    def body(i, lanes):
                        for lane in lanes:
                            b = i * EL + lane
                            hold(pool, gathered[lane].sem, S.dma("gathered", lane, i, rounds=0))
                            pool.tensor_copy(idx_stage[lane][:, 0:J], last_dst_idx[:, ds(b * J, J)]).then_inc(gather_ready[lane].sem, 1)
                            hold(pool, gather_ready[lane].sem, i + (stage0[lane] + 1))
                            hold(pool, loaded[lane].sem, S.dma("loaded", lane, i))
                            for j in range(J):
                                pool.indirect_dma_start(out[:, :], bass.IndirectOffsetOnAxis(idx_stage[lane][:, j:j + 1], 0),
                                                        rows_in[lane][:, j * P + D:(j + 1) * P], None,
                                                        bounds_check=N - 1, oob_is_err=False).then_inc(gathered[lane].sem, 16)
                    S.run_in_order(pool, body)
                    for lane in range(EL):
                        pool.wait_ge(gathered[lane].sem, S.at["gathered"][lane] + (S.rounds + (lane < S.rest)) * 16 * J)

        def node_rows(table, i, lane):
            if isinstance(i, int) and i * DL + lane == NB - 1:
                return table[N - BLK:N, :].rearrange("(p j) d -> p j d", j=J)
            return rows(table, i * DL + lane)

        def as3(tile):
            return tile.rearrange("p (j d) -> p j d", j=J)

        def node_store(act, S, i, lane, table, tile, sem):
            first = OVER if isinstance(i, int) and i * DL + lane == NB - 1 else 0
            act.dma_start(node_rows(table, i, lane)[first:P, :, :], as3(tile)[first:P, :, :]).then_inc(sem, 16)

        def node_sums_vector(dve, S, lane, i, h):
            hm = as3(masked[lane][:, :])
            mask = node_mask[:, ds((i * DL + lane) * J, J)] if not isinstance(i, int) else \
                node_mask[:, (i * DL + lane) * J:(i * DL + lane + 1) * J]
            dve.tensor_tensor(hm[:, :, 0:D], as3(h), mask.unsqueeze(2).broadcast_to([P, J, D]), ALU.mult).then_inc(chain[lane].sem, 1)
            dve.tensor_copy(hm[:, :, D], mask).then_inc(chain[lane].sem, 1)

        def node_sums_tensor(pe, S, lane, i, h):
            hm = as3(masked[lane][:, :])
            for j in range(J):
                op = pe.matmul(gram_nodes[0:D, 0:D + 1], h[:, j * D:(j + 1) * D], hm[:, j, :],
                               start=False, stop=False, skip_group_check=True)
            op.then_inc(chain[lane].sem, 1)

        def transpose4(pe, bank, src):
            for q in range(4):
                op = pe.transpose(bank[:, q * P:(q + 1) * P], src[:, q * P:(q + 1) * P], ident[:, :])
            return op

        def node_sage_phase():
            names = LN + ["t_in", "feat"] + [s + str(k) for k in range(3) for s in ("mm", "act")] + ["t_out", "x1"] \
                + ["again_" + s for s in LN] + ["masked", "mask", "gram"]
            S = Steps(names, DL, NB, loads=1, stores=2)
            with nc.Block() as block:
                @block.sync
                def _(sp):
                    def body(i, lanes):
                        for lane in lanes:
                            hold(sp, chain[lane].sem, S.after(lane, i - 1, "x1"))
                            sp.dma_start(as3(n_rows_in[lane][:, 0:W]), node_rows(t["x"], i, lane)).then_inc(loaded[lane].sem, 16)
                    S.run_in_order(sp, body)

                @block.tensor
                def _(pe):
                    pe.matmul(gram_nodes[0:D, 0:D + 1], zeros[:, 0:D], zeros[:, 0:D + 1], start=True, stop=True)

                    def body(at):
                        for i, lane in at("t_in"):
                            A = node_psum(lane)
                            pe.wait_ge(chain[lane].sem, S.after(lane, i, "ln_out"))
                            transpose4(pe, A, n_centered[lane]).then_inc(chain[lane].sem, 1)
                        for k in range(3):
                            for i, lane in at(f"mm{k}"):
                                A = node_psum(lane)
                                pe.wait_ge(chain[lane].sem, S.after(lane, i, f"act{k - 1}" if k else "feat"))
                                pe.matmul(A, sage[k]["own"][:, :], n_feat[lane][:, 0:W], start=True, stop=True).then_inc(chain[lane].sem, 1)
                        for i, lane in at("t_out"):
                            A = node_psum(lane)
                            pe.wait_ge(chain[lane].sem, S.after(lane, i, "act2"))
                            transpose4(pe, A, n_feat[lane]).then_inc(chain[lane].sem, 1)
                        for i, lane in at("gram"):
                            pe.wait_ge(chain[lane].sem, S.after(lane, i, "mask"))
                            node_sums_tensor(pe, S, lane, i, n_centered[lane][:, 0:W])
                    S.run(pe, body)

                @block.scalar
                def _(act):
                    def body(at):
                        ln_scalar(act, S, at, n_centered, n_squares, J)
                        for i, lane in at("feat"):
                            A = node_psum(lane)
                            act.wait_ge(chain[lane].sem, S.after(lane, i, "t_in"))
                            act.activation(n_feat[lane][:, 0:W], A, ACT.Copy).then_inc(chain[lane].sem, 1)
                        for k in range(3):
                            for i, lane in at(f"act{k}"):
                                A = node_psum(lane)
                                act.wait_ge(chain[lane].sem, S.after(lane, i, f"mm{k}"))
                                act.activation(n_feat[lane][:, 0:W], A, ACT.Relu, bias=sage[k]["bias"][:, :]).then_inc(chain[lane].sem, 1)
                        for i, lane in at("again_ln_sum"):
                            act.wait_ge(chain[lane].sem, S.after(lane, i, "x1"))
                            node_store(act, S, i, lane, x1_nodes, n_rows_out[lane][:, 0:W], stored[lane].sem)
                        ln_scalar(act, S, at, n_centered, n_squares, J, "again_")
                        for i, lane in at("masked"):
                            act.wait_ge(chain[lane].sem, S.after(lane, i, "again_ln_out"))
                            node_store(act, S, i, lane, h_nodes[0], n_centered[lane][:, 0:W], stored[lane].sem)
                    S.run(act, body)
                    for lane in range(DL):
                        act.wait_ge(stored[lane].sem, S.at["stored"][lane] + (S.rounds + (lane < S.rest)) * 32)

                @block.vector
                def _(dve):
                    def body(at):
                        def ready(i, lane):
                            dve.wait_ge(chain[lane].sem, S.start(lane, i))
                            dve.wait_ge(stored[lane].sem, S.dma("stored", lane, i, rounds=0))
                            dve.wait_ge(loaded[lane].sem, S.dma("loaded", lane, i))

                        ln_vector(dve, S, at, ready, n_rows_in, n_centered, n_squares, J)
                        for i, lane in at("x1"):
                            A = node_psum(lane)
                            dve.wait_ge(chain[lane].sem, S.after(lane, i, "t_out"))
                            dve.tensor_tensor(n_rows_out[lane][:, 0:W], A, n_rows_in[lane][:, 0:W], ALU.add).then_inc(chain[lane].sem, 1)
                        def ready(i, lane):
                            dve.wait_ge(chain[lane].sem, S.after(lane, i, "x1"))

                        ln_vector(dve, S, at, ready, n_rows_out, n_centered, n_squares, J, "again_")
                        for i, lane in at("masked"):
                            dve.wait_ge(chain[lane].sem, S.after(lane, i, "again_ln_out"))
                            node_sums_vector(dve, S, lane, i, n_centered[lane][:, 0:W])
                    S.run(dve, body)
            S.close()

        def node_gin_phase(l):
            w = gin[l]
            final = l == 2
            tin, tout = h_nodes[l % 2], x2_nodes if final else h_nodes[(l + 1) % 2]
            names = ["t_in", "feat", "w1_even", "norm_even", "w1_odd", "norm_odd", "w2", "y", "t_out", "rows"] + ([] if final else ["masked", "mask", "gram"])
            S = Steps(names, DL, NB, loads=1, more=int(final), stores=1)
            with nc.Block() as block:
                @block.sync
                def _(sp):
                    def body(i, lanes):
                        for lane in lanes:
                            hold(sp, chain[lane].sem, S.after(lane, i - 1, "t_in"))
                            sp.dma_start(as3(n_rows_in[lane][:, 0:W]), node_rows(tin, i, lane)).then_inc(loaded[lane].sem, 16)
                        for lane in lanes:
                            if final:
                                hold(sp, chain[lane].sem, S.start(lane, i))
                                sp.dma_start(as3(n_resid[lane][:, 0:W]), node_rows(x1_nodes, i, lane)).then_inc(more_loaded[lane].sem, 16)
                    S.run_in_order(sp, body)

                @block.tensor
                def _(pe):
                    if not final:
                        pe.matmul(gram_nodes[0:D, 0:D + 1], zeros[:, 0:D], zeros[:, 0:D + 1], start=True, stop=True)

                    def body(at):
                        for i, lane in at("t_in"):
                            A = node_psum(lane)
                            pe.wait_ge(chain[lane].sem, S.start(lane, i))
                            pe.wait_ge(loaded[lane].sem, S.dma("loaded", lane, i))
                            transpose4(pe, A, n_rows_in[lane]).then_inc(chain[lane].sem, 1)
                        for i, lane in at("w1_even"):
                            A = node_psum(lane)
                            pe.wait_ge(chain[lane].sem, S.after(lane, i, "feat"))
                            pe.matmul(A, w["w1_own"][0:D, :], n_feat[lane][0:D, 0:W], start=True, stop=True).then_inc(chain[lane].sem, 1)
                        for i, lane in at("w1_odd"):
                            A = node_psum(lane)
                            pe.wait_ge(chain[lane].sem, S.after(lane, i, "norm_even"))
                            pe.matmul(A, w["w1_own"][D:P, :], n_feat[lane][D:P, 0:W], start=True, stop=True).then_inc(chain[lane].sem, 1)
                        for i, lane in at("w2"):
                            A = node_psum(lane)
                            pe.wait_ge(chain[lane].sem, S.after(lane, i, "norm_odd"))
                            pe.matmul(A, w["w2_src"][:, :], n_centered[lane][:, 0:W], start=True, stop=False)
                            pe.matmul(A, w["w2_dst"][:, :], n_squares[lane][:, 0:W], start=False, stop=True).then_inc(chain[lane].sem, 1)
                        for i, lane in at("t_out"):
                            A = node_psum(lane)
                            pe.wait_ge(chain[lane].sem, S.after(lane, i, "y"))
                            transpose4(pe, A, n_feat_out[lane]).then_inc(chain[lane].sem, 1)
                        if not final:
                            for i, lane in at("gram"):
                                pe.wait_ge(chain[lane].sem, S.after(lane, i, "mask"))
                                node_sums_tensor(pe, S, lane, i, n_rows_out[lane][:, 0:W])
                    S.run(pe, body)

                @block.scalar
                def _(act):
                    def body(at):
                        for i, lane in at("feat"):
                            A = node_psum(lane)
                            act.wait_ge(chain[lane].sem, S.after(lane, i, "t_in"))
                            act.activation(n_feat[lane][:, 0:W], A, ACT.Copy).then_inc(chain[lane].sem, 1)
                        for part, dest in (("even", n_centered), ("odd", n_squares)):
                            for i, lane in at("norm_" + part):
                                A = node_psum(lane)
                                act.wait_ge(chain[lane].sem, S.after(lane, i, "w1_" + part))
                                act.activation(dest[lane][:, 0:W], A, ACT.Relu, bias=w["shift"][:, :],
                                               scale=w["scale"][:, :]).then_inc(chain[lane].sem, 1)
                        for i, lane in at("y"):
                            A = node_psum(lane)
                            act.wait_ge(chain[lane].sem, S.after(lane, i, "w2"))
                            act.activation(n_feat_out[lane][:, 0:W], A, ACT.Identity, bias=w["b2"][:, :]).then_inc(chain[lane].sem, 1)
                        for i, lane in at("end" if final else "masked"):
                            act.wait_ge(chain[lane].sem, S.after(lane, i, "rows"))
                            node_store(act, S, i, lane, tout, n_rows_out[lane][:, 0:W], stored[lane].sem)
                    S.run(act, body)
                    for lane in range(DL):
                        act.wait_ge(stored[lane].sem, S.at["stored"][lane] + (S.rounds + (lane < S.rest)) * 16)

                @block.vector
                def _(dve):
                    def body(at):
                        for i, lane in at("rows"):
                            A = node_psum(lane)
                            dve.wait_ge(chain[lane].sem, S.after(lane, i, "t_out"))
                            dve.wait_ge(stored[lane].sem, S.dma("stored", lane, i, rounds=0))
                            if final:
                                dve.wait_ge(more_loaded[lane].sem, S.dma("more", lane, i))
                                dve.tensor_tensor(n_rows_out[lane][:, 0:W], A, n_resid[lane][:, 0:W], ALU.add).then_inc(chain[lane].sem, 1)
                            else:
                                dve.tensor_copy(n_rows_out[lane][:, 0:W], A).then_inc(chain[lane].sem, 1)
                        if not final:
                            for i, lane in at("masked"):
                                dve.wait_ge(chain[lane].sem, S.after(lane, i, "rows"))
                                node_sums_vector(dve, S, lane, i, n_rows_out[lane][:, 0:W])
                    S.run(dve, body)
            S.close()

        def node_final_phase():
            layer = ["t", "feat", "mm", "act", "back", "l2_square", "l2_sum", "l2_root", "l2_floor", "l2_inverse", "rows"]
            names = ["t_in", "feat", "mm", "act", "t_out", "x3"] + LN + [s + str(k) for k in range(3) for s in layer] + ["out"]
            S = Steps(names, DL, NB, loads=1, more=1, stores=1)
            with nc.Block() as block:
                @block.sync
                def _(sp):
                    def body(i, lanes):
                        for lane in lanes:
                            hold(sp, chain[lane].sem, S.after(lane, i - 1, "t_in"))
                            sp.dma_start(as3(n_rows_in[lane][:, 0:W]), node_rows(attn_nodes, i, lane)).then_inc(loaded[lane].sem, 16)
                        for lane in lanes:
                            hold(sp, chain[lane].sem, S.after(lane, i - 1, "x3"))
                            sp.dma_start(as3(n_resid[lane][:, 0:W]), node_rows(x2_nodes, i, lane)).then_inc(more_loaded[lane].sem, 16)
                    S.run_in_order(sp, body)

                @block.tensor
                def _(pe):
                    def body(at):
                        for i, lane in at("t_in"):
                            A = node_psum(lane)
                            pe.wait_ge(chain[lane].sem, S.start(lane, i))
                            pe.wait_ge(loaded[lane].sem, S.dma("loaded", lane, i))
                            transpose4(pe, A, n_rows_in[lane]).then_inc(chain[lane].sem, 1)
                        for i, lane in at("mm"):
                            A = node_psum(lane)
                            pe.wait_ge(chain[lane].sem, S.after(lane, i, "feat"))
                            pe.matmul(A, w_o[:, :], n_feat[lane][:, 0:W], start=True, stop=True).then_inc(chain[lane].sem, 1)
                        for i, lane in at("t_out"):
                            A = node_psum(lane)
                            pe.wait_ge(chain[lane].sem, S.after(lane, i, "act"))
                            transpose4(pe, A, n_feat_out[lane]).then_inc(chain[lane].sem, 1)
                        for k in range(3):
                            for i, lane in at(f"t{k}"):
                                A = node_psum(lane)
                                pe.wait_ge(chain[lane].sem, S.after(lane, i, f"rows{k - 1}" if k else "ln_out"))
                                transpose4(pe, A, n_centered[lane]).then_inc(chain[lane].sem, 1)
                            for i, lane in at(f"mm{k}"):
                                A = node_psum(lane)
                                pe.wait_ge(chain[lane].sem, S.after(lane, i, f"feat{k}"))
                                pe.matmul(A, gnn[k]["own"][:, :], n_feat[lane][:, 0:W], start=True, stop=True).then_inc(chain[lane].sem, 1)
                            for i, lane in at(f"back{k}"):
                                A = node_psum(lane)
                                pe.wait_ge(chain[lane].sem, S.after(lane, i, f"act{k}"))
                                transpose4(pe, A, n_feat_out[lane]).then_inc(chain[lane].sem, 1)
                    S.run(pe, body)

                @block.scalar
                def _(act):
                    def body(at):
                        for i, lane in at("feat"):
                            A = node_psum(lane)
                            act.wait_ge(chain[lane].sem, S.after(lane, i, "t_in"))
                            act.activation(n_feat[lane][:, 0:W], A, ACT.Copy).then_inc(chain[lane].sem, 1)
                        for i, lane in at("act"):
                            A = node_psum(lane)
                            act.wait_ge(chain[lane].sem, S.after(lane, i, "mm"))
                            act.activation(n_feat_out[lane][:, 0:W], A, ACT.Identity, bias=b_o[:, :]).then_inc(chain[lane].sem, 1)
                        ln_scalar(act, S, at, n_centered, n_squares, J)
                        for k in range(3):
                            for i, lane in at(f"feat{k}"):
                                A = node_psum(lane)
                                act.wait_ge(chain[lane].sem, S.after(lane, i, f"t{k}"))
                                act.activation(n_feat[lane][:, 0:W], A, ACT.Copy).then_inc(chain[lane].sem, 1)
                            for i, lane in at(f"act{k}"):
                                A = node_psum(lane)
                                act.wait_ge(chain[lane].sem, S.after(lane, i, f"mm{k}"))
                                act.activation(n_feat_out[lane][:, 0:W], A, ACT.Relu, bias=gnn[k]["bias"][:, :]).then_inc(chain[lane].sem, 1)
                            for i, lane in at(f"l2_square{k}"):
                                A = node_psum(lane)
                                act.wait_ge(chain[lane].sem, S.after(lane, i, f"back{k}"))
                                act.activation(n_squares[lane][:, 0:W], A, ACT.Square).then_inc(chain[lane].sem, 1)
                            for i, lane in at(f"l2_root{k}"):
                                act.wait_ge(chain[lane].sem, S.after(lane, i, f"l2_sum{k}"))
                                act.activation(stats[lane][:, 16:16 + J], stats[lane][:, 0:J], ACT.Sqrt).then_inc(chain[lane].sem, 1)
                        for i, lane in at("end"):
                            act.wait_ge(chain[lane].sem, S.after(lane, i, "out"))
                            node_store(act, S, i, lane, out, n_rows_out[lane][:, 0:W], stored[lane].sem)
                    S.run(act, body)
                    for lane in range(DL):
                        act.wait_ge(stored[lane].sem, S.at["stored"][lane] + (S.rounds + (lane < S.rest)) * 16)

                @block.vector
                def _(dve):
                    def body(at):
                        for i, lane in at("x3"):
                            A = node_psum(lane)
                            dve.wait_ge(chain[lane].sem, S.after(lane, i, "t_out"))
                            dve.wait_ge(stored[lane].sem, S.dma("stored", lane, i, rounds=0))
                            dve.wait_ge(more_loaded[lane].sem, S.dma("more", lane, i))
                            dve.tensor_tensor(n_rows_out[lane][:, 0:W], A, n_resid[lane][:, 0:W], ALU.add).then_inc(chain[lane].sem, 1)
                        def ready(i, lane):
                            dve.wait_ge(chain[lane].sem, S.after(lane, i, "x3"))

                        ln_vector(dve, S, at, ready, n_rows_out, n_centered, n_squares, J)
                        for k in range(3):
                            for i, lane in at(f"l2_sum{k}"):
                                dve.wait_ge(chain[lane].sem, S.after(lane, i, f"l2_square{k}"))
                                dve.tensor_reduce(stats[lane][:, 0:J], as3(n_squares[lane][:, 0:W]), AX, ALU.add).then_inc(chain[lane].sem, 1)
                            for i, lane in at(f"l2_floor{k}"):
                                dve.wait_ge(chain[lane].sem, S.after(lane, i, f"l2_root{k}"))
                                dve.tensor_scalar(stats[lane][:, 32:32 + J], stats[lane][:, 16:16 + J], L2_EPS, None, ALU.max).then_inc(chain[lane].sem, 1)
                            for i, lane in at(f"l2_inverse{k}"):
                                dve.wait_ge(chain[lane].sem, S.after(lane, i, f"l2_floor{k}"))
                                dve.reciprocal(stats[lane][:, 48:48 + J], stats[lane][:, 32:32 + J]).then_inc(chain[lane].sem, 1)
                            for i, lane in at(f"rows{k}"):
                                dve.wait_ge(chain[lane].sem, S.after(lane, i, f"l2_inverse{k}"))
                                dve.tensor_tensor(as3(n_centered[lane][:, 0:W]), as3(node_psum(lane)), stats[lane][:, 48:48 + J].unsqueeze(2).broadcast_to([P, J, D]),
                                                  ALU.mult).then_inc(chain[lane].sem, 1)
                        for i, lane in at("out"):
                            dve.wait_ge(chain[lane].sem, S.after(lane, i, "rows2"))
                            dve.tensor_tensor(n_rows_out[lane][:, 0:W], n_rows_out[lane][:, 0:W], n_centered[lane][:, 0:W], ALU.add).then_inc(chain[lane].sem, 1)
                    S.run(dve, body)
            S.close()

        def coefficients_phase(l):
            w = gin[l]
            s0 = setup_step.base
            with nc.Block() as block:
                @block.vector
                def _(dve):
                    step = [s0]

                    def link(op):
                        step[0] += 1
                        op.then_inc(setup_step.sem, 1)
                        dve.wait_ge(setup_step.sem, step[0])

                    k = w["keep"][0:D, :]
                    link(dve.tensor_copy(moments_edges[:, :], gram_edges[0:D, 0:D + 1]))
                    link(dve.tensor_scalar(moments[:, :], gram_nodes[0:D, 0:D + 1], k, None, ALU.mult))
                    link(dve.tensor_scalar(moments[:, 0:D], moments[:, 0:D], k, None, ALU.mult))
                    link(dve.tensor_tensor(moments[:, :], moments[:, :], moments_edges[:, :], ALU.add))
                    link(dve.tensor_scalar(moments[:, :], moments[:, :], 1.0 / N, None, ALU.mult))
                    step[0] += 1
                    dve.wait_ge(setup_step.sem, step[0])
                    link(dve.tensor_tensor(w1_moments[:, :], work[0:D, 0:H], w["w1"][0:D, :], ALU.mult))
                    link(dve.tensor_copy(coef[:, 0:1], work[:, 512:513]))
                    link(dve.tensor_tensor(coef[:, 1:2], coef[:, 0:1], coef[:, 0:1], ALU.mult))
                    step[0] += 1
                    dve.wait_ge(setup_step.sem, step[0])
                    link(dve.tensor_tensor(coef[:, 2:3], work[:, 1024:1025], coef[:, 1:2], ALU.subtract))
                    link(dve.tensor_scalar(coef[:, 2:3], coef[:, 2:3], 0.0, None, ALU.max))
                    step[0] += 1
                    dve.wait_ge(setup_step.sem, step[0])
                    link(dve.reciprocal(coef[:, 4:5], coef[:, 3:4]))
                    link(dve.tensor_tensor(w["scale"][:, :], coef[:, 4:5], w["gamma"][:, :], ALU.mult))
                    link(dve.tensor_tensor(coef[:, 5:6], coef[:, 0:1], w["b1"][:, :], ALU.add))
                    link(dve.tensor_tensor(coef[:, 6:7], w["b1"][:, :], coef[:, 5:6], ALU.subtract))
                    link(dve.tensor_tensor(coef[:, 7:8], coef[:, 6:7], w["scale"][:, :], ALU.mult))
                    link(dve.tensor_tensor(w["shift"][:, :], coef[:, 7:8], w["beta"][:, :], ALU.add))

                @block.tensor
                def _(pe):
                    pe.wait_ge(setup_step.sem, s0 + 5)
                    pe.matmul(work[0:D, 0:H], moments[0:D, 0:D], w["w1"][0:D, :], start=True, stop=True)
                    pe.matmul(work[:, 512:513], w["w1"][0:D, :], moments[0:D, D:D + 1], start=True, stop=True).then_inc(setup_step.sem, 1)
                    pe.wait_ge(setup_step.sem, s0 + 9)
                    pe.matmul(work[:, 1024:1025], w1_moments[0:D, :], ones[0:D, 0:1], start=True, stop=True).then_inc(setup_step.sem, 1)

                @block.scalar
                def _(act):
                    act.wait_ge(setup_step.sem, s0 + 12)
                    act.activation(coef[:, 3:4], coef[:, 2:3], ACT.Sqrt, bias=eps_bn[:, :]).then_inc(setup_step.sem, 1)
            setup_step.base += 19

        node_sage_phase()
        edge_phase("sage", 0, "nodes", None, sd[0], ln=True)
        edge_phase("sage", 1, "links", sd[0], sd[1])
        edge_phase("sage", 2, "links", sd[1], sd[0], add_resid=True)
        edge_phase("gin", 0, "links", sd[0], None, ln=True)
        coefficients_phase(0)
        node_gin_phase(0)
        gin_edge_phase(0, sd[1], False)
        edge_phase("gin", 1, "links", sd[1], None)
        coefficients_phase(1)
        node_gin_phase(1)
        gin_edge_phase(1, sd[0], False)
        edge_phase("gin", 2, "links", sd[0], None)
        coefficients_phase(2)
        node_gin_phase(2)
        gin_edge_phase(2, sd[1], True)
        edge_phase("qkv", 0, "links", sd[1], None, ln=True)
        attention_phase()
        edge_phase("proj", 0, "attention", None, sd[0], add_resid=True)
        node_final_phase()
        edge_phase("gnn", 0, "rows", sd[0], sd[1], ln=True)
        edge_phase("gnn", 1, "links", sd[1], sd[0])
        edge_phase("gnn", 2, "links", sd[0], sd[1], add_resid=True)
        scatter_phase(sd[1])


_CONST = None


def kernel(**inputs):
    import numpy as _np
    import concourse.bacc as _bacc
    from concourse import mybir as _mybir
    from concourse.bass_utils import run_bass_kernel_spmd as _run

    nc = _bacc.Bacc("TRN2", target_bir_lowering=False, num_devices=1)
    arrays, tensors = {}, {}
    for name, value in inputs.items():
        a = _np.asarray(value)
        if name.startswith("L0_gnn_w"):
            a = a.T
        a = _np.ascontiguousarray(a)
        arrays[f"in_{name}"] = a
        tensors[name] = nc.dram_tensor(f"in_{name}", a.shape, _mybir.dt.from_np(a.dtype), kind="ExternalInput").ap()
    shape = tuple(int(n) for n in inputs["x"].shape)
    out = nc.dram_tensor("out", shape, _mybir.dt.float32, kind="ExternalOutput").ap()
    build_program(nc, tensors, out)
    r = _run(nc, [arrays], core_ids=[0])
    return r.results[0]["out"]
```

```python
class Counted:

    def __init__(self, sem):
        self.sem, self.base = sem, 0


def build_program(nc, t, out):
    import concourse.bass as bass
    from concourse import mybir
    from contextlib import ExitStack
    import numpy as np

    f32, i32, bf16 = mybir.dt.float32, mybir.dt.int32, mybir.dt.bfloat16
    ALU = mybir.AluOpType
    ACT = mybir.ActivationFunctionType
    AX = mybir.AxisListType.X
    ds = bass.ds

    P = 128
    N, D = t["x"].shape
    E = t["src"].shape[0]
    J = 8
    BLK = P * J
    H = t["L1_gnn_W1"].shape[2]
    HEADS = 8
    HD = D // HEADS
    EB = -(-E // BLK)
    EP = EB * BLK
    ET = EB * J
    NB = -(-N // BLK)
    OVER = (NB * BLK - N) // J
    assert NB * BLK - N == OVER * J and E % J == 0
    BIG = 1 << 22
    NEG = -1.0e30
    LN_EPS, BN_EPS, L2_EPS, SM_EPS = 1e-5, 1e-5, 1e-12, 1e-8
    DL, EL = 6, 3
    REC = 80
    DIGIT = 6
    RADIX = 1 << DIGIT
    PASSES = -(-int(N).bit_length() // DIGIT)

    ctx = ExitStack()
    with ctx:
        def dram(name, shape, dt=f32):
            return nc.dram_tensor(name, shape, dt).ap()

        def sb(name, shape, dt=f32, c=ctx):
            return c.enter_context(nc.sbuf_tensor(name, shape, dt))

        def counted(name):
            return Counted(ctx.enter_context(nc.semaphore(name)))

        x1_nodes = dram("x1_nodes", (N, D))
        x2_nodes = dram("x2_nodes", (N, D))
        h_nodes = [dram(f"h_nodes{k}", (N, D)) for k in range(2)]
        attn_nodes = dram("attn_nodes", (N, D))
        pos_nodes = dram("pos_nodes", (N, 1), i32)
        sd = [dram(f"sd{k}", (EP, 2 * D)) for k in range(2)]
        sd_resid = dram("sd_resid", (EP, 2 * D))
        gin_x = dram("gin_x", (EB, P, BLK))
        gin_agg = dram("gin_agg", (EB, D, BLK))
        edge_state = dram("edge_state", (EB, D, BLK))
        records = dram("records", (EP, REC))
        src_pad = dram("src_pad", (EP,), i32)
        dst_pad = dram("dst_pad", (EP + 2 * J,), i32)
        key_pad = dram("key_pad", (EP + 2 * J,), i32)
        same_dst = dram("same_dst", (EP,))
        inv_deg = dram("inv_deg", (EP,))
        neg_start = dram("neg_start", (EP,))
        sorting = [dram(f"sorting{k}", (EP, 2), i32) for k in range(2)]

        def rows(table, b, width=None):
            return table[ds(b * BLK, BLK), :].rearrange("(p j) d -> p j d", j=J)

        def cols_bj(vec):
            return vec.rearrange("(b p j) -> p b j", p=P, j=J)

        chain = [counted(f"lane{k}_steps_done") for k in range(DL)]
        loaded = [counted(f"lane{k}_loaded") for k in range(DL)]
        stored = [counted(f"lane{k}_stored") for k in range(DL)]
        gathered = [counted(f"lane{k}_gathered") for k in range(EL)]
        held = {nc.gpsimd.engine: counted("gpsimd_waits_passed"), nc.sync.engine: counted("sync_waits_passed")}
        staged = [counted(f"indices_staged{k}") for k in range(EL)]
        setup_dma = counted("setup_dma")
        setup_step = counted("setup_step")
        weights_in = counted("weights_in")
        zeroed = counted("weights_zeroed")
        attn_zeroed = counted("attention_table_zeroed")

        ident = sb("ident", [P, P])
        src_clamped = sb("src_clamped", [P, ET], i32)
        dst_clamped = sb("dst_clamped", [P, ET], i32)
        link_idx = sb("link_idx", [P, ET], i32)
        home_idx = sb("home_idx", [P, ET], i32)
        last_dst_idx = sb("last_dst_idx", [P, ET], i32)
        rep_mask = sb("rep_mask", [P, ET])
        node_mask = sb("node_mask", [P, NB * J])
        sorted_edge = sb("sorted_edge", [P, ET], i32)
        attn_out_idx = sb("attn_out_idx", [P, ET], i32)
        idx_stage = [sb(f"idx_stage{k}", [P, 2 * J], i32) for k in range(EL)]
        val_stage = [sb(f"val_stage{k}", [P, J], i32) for k in range(EL)]
        rec_stage = [sb(f"rec_stage{k}", [P, J, 2], i32) for k in range(EL)]
        rec_i = sb("rec_i", [P, EB, J, 2], i32)
        edge_rank = sb("edge_rank", [P, ET], i32)
        zeros = sb("zeros", [P, J * D])
        eps_ln = sb("eps_ln", [P, 1])
        eps_bn = sb("eps_bn", [P, 1])
        ones = sb("ones", [P, P])

        work = ctx.enter_context(nc.psum_tensor("work", [P, 6 * 512], f32))
        gram_nodes = ctx.enter_context(nc.psum_tensor("gram_nodes", [P, 512], f32))
        gram_edges = ctx.enter_context(nc.psum_tensor("gram_edges", [P, 512], f32))

        zero_tiles, weight_loads = [], []

        def weight(name, shape, parts, zero=False):
            tile = sb(name, shape)
            if zero:
                zero_tiles.append(tile)
            for where, src in parts(tile):
                weight_loads.append((where, src))
            return tile

        def column(name, vec, copies):
            n = vec.shape[0]
            return weight(name, [P, 1], lambda w: [
                (w[k * n:(k + 1) * n, :], vec.rearrange("(n o) -> n o", o=1)) for k in range(copies)])

        def block_diag(name, m):
            return weight(name, [P, P], lambda w: [(w[0:D, 0:D], m), (w[D:P, D:P], m)], zero=True)

        def to_dst(name, m, at=0):
            return weight(name, [P, P], lambda w: [(w[at:at + m.shape[0], D:P], m)], zero=True)

        sage = []
        for l in range(3):
            sage.append(dict(own=block_diag(f"sage_own{l}", t[f"L0_gnn_wr{l}"]),
                             agg=to_dst(f"sage_agg{l}", t[f"L0_gnn_wl{l}"]),
                             bias=column(f"sage_bias{l}", t[f"L0_gnn_bl{l}"], 2)))
        gin = []
        for l in range(3):
            w1, w2 = t["L1_gnn_W1"][l], t["L1_gnn_W2"][l]
            eps_all = t["L1_gnn_eps"]
            gin.append(dict(
                w1=weight(f"gin_w1_{l}", [P, H], lambda w: [(w[0:D, :], w1), (w[D:P, :], w1)]),
                w1_own=sb(f"gin_w1_own{l}", [P, H]),
                w1_dst=sb(f"gin_w1_dst{l}", [P, H]),
                keep=weight(f"gin_keep{l}", [P, 1], lambda w: [(w[:, :], eps_all[l:l + 1].partition_broadcast(P))]),
                keep_ident=sb(f"gin_keep_ident{l}", [P, D]),
                w2_src=weight(f"gin_w2_src{l}", [P, P], lambda w: [(w[:, 0:D], w2)], zero=True),
                w2_dst=weight(f"gin_w2_dst{l}", [P, P], lambda w: [(w[:, D:P], w2)], zero=True),
                b1=column(f"gin_b1_{l}", t["L1_gnn_b1"][l], 1),
                gamma=column(f"gin_gamma{l}", t["L1_gnn_gamma"][l], 1),
                beta=column(f"gin_beta{l}", t["L1_gnn_beta"][l], 1),
                b2=column(f"gin_b2_{l}", t["L1_gnn_b2"][l], 2),
                scale=sb(f"gin_scale{l}", [P, 1]), shift=sb(f"gin_shift{l}", [P, 1])))
        w_qkv = weight("w_qkv", [P, 2 * D], lambda w: [
            (w[0:D, 0:D], t["L2_gnn_Wq"]), (w[D:P, 0:D], t["L2_gnn_Wk"]), (w[D:P, D:P], t["L2_gnn_Wv"])], zero=True)
        b_qkv = weight("b_qkv", [P, 3, D], lambda w: [
            (w[:, k, :], t[f"L2_gnn_b{c}"].partition_broadcast(P)) for k, c in enumerate("qkv")])
        w_o = block_diag("w_o", t["L2_gnn_Wo"])
        b_o = column("b_o", t["L2_gnn_bo"], 2)
        gnn = []
        for l in range(3):
            aw = t["L3_gnn_agg_W"][l]
            g = dict(msg=weight(f"gnn_msg{l}", [P, D], lambda w: [(w[:, :], t["L3_gnn_msg_W"][l])]),
                     msg_b=column(f"gnn_msg_b{l}", t["L3_gnn_msg_b"][l], 1),
                     own=block_diag(f"gnn_own{l}", aw[D:2 * D, :]),
                     agg=to_dst(f"gnn_agg{l}", aw[0:D, :]),
                     bias=column(f"gnn_bias{l}", t["L3_gnn_agg_b"][l], 2))
            if l > 0:
                ew, eb = t["L3_gnn_edge_W"][l - 1], t["L3_gnn_edge_b"][l - 1]
                g.update(edge_nodes=to_dst(f"gnn_edge_nodes{l}", ew[0:2 * D, :]),
                         edge_own=to_dst(f"gnn_edge_own{l}", ew[2 * D:3 * D, :], at=D),
                         edge_b=column(f"gnn_edge_b{l}", eb, 2))
            gnn.append(g)
        pick_max = sb("pick_max", [P, 72])
        pick_score = sb("pick_score", [P, 72])

        def engine_setup_counts(n):
            setup_step.base += n

        with nc.Block() as block:
            @block.gpsimd
            def _(pool):
                for tile in zero_tiles:
                    pool.memset(tile[:, :], 0.0).then_inc(zeroed.sem, 1)
                pool.memset(ones[:, :], 1.0).then_inc(setup_step.sem, 1)
                pool.memset(eps_ln[:, :], LN_EPS).then_inc(setup_step.sem, 1)
                pool.memset(eps_bn[:, :], BN_EPS).then_inc(setup_step.sem, 1)
                pool.memset(ident[:, :], 0.0).then_inc(setup_step.sem, 1)
                pool.memset(pick_max[:, :], 0.0).then_inc(setup_step.sem, 1)
                pool.memset(pick_score[:, :], 0.0).then_inc(setup_step.sem, 1)
                pool.wait_ge(setup_step.sem, 6)
                pool.affine_select(out=ident[:, :], in_=ident[:, :], compare_op=ALU.not_equal, fill=1.0,
                                   base=0, pattern=[[-1, P]], channel_multiplier=1).then_inc(setup_step.sem, 1)
                pool.affine_select(out=pick_max[:, :], in_=pick_max[:, :], compare_op=ALU.not_equal, fill=1.0,
                                   base=-72, pattern=[[0, 72]], channel_multiplier=1).then_inc(setup_step.sem, 1)
                pool.affine_select(out=pick_score[:, 0:D].rearrange("p (h d) -> p h d", d=HD),
                                   in_=pick_score[:, 0:D].rearrange("p (h d) -> p h d", d=HD),
                                   compare_op=ALU.not_equal, fill=1.0, base=-D,
                                   pattern=[[-1, HEADS], [0, HD]], channel_multiplier=1).then_inc(setup_step.sem, 1)
                pool.affine_select(out=pick_score[:, D:72], in_=pick_score[:, D:72],
                                   compare_op=ALU.not_equal, fill=1.0, base=-D,
                                   pattern=[[-1, HEADS]], channel_multiplier=1).then_inc(setup_step.sem, 1)
                pool.wait_ge(setup_step.sem, 10)

        setup_step.base = 10

        def load_weights(act):
            act.wait_ge(zeroed.sem, len(zero_tiles))
            for where, src in weight_loads:
                act.dma_start(where, src).then_inc(weights_in.sem, 16)

        def scale_weights():
            s0 = setup_step.base
            with nc.Block() as block:
                @block.vector
                def _(dve):
                    dve.wait_ge(weights_in.sem, 16 * len(weight_loads))
                    for g in gin:
                        dve.tensor_scalar(g["keep"][:, :], g["keep"][:, :], 1.0, None, ALU.add).then_inc(setup_step.sem, 1)
                    dve.wait_ge(setup_step.sem, s0 + 3)
                    for g in gin:
                        dve.tensor_scalar(g["w1_own"][:, :], g["w1"][:, :], g["keep"][:, :], None, ALU.mult)
                        dve.memset(g["w1_dst"][0:D, :], 0.0)
                        dve.tensor_scalar(g["w1_dst"][D:P, :], g["w1"][D:P, :], g["keep"][D:P, :], None, ALU.mult)
                        dve.memset(g["keep_ident"][0:D, :], 0.0)
                        dve.tensor_scalar(g["keep_ident"][D:P, :], ident[D:P, D:P], g["keep"][D:P, :], None,
                                          ALU.mult).then_inc(setup_step.sem, 1)
                    dve.wait_ge(setup_step.sem, s0 + 6)
            setup_step.base += 6

        def segment_phase(key_table, first_name, as_flags, out_idx, rep, start_table):
            with ExitStack() as c:
                keys = sb(first_name + "_keys", [P, 3, EB, J], i32, c)
                keysf = sb(first_name + "_keysf", [P, 3, ET], f32, c)
                start = sb(first_name + "_start", [P, ET], f32, c)
                last = sb(first_name + "_last", [P, ET], f32, c)
                valid = sb(first_name + "_valid", [P, ET], f32, c)
                idxf = sb(first_name + "_idxf", [P, ET], f32, c)
                with nc.Block() as block:
                    d0, s0 = setup_dma.base, setup_step.base

                    @block.sync
                    def _(sp):
                        for k, shift in enumerate((J - 1, J, J + 1)):
                            sp.dma_start(keys[:, k, :, :], cols_bj(key_table[shift:shift + EP])).then_inc(setup_dma.sem, 16)
                        sp.wait_ge(setup_step.sem, s0 + 7)
                        sp.dma_start(cols_bj(start_table[:]), start[:, :].rearrange("p (b j) -> p b j", j=J)).then_inc(setup_dma.sem, 16)
                        sp.wait_ge(setup_dma.sem, d0 + 64)

                    @block.vector
                    def _(dve):
                        step = [s0]

                        def link(op):
                            step[0] += 1
                            op.then_inc(setup_step.sem, 1)
                            dve.wait_ge(setup_step.sem, step[0])

                        dve.wait_ge(setup_dma.sem, d0 + 48)
                        link(dve.tensor_copy(keysf[:, :, :], keys[:, :, :, :].rearrange("p k b j -> p k (b j)")))
                        link(dve.tensor_tensor(start[:, :], keysf[:, 1, :], keysf[:, 0, :], ALU.is_equal))
                        link(dve.tensor_tensor(last[:, :], keysf[:, 1, :], keysf[:, 2, :], ALU.not_equal))
                        link(dve.scalar_tensor_tensor(rep, keysf[:, 1, :], float(N), last[:, :], ALU.is_lt, ALU.mult))
                        link(dve.scalar_tensor_tensor(idxf[:, :], keysf[:, 1, :], -float(BIG), rep, ALU.add, ALU.mult))
                        link(dve.tensor_scalar(out_idx, idxf[:, :], float(BIG), None, ALU.add))
                        if as_flags:
                            link(dve.tensor_scalar(start[:, :], start[:, :], 1.0, None, ALU.mult))
                        else:
                            link(dve.tensor_scalar(start[:, :], start[:, :], -NEG, NEG, ALU.mult, ALU.add))
                        step_total[0] = step[0]

                    setup_step.base = step_total[0]
                    setup_dma.base = d0 + 64

        step_total = [0]
        KP = EP // P
        full, rest = E // KP, E % KP
        with ExitStack() as c:
            keys_in = sb("keys_in", [P, 2, KP], i32, c)
            edge_marks = sb("edge_marks", [1, J], i32, c)
            key_big = sb("key_big", [P, 1024], i32, c)
            with nc.Block() as block:
                d0, s0 = setup_dma.base, setup_step.base

                @block.vector
                def _(dve):
                    dve.memset(keys_in[:, :, :], N).then_inc(setup_step.sem, 1)
                    dve.memset(edge_marks[:, :], -1).then_inc(setup_step.sem, 1)
                    dve.memset(key_big[:, :], BIG).then_inc(setup_step.sem, 1)
                    dve.memset(zeros[:, :], 0.0).then_inc(setup_step.sem, 1)

                @block.sync
                def _(sp):
                    sp.wait_ge(setup_step.sem, s0 + 4)
                    n = 0
                    for k, key in enumerate(("src", "dst")):
                        sp.dma_start(keys_in[0:full, k, :], t[key][0:full * KP].rearrange("(p k) -> p k", k=KP)).then_inc(setup_dma.sem, 16)
                        n += 1
                        if rest:
                            sp.dma_start(keys_in[full:full + 1, k, 0:rest], t[key][full * KP:E].rearrange("(p k) -> p k", p=1)).then_inc(setup_dma.sem, 16)
                            n += 1
                    sp.wait_ge(setup_dma.sem, d0 + 16 * n)
                    sp.dma_start(src_pad.rearrange("(p k) -> p k", k=KP), keys_in[:, 0, :]).then_inc(setup_dma.sem, 16)
                    sp.dma_start(dst_pad[J:J + EP].rearrange("(p k) -> p k", k=KP), keys_in[:, 1, :]).then_inc(setup_dma.sem, 16)
                    n += 2
                    for table in (dst_pad, key_pad):
                        for at in (0, J + EP):
                            sp.dma_start(table[at:at + J].rearrange("(o j) -> o j", o=1), edge_marks[:, :]).then_inc(setup_dma.sem, 16)
                            n += 1
                    for k in range(-(-N // (P * 512))):
                        lo, hi = k * P * 512, min(N, (k + 1) * P * 512)
                        w = (hi - lo) // P
                        if w:
                            sp.dma_start(pos_nodes[lo:lo + w * P, :].rearrange("(p w) o -> p (w o)", p=P), key_big[:, 0:w]).then_inc(setup_dma.sem, 16)
                            n += 1
                        r = (hi - lo) - w * P
                        if r:
                            sp.dma_start(pos_nodes[hi - r:hi, :].rearrange("(o w) u -> o (w u)", o=1), key_big[0:1, 0:r]).then_inc(setup_dma.sem, 16)
                            n += 1
                    sp.wait_ge(setup_dma.sem, d0 + 16 * n)
                    step_total[0] = d0 + 16 * n

            setup_step.base += 4
            setup_dma.base = step_total[0]

        segment_phase(dst_pad, "dst", True, last_dst_idx[:, :], rep_mask[:, :], same_dst)

        def hold(engine, sem, value):
            engine.wait_ge(sem, value)
            engine.sem_inc(held[engine.engine].sem, 1)

        def in_turns(pool, slots, issue, finish):
            turns, rest = EB // slots, EB % slots
            for slot in range(min(slots, EB)):
                issue(slot, 0, slot)
            if turns > 1:
                with pool.Fori(1, turns) as n:
                    for slot in range(slots):
                        finish(slot, n - 1, (n - 1) * slots + slot)
                        issue(slot, n, n * slots + slot)
            for slot in range(rest if turns else 0):
                finish(slot, turns - 1, (turns - 1) * slots + slot)
                issue(slot, turns, turns * slots + slot)
            for slot in range(min(slots, EB)):
                last = turns if slot < rest else turns - 1
                if turns == 0:
                    last = 0
                finish(slot, last, last * slots + slot)

        def turns_of(slot, slots):
            return EB // slots + (slot < EB % slots)

        def read_slots(pool, table, found):
            def read(slot, n, b):
                pool.tensor_copy(idx_stage[slot][:, 0:J], table[:, ds(b * J, J)]).then_inc(staged[slot].sem, 1)
                hold(pool, staged[slot].sem, n * 2 + (staged[slot].base + 1))
                for j in range(J):
                    pool.indirect_dma_start(val_stage[slot][:, j:j + 1], None, pos_nodes[:, :],
                                            bass.IndirectOffsetOnAxis(idx_stage[slot][:, j:j + 1], 0),
                                            bounds_check=N - 1, oob_is_err=False).then_inc(gathered[slot].sem, 16)

            def keep(slot, n, b):
                hold(pool, gathered[slot].sem, n * (16 * J) + (gathered[slot].base + 16 * J))
                pool.tensor_copy(found[:, ds(b * J, J)], val_stage[slot][:, :]).then_inc(staged[slot].sem, 1)
                hold(pool, staged[slot].sem, n * 2 + (staged[slot].base + 2))

            in_turns(pool, EL, read, keep)
            for slot in range(EL):
                staged[slot].base += 2 * turns_of(slot, EL)
                gathered[slot].base += 16 * J * turns_of(slot, EL)

        def scatter_to_ranks(pool, table, rank, rec):
            def scatter(slot, n, b):
                pool.tensor_copy(idx_stage[slot][:, 0:J], rank[:, ds(b * J, J)]).then_inc(staged[slot].sem, 1)
                pool.tensor_copy(rec_stage[slot][:, :, :].rearrange("p j t -> p (j t)"),
                                 rec[:, :, :, :].rearrange("p b j t -> p (b j t)")[:, ds(b * (2 * J), 2 * J)]).then_inc(staged[slot].sem, 1)
                hold(pool, staged[slot].sem, n * 2 + (staged[slot].base + 2))
                for j in range(J):
                    pool.indirect_dma_start(table[:, :], bass.IndirectOffsetOnAxis(idx_stage[slot][:, j:j + 1], 0),
                                            rec_stage[slot][:, j, :], None, bounds_check=EP - 1,
                                            oob_is_err=False).then_inc(gathered[slot].sem, 16)

            def landed(slot, n, b):
                hold(pool, gathered[slot].sem, n * (16 * J) + (gathered[slot].base + 16 * J))

            in_turns(pool, EL, scatter, landed)
            for slot in range(EL):
                staged[slot].base += 2 * turns_of(slot, EL)
                gathered[slot].base += 16 * J * turns_of(slot, EL)

        with ExitStack() as c:
            iota_edge = sb("iota_edge", [P, ET], i32, c)
            src_i = sb("src_i", [P, EB, J], i32, c)
            dst_i = sb("dst_i", [P, EB, J], i32, c)
            pos_i = sb("pos_i", [P, NB, J], i32, c)
            slots_written = counted("slots_written")
            length_dma = counted("length_dma")
            length_step = counted("length_step")
            CH = EP // 4 if EP % (4 * J) == 0 else EP
            run = sb("run", [1, CH], f32, c)
            length = sb("length", [1, CH + 1], f32, c)
            one_row = sb("one_row", [1, CH], f32, c)
            with nc.Block() as block:
                d0, s0, g0 = setup_dma.base, setup_step.base, [g.base for g in gathered]

                @block.sync
                def _(sp):
                    sp.dma_start(src_i[:, :, :], cols_bj(src_pad[:])).then_inc(setup_dma.sem, 16)
                    sp.dma_start(dst_i[:, :, :], cols_bj(dst_pad[J:J + EP])).then_inc(setup_dma.sem, 16)
                    for k in range(EP // CH):
                        if k:
                            sp.wait_ge(length_step.sem, 1 + 2 * k)
                        sp.dma_start(run[0:1, :], same_dst[k * CH:(k + 1) * CH].rearrange("(o n) -> o n", o=1)).then_inc(length_dma.sem, 16)
                        sp.wait_ge(length_step.sem, 1 + 2 * (k + 1))
                        sp.dma_start(inv_deg[k * CH:(k + 1) * CH].rearrange("(o n) -> o n", o=1), run[0:1, :]).then_inc(length_dma.sem, 16)
                        sp.wait_ge(length_dma.sem, 32 * (k + 1))
                    sp.wait_ge(slots_written.sem, 1)
                    sp.dma_start(pos_i[:, 0:NB - 1, :], pos_nodes[0:(NB - 1) * BLK, :].rearrange("(b p j) o -> p b (j o)", p=P, j=J)).then_inc(setup_dma.sem, 16)
                    sp.dma_start(pos_i[:, NB - 1, :], pos_nodes[N - BLK:N, :].rearrange("(p j) o -> p (j o)", j=J)).then_inc(setup_dma.sem, 16)

                @block.vector
                def _(dve):
                    dve.wait_ge(setup_dma.sem, d0 + 32)
                    dve.tensor_scalar(src_clamped[:, :], src_i[:, :, :].rearrange("p b j -> p (b j)"), float(N - 1), None, ALU.min).then_inc(setup_step.sem, 1)
                    dve.tensor_scalar(dst_clamped[:, :], dst_i[:, :, :].rearrange("p b j -> p (b j)"), float(N - 1), None, ALU.min).then_inc(setup_step.sem, 1)
                    dve.memset(one_row[0:1, :], 1.0).then_inc(length_step.sem, 1)
                    for k in range(EP // CH):
                        dve.wait_ge(length_step.sem, 1 + 2 * k)
                        dve.wait_ge(length_dma.sem, 32 * k + 16)
                        dve.tensor_tensor_scan(length[0:1, 1:CH + 1], run[0:1, :], one_row[0:1, :],
                                               length[0:1, CH:CH + 1] if k else 0.0, ALU.mult, ALU.add).then_inc(length_step.sem, 1)
                        dve.wait_ge(length_step.sem, 2 + 2 * k)
                        dve.reciprocal(run[0:1, :], length[0:1, 1:CH + 1]).then_inc(length_step.sem, 1)
                    dve.wait_ge(setup_dma.sem, d0 + 64)
                    dve.tensor_scalar(node_mask[:, :], pos_i[:, :, :].rearrange("p b j -> p (b j)"), float(BIG), None, ALU.is_equal).then_inc(setup_step.sem, 1)
                    dve.wait_ge(setup_step.sem, s0 + 4)
                    dve.memset(node_mask[0:max(OVER, 1), (NB - 1) * J:NB * J], 0.0).then_inc(setup_step.sem, 1)
                    dve.wait_ge(setup_step.sem, s0 + 5)

                @block.gpsimd
                def _(pool):
                    def write_slots(slot, n, b):
                        pool.tensor_copy(idx_stage[slot][:, 0:J], last_dst_idx[:, ds(b * J, J)]).then_inc(staged[slot].sem, 1)
                        pool.tensor_copy(val_stage[slot][:, :], iota_edge[:, ds(b * J, J)]).then_inc(staged[slot].sem, 1)
                        hold(pool, staged[slot].sem, n * 2 + (staged[slot].base + 2))
                        for j in range(J):
                            pool.indirect_dma_start(pos_nodes[:, :], bass.IndirectOffsetOnAxis(idx_stage[slot][:, j:j + 1], 0),
                                                    val_stage[slot][:, j:j + 1], None, bounds_check=N - 1,
                                                    oob_is_err=False).then_inc(gathered[slot].sem, 16)

                    def written(slot, n, b):
                        hold(pool, gathered[slot].sem, n * (16 * J) + (gathered[slot].base + 16 * J))

                    pool.iota(iota_edge[:, :], pattern=[[BLK, EB], [1, J]], base=0, channel_multiplier=J).then_inc(setup_step.sem, 1)
                    pool.wait_ge(setup_step.sem, s0 + 3)
                    in_turns(pool, EL, write_slots, written)
                    pool.nop().then_inc(slots_written.sem, 1)
                    for slot in range(EL):
                        staged[slot].base += 2 * turns_of(slot, EL)
                        gathered[slot].base += 16 * J * turns_of(slot, EL)
            setup_dma.base += 64
            setup_step.base += 5

        with ExitStack() as c:
            tile_major = [sb(f"sort_keys{k}", [P, ET], i32, c) for k in range(2)]
            digit_i = sb("digit_i", [P, ET], i32, c)
            digit = sb("digit", [P, ET], bf16, c)
            digit_iota = sb("digit_iota", [P, RADIX], bf16, c)
            onehot = sb("onehot", [P, ET * RADIX], bf16, c)
            earlier = sb("earlier", [P, P], bf16, c)
            ones_bf = sb("ones_bf", [P, P], bf16, c)
            counts = sb("counts", [P, RADIX * ET], f32, c)
            place = sb("place", [P, ET * RADIX], f32, c)
            rank = sb("rank", [P, ET], f32, c)
            rank_i = [sb(f"rank_i{k}", [P, ET], i32, c) for k in range(3)]
            rank_made = counted("rank_made")
            src_i_again = sb("src_i_again", [P, EB, J], i32, c)
            iota_again = sb("iota_again", [P, ET], i32, c)
            setup_edge = counted("sort_constants")
            setup_edge0 = counted("sort_zeros")
            TPC = 512 // RADIX
            NCH = ET // TPC
            for n_pass in range(PASSES):
                last_pass = n_pass == PASSES - 1
                with nc.Block() as block:
                    d0, s0 = setup_dma.base, setup_step.base
                    c0, r0 = chain[0].base, chain[1].base
                    m0 = rank_made.base

                    @block.sync
                    def _(sp):
                        if n_pass:
                            sp.dma_start(rec_i[:, :, :, :], sorting[(n_pass - 1) % 2].rearrange("(b p j) t -> p b (j t)", p=P, j=J)).then_inc(setup_dma.sem, 16)
                        else:
                            sp.dma_start(src_i_again[:, :, :], cols_bj(src_pad[:])).then_inc(setup_dma.sem, 16)
                            with sp.Fori(0, NB - 1) as b:
                                sp.dma_start(rows(attn_nodes, b), zeros[:, :].rearrange("p (j d) -> p j d", j=J)).then_inc(attn_zeroed.sem, 16)
                            sp.dma_start(attn_nodes[(NB - 1) * BLK:N, :].rearrange("(p j) d -> p j d", j=J),
                                         zeros[OVER:P, :].rearrange("p (j d) -> p j d", j=J)).then_inc(attn_zeroed.sem, 16)

                    @block.vector
                    def _(dve):
                        step = [s0]

                        def link(op):
                            step[0] += 1
                            op.then_inc(setup_step.sem, 1)
                            dve.wait_ge(setup_step.sem, step[0])

                        dve.wait_ge(setup_dma.sem, d0 + 16)
                        if n_pass == 0:
                            dve.wait_ge(setup_edge.sem, 4)
                            link(dve.tensor_copy(rec_i[:, :, :, 0], src_i_again[:, :, :]))
                            link(dve.tensor_copy(rec_i[:, :, :, 1], iota_again[:, :].rearrange("p (b j) -> p b j", j=J)))
                        keys = rec_i[:, :, :, 0].rearrange("p b j -> p (b j)")
                        link(dve.tensor_copy(tile_major[0][:, :], keys))
                        link(dve.tensor_scalar(digit_i[:, :], tile_major[0][:, :], DIGIT * n_pass, RADIX - 1,
                                               ALU.logical_shift_right, ALU.bitwise_and))
                        link(dve.tensor_copy(digit[:, :], digit_i[:, :]))
                        link(dve.tensor_tensor(onehot[:, :].rearrange("p (t r) -> p t r", r=RADIX),
                                               digit[:, :].unsqueeze(2).broadcast_to([P, ET, RADIX]),
                                               digit_iota[:, :].unsqueeze(1).broadcast_to([P, ET, RADIX]), ALU.is_equal))
                        dve.wait_ge(chain[1].sem, r0 + NCH)
                        link(dve.tensor_tensor_scan(counts[:, :], counts[:, :], counts[:, :], 0.0, ALU.add, ALU.bypass))
                        for k in range(NCH):
                            dve.wait_ge(chain[2].sem, chain[2].base + k + 1)
                            bank = work[:, (3 + k % 3) * 512:(4 + k % 3) * 512]
                            dve.tensor_tensor(place[:, k * 512:(k + 1) * 512].rearrange("p (t r) -> p t r", r=RADIX),
                                              bank.rearrange("p (t r) -> p t r", r=RADIX),
                                              counts[:, :].rearrange("p (r t) -> p t r", r=RADIX)[:, k * TPC:(k + 1) * TPC, :],
                                              ALU.add).then_inc(rank_made.sem, 1)
                        dve.wait_ge(rank_made.sem, m0 + NCH)
                        link(dve.tensor_tensor(place[:, :], place[:, :], onehot[:, :], ALU.mult))
                        link(dve.tensor_reduce(rank[:, :], place[:, :].rearrange("p (t r) -> p t r", r=RADIX), AX, ALU.add))
                        link(dve.tensor_copy(rank_i[0][:, :], rank[:, :]))
                        if last_pass:
                            link(dve.tensor_copy(edge_rank[:, :], rank_i[0][:, :]))
                        else:
                            link(dve.tensor_scalar(rank_i[1][:, :], rank_i[0][:, :], P - 1, J.bit_length() - 1, ALU.bitwise_and, ALU.logical_shift_left))
                            link(dve.tensor_scalar(rank_i[2][:, :], rank_i[0][:, :], P.bit_length() - 1, J - 1, ALU.logical_shift_right, ALU.bitwise_and))
                            link(dve.tensor_tensor(rank_i[1][:, :], rank_i[1][:, :], rank_i[2][:, :], ALU.bitwise_or))
                            link(dve.tensor_scalar(rank_i[2][:, :], rank_i[0][:, :], BLK.bit_length() - 1, BLK.bit_length() - 1, ALU.logical_shift_right, ALU.logical_shift_left))
                            link(dve.tensor_tensor(edge_rank[:, :], rank_i[1][:, :], rank_i[2][:, :], ALU.bitwise_or))
                        step_total[0] = step[0]

                    onehot_step = s0 + (6 if n_pass == 0 else 4)

                    @block.tensor
                    def _(pe):
                        pe.wait_ge(setup_step.sem, onehot_step)
                        for k in range(NCH):
                            if k >= 3:
                                pe.wait_ge(chain[1].sem, r0 + k - 2)
                            pe.matmul(work[:, (k % 3) * 512:(k % 3 + 1) * 512], ones_bf[:, :], onehot[:, k * 512:(k + 1) * 512],
                                      start=True, stop=True).then_inc(chain[0].sem, 1)
                        for k in range(NCH):
                            if k >= 3:
                                pe.wait_ge(rank_made.sem, m0 + k - 2)
                            pe.matmul(work[:, (3 + k % 3) * 512:(4 + k % 3) * 512], earlier[:, :], onehot[:, k * 512:(k + 1) * 512],
                                      start=True, stop=True).then_inc(chain[2].sem, 1)

                    @block.scalar
                    def _(act):
                        if n_pass == 1 or PASSES == 1:
                            load_weights(act)
                        for k in range(NCH):
                            act.wait_ge(chain[0].sem, c0 + k + 1)
                            act.activation(counts[:, :].rearrange("p (r t) -> p t r", r=RADIX)[:, k * TPC:(k + 1) * TPC, :],
                                           work[:, (k % 3) * 512:(k % 3 + 1) * 512].rearrange("p (t r) -> p t r", r=RADIX),
                                           ACT.Copy).then_inc(chain[1].sem, 1)

                    n_links = 7 + (2 if n_pass == 0 else 0) + 2 + (1 if last_pass else 5)
                    rank_step = s0 + (6 if n_pass == 0 else 4) + 1 + 3 + (1 if last_pass else 5)

                    @block.gpsimd
                    def _(pool):
                        if n_pass == 0:
                            pool.iota(iota_again[:, :], pattern=[[BLK, EB], [1, J]], base=0, channel_multiplier=J).then_inc(setup_edge.sem, 1)
                            pool.iota(digit_iota[:, :], pattern=[[1, RADIX]], base=0, channel_multiplier=0,
                                      allow_small_or_imprecise_dtypes=True).then_inc(setup_edge.sem, 1)
                            pool.memset(ones_bf[:, :], 1.0).then_inc(setup_edge.sem, 1)
                            pool.memset(earlier[:, :], 0.0).then_inc(setup_edge0.sem, 1)
                            pool.wait_ge(setup_edge0.sem, 1)
                            pool.affine_select(out=earlier[:, :], in_=earlier[:, :], compare_op=ALU.is_gt, fill=-1.0,
                                               base=0, pattern=[[1, P]], channel_multiplier=-1).then_inc(setup_edge.sem, 1)
                        pool.wait_ge(setup_step.sem, rank_step)
                        if not last_pass:
                            scatter_to_ranks(pool, sorting[n_pass % 2], edge_rank, rec_i)
                assert step_total[0] == rank_step, (step_total[0], rank_step)
                setup_step.base = step_total[0]
                setup_dma.base += 16
                chain[0].base += NCH
                chain[1].base += NCH
                chain[2].base += NCH
                rank_made.base += NCH

        scale_weights()

        def beside_first_nodes(pool):
            scatter_to_ranks(pool, sorting[(PASSES - 1) % 2], edge_rank, rec_i)
            read_slots(pool, src_clamped, link_idx)
            read_slots(pool, dst_clamped, home_idx)

        def links_and_sorted_list():
            with ExitStack() as c:
                slot_f = sb("slot_f", [P, ET], f32, c)
                home_f = sb("home_f", [P, ET], f32, c)
                key_lin = sb("key_lin", [P, EB, J], i32, c)
                with nc.Block() as block:
                    d0, s0 = setup_dma.base, setup_step.base

                    @block.sync
                    def _(sp):
                        sp.dma_start(rec_i[:, :, :, :], sorting[(PASSES - 1) % 2].rearrange("(b p j) t -> p b (j t)", p=P, j=J)).then_inc(setup_dma.sem, 16)
                        sp.wait_ge(setup_step.sem, s0 + 4)
                        sp.dma_start(cols_bj(key_pad[J:J + EP]), key_lin[:, :, :]).then_inc(setup_dma.sem, 16)
                        sp.wait_ge(setup_dma.sem, d0 + 32)

                    @block.vector
                    def _(dve):
                        dve.tensor_scalar(slot_f[:, :], link_idx[:, :], 2.0, 1.0, ALU.mult, ALU.add).then_inc(setup_step.sem, 1)
                        dve.tensor_scalar(home_f[:, :], home_idx[:, :], 2.0, 1.0, ALU.mult, ALU.add).then_inc(setup_step.sem, 1)
                        dve.wait_ge(setup_dma.sem, d0 + 16)
                        dve.tensor_copy(key_lin[:, :, :], rec_i[:, :, :, 0]).then_inc(setup_step.sem, 1)
                        dve.tensor_copy(sorted_edge[:, :], rec_i[:, :, :, 1].rearrange("p b j -> p (b j)")).then_inc(setup_step.sem, 1)
                        dve.wait_ge(setup_step.sem, s0 + 4)
                        dve.tensor_copy(link_idx[:, :], slot_f[:, :]).then_inc(setup_step.sem, 1)
                        dve.tensor_copy(home_idx[:, :], home_f[:, :]).then_inc(setup_step.sem, 1)
                        dve.wait_ge(setup_step.sem, s0 + 6)
                setup_dma.base += 32
                setup_step.base += 6

        def lane_tiles(name, lanes, width=BLK):
            return [sb(f"{name}{k}", [P, width]) for k in range(lanes)]

        W = J * D
        rows_in = lane_tiles("rows_in", EL)
        centered = lane_tiles("centered", EL)
        squares = lane_tiles("squares", EL)
        feat = lane_tiles("feat", EL)
        feat_out = lane_tiles("feat_out", EL)
        rows_out = lane_tiles("rows_out", EL)
        resid = lane_tiles("resid", EL)
        masked = lane_tiles("masked", DL, J * (D + 1))
        stats = lane_tiles("stats", DL, 4 * 2 * J)
        agg = lane_tiles("agg", EL, BLK + 1)
        mean_agg = lane_tiles("mean_agg", EL)
        flags = lane_tiles("flags", EL)
        inverse = lane_tiles("inverse", EL)
        edge_in = lane_tiles("edge_in", EL)
        edge_rows = resid
        record_rows = mean_agg
        running_max = agg
        messages = centered

        extra = []

        class Seats:
            kinds = dict(rows_in=rows_in, centered=centered, squares=squares, feat=feat, feat_out=feat_out,
                         rows_out=rows_out, resid=resid)

            def __init__(self, edge_lanes=0):
                def halves(tiles):
                    return [tile[:, h * W:(h + 1) * W] for tile in tiles for h in range(2)]

                spare = {0: [], 2: halves([agg[2], mean_agg[2], flags[2], inverse[2], edge_in[2]]),
                         3: extra + [zeros[:, :]]}[edge_lanes]
                spare += [tile[:, 0:W] for tile in masked[0 if edge_lanes == 3 else 2:DL]]
                self.banks = [work[:, k * 512:(k + 1) * 512] for k in range(DL)]
                self.first, self.lanes, moved = {0: (0, DL, ()), 2: (2, 4, (2, 3)), 3: (3, 2, (3, 4))}[edge_lanes]
                self.edge_lanes = edge_lanes
                self.tiles = {}
                for kind, tiles in self.kinds.items():
                    views = [tiles[k // 2][:, (k % 2) * W:(k % 2 + 1) * W] for k in range(DL)]
                    for lane in moved:
                        views[lane] = spare.pop(0)
                    self.tiles[kind] = views
                for lane, bank in zip(moved, (gram_nodes, gram_edges)):
                    self.banks[lane] = bank[:, :]

            def tile(self, kind, lane):
                return self.tiles[kind][lane]

        assert DL == 2 * EL and EL == 3
        moments = squares[0][0:D, 0:D + 1]
        moments_edges = squares[0][0:D, 2 * D:3 * D + 1]
        w1_moments = squares[0][0:D, 4 * D:4 * D + H]
        coef = squares[1][:, 0:8]

        class Steps:

            def __init__(self, names, lanes, blocks, loads=0, more=0, stores=1, gathers=0, first_lane=0, first_block=0):
                self.names, self.K, self.lanes = names, len(names), lanes
                self.first_lane, self.first_block = first_lane, first_block
                self.rounds = (blocks - 1) // lanes
                self.rest = blocks - self.rounds * lanes
                self.per = dict(loaded=16 * loads, more=16 * more, stored=16 * stores, gathered=16 * gathers)
                self.base = [s.base for s in chain]
                self.at = {k: [s.base for s in sems] for k, sems in lane_sems.items()}

            def after(self, lane, i, name):
                return i * self.K + (self.base[lane] + self.names.index(name) + 1)

            def start(self, lane, i):
                return i * self.K + self.base[lane]

            def dma(self, what, lane, i, rounds=1):
                return i * self.per[what] + (self.at[what][lane] + rounds * self.per[what])

            def block(self, lane, i):
                return i * self.lanes + (self.first_block + lane - self.first_lane)

            def blocks_of(self, lane):
                return self.rounds + (lane - self.first_lane < self.rest)

            def all_lanes(self):
                return range(self.first_lane, self.first_lane + self.lanes)

            def round_in_order(self, body, i):
                if isinstance(i, int) and i >= self.rounds:
                    if i == self.rounds:
                        body(i, self.all_lanes()[:self.rest])
                else:
                    body(i, self.all_lanes())

            def slot_of_round(self, body, i, slot):
                slots = self.names + ["end"]
                T = len(slots)

                def at(step):
                    due = []
                    for lane in self.all_lanes():
                        late = (lane - self.first_lane) * T // self.lanes
                        if (slots.index(step) + late) % T == slot:
                            k = i if slot >= late else i - 1
                            if not isinstance(k, int) or 0 <= k < self.blocks_of(lane):
                                due.append((k, lane))
                    return due
                body(at)

            def run_in_order(self, engine, body, part=None):
                pace = part.pace if part else 1

                def turn(n):
                    if part:
                        part.S.round_in_order(lambda i, lanes: part.sync(engine, i, lanes), n)
                    for k in range(pace):
                        self.round_in_order(body, n * pace + k)
                    if part:
                        part.S.round_in_order(lambda i, lanes: part.sync_late(engine, i, lanes), n)

                full = min(self.rounds // pace, part.S.rounds) if part else self.rounds
                if full > 1:
                    turn(0)
                    with engine.Fori(1, full) as n:
                        turn(n)
                for n in range(full if full > 1 else 0, max(self.rounds // pace, part.S.rounds if part else 0) + 1):
                    turn(n)

            def run(self, engine, body, part=None, part_body=None):
                pace = part.pace if part else 1
                T = len(self.names) + 1

                def turn(n):
                    given = 0
                    for k in range(pace):
                        for slot in range(T):
                            self.slot_of_round(body, n * pace + k, slot)
                            if part:
                                T_part = len(part.S.names) + 1
                                while given * pace * T < (k * T + slot + 1) * T_part:
                                    part.S.slot_of_round(part_body, n, given)
                                    given += 1

                full = min(self.rounds // pace, part.S.rounds) if part else self.rounds
                turn(0)
                if full > 1:
                    with engine.Fori(1, full) as n:
                        turn(n)
                for n in range(max(full, 1), max((self.rounds + 1) // pace, part.S.rounds + 1 if part else 0) + 1):
                    turn(n)

            def close(self):
                for k in self.all_lanes():
                    n = self.blocks_of(k)
                    chain[k].base += n * self.K
                    for what, sems in lane_sems.items():
                        if k < len(sems):
                            sems[k].base += n * self.per[what]

        more_loaded = [counted(f"lane{k}_more_loaded") for k in range(DL)]
        lane_sems = dict(loaded=loaded, more=more_loaded, stored=stored, gathered=gathered)
        gather_ready = [counted(f"lane{k}_gather_indices") for k in range(EL)]
        scattered = [counted(f"lane{k}_scattered") for k in range(EL)]
        scatter_ready = [counted(f"lane{k}_scatter_indices") for k in range(EL)]
        scatter_done = [counted(f"lane{k}_scatter_done") for k in range(EL)]
        resid_saved = [counted(f"lane{k}_residual_saved") for k in range(EL)]

        LN = ["ln_sum", "ln_center", "ln_square", "ln_var", "ln_root", "ln_inverse", "ln_out"]

        def ln_vector(dve, S, at, ready, src, centered, squares, T, tag=""):
            def x(lane):
                return src[lane][:, 0:T * D].rearrange("p (t d) -> p t d", d=D)

            def c(lane):
                return centered[lane][:, 0:T * D].rearrange("p (t d) -> p t d", d=D)

            for i, lane in at(tag + "ln_sum"):
                ready(i, lane)
                dve.tensor_reduce(stats[lane][:, 0:T], x(lane), AX, ALU.add).then_inc(chain[lane].sem, 1)
            for i, lane in at(tag + "ln_center"):
                dve.wait_ge(chain[lane].sem, S.after(lane, i, tag + "ln_sum"))
                dve.scalar_tensor_tensor(c(lane), stats[lane][:, 0:T].unsqueeze(2).broadcast_to([P, T, D]), -1.0 / D, x(lane),
                                         ALU.mult, ALU.add).then_inc(chain[lane].sem, 1)
            for i, lane in at(tag + "ln_var"):
                dve.wait_ge(chain[lane].sem, S.after(lane, i, tag + "ln_square"))
                dve.tensor_reduce(stats[lane][:, 16:16 + T], squares[lane][:, 0:T * D].rearrange("p (t d) -> p t d", d=D), AX,
                                  ALU.add).then_inc(chain[lane].sem, 1)
            for i, lane in at(tag + "ln_inverse"):
                dve.wait_ge(chain[lane].sem, S.after(lane, i, tag + "ln_root"))
                dve.reciprocal(stats[lane][:, 32:32 + T], stats[lane][:, 48:48 + T]).then_inc(chain[lane].sem, 1)
            for i, lane in at(tag + "ln_out"):
                dve.wait_ge(chain[lane].sem, S.after(lane, i, tag + "ln_inverse"))
                dve.scalar_tensor_tensor(c(lane), c(lane), 0.0, stats[lane][:, 32:32 + T].unsqueeze(2).broadcast_to([P, T, D]),
                                         ALU.max, ALU.mult).then_inc(chain[lane].sem, 1)

        def ln_scalar(act, S, at, centered, squares, T, tag=""):
            for i, lane in at(tag + "ln_square"):
                act.wait_ge(chain[lane].sem, S.after(lane, i, tag + "ln_center"))
                act.activation(squares[lane][:, 0:T * D], centered[lane][:, 0:T * D], ACT.Square).then_inc(chain[lane].sem, 1)
            for i, lane in at(tag + "ln_root"):
                act.wait_ge(chain[lane].sem, S.after(lane, i, tag + "ln_var"))
                act.activation(stats[lane][:, 48:48 + T], stats[lane][:, 16:16 + T], ACT.Sqrt, bias=eps_ln[:, :],
                               scale=1.0 / D).then_inc(chain[lane].sem, 1)

        def edge_psum(lane):
            return work[:, lane * 1024:(lane + 1) * 1024]

        def tiles_of(tile, j):
            return tile.rearrange("f (p j) -> f j p", j=J)[:, j, :]

        def in_order(tile):
            return tile.rearrange("f (p j) -> f p j", j=J)

        def by_tile(bank):
            return bank.rearrange("f (j p) -> f p j", p=P)

        cleared = agg + mean_agg + feat_out + masked + resid + edge_in
        lane_counts = chain + loaded + more_loaded + stored + scatter_done + scatter_ready + gather_ready + resid_saved
        with nc.Block() as block:
            @block.vector
            def _(dve):
                for tile in cleared:
                    dve.memset(tile[:, :], 0.0).then_inc(setup_step.sem, 1)
                dve.wait_ge(setup_step.sem, setup_step.base + len(cleared))

            @block.gpsimd
            def _(pool):
                for c in lane_counts:
                    pool.sem_inc(c.sem, 64)
        setup_step.base += len(cleared)
        for c in lane_counts:
            c.base += 64

        def edge_phase(kind, l, source, tin, tout, ln=False, add_resid=False, beside=None):
            EL = beside.seats.edge_lanes if beside else 3
            names = list(LN) if ln else []
            names += ["t_in", "feat"]
            if kind == "gnn":
                names += ["edge_mm", "edge_act"] if l > 0 else ["edge_t", "edge_feat"]
                names += ["edge_pair", "msg_mm", "msg_act"]
            if kind in ("sage", "gnn"):
                names += ["scan", "mean"]
            if kind in ("sage", "gnn", "proj"):
                names += ["mm", "act", "t_out"]
                if kind == "gnn":
                    names += ["l2_square", "l2_sum", "l2_root", "l2_floor", "l2_inverse"]
                names += ["rows"]
                if kind == "gnn" and add_resid:
                    names += ["add_resid"]
            if kind == "gin":
                names += ["scan", "z", "z_rows", "z_masked", "z_mask", "gram"]
            if kind == "qkv":
                names += ["qk_mm", "q_bias", "k_bias", "v_mm", "v_bias", "q_times_k", "dot", "score", "max_score"]
            last = names[-1]
            scans = kind in ("sage", "gnn", "gin")
            homes = source == "links" and kind in ("qkv", "gnn")
            gathers = {"nodes": 2 * J, "attention": 2 * J, "links": J * (1 + homes), "rows": 0}[source]
            save_resid = ln
            n_more = 2 * (kind in ("sage", "gnn")) + (kind == "gin") + add_resid + (kind == "gnn")
            n_load = int(source in ("links", "rows"))
            n_store = {"sage": 1, "proj": 1, "qkv": 1, "gin": 2, "gnn": 1 + (l < 2)}[kind]
            S = Steps(names, EL, EB, loads=n_load, more=n_more, stores=n_store, gathers=gathers)
            stage0 = [g.base for g in gather_ready]
            saved0 = [g.base for g in resid_saved]
            nodes = {"nodes": t["x"], "attention": attn_nodes, "links": None, "rows": None}[source]
            slots = tin.rearrange("e (h d) -> (e h) d", h=2) if source == "links" else None
            reads_rows = "ln_center" if ln else "t_in"
            relu = ACT.Relu if kind != "proj" else ACT.Identity
            w = {"sage": sage, "gnn": gnn, "proj": [dict(own=w_o, agg=None, bias=b_o)], "gin": gin, "qkv": [None] * 3}[kind]
            w = w[0] if kind == "proj" else w[l]

            with nc.Block() as block:
                @block.sync
                def _(sp):
                    if kind == "gnn" and l == 0:
                        pass

                    def body(i, lanes):
                        for lane in lanes:
                            b = i * EL + lane
                            if n_load:
                                hold(sp, chain[lane].sem, S.after(lane, i - 1, reads_rows))
                                if save_resid:
                                    hold(sp, resid_saved[lane].sem, i * 16 + saved0[lane])
                                sp.dma_start(rows_in[lane][:, :].rearrange("p (j d) -> p j d", j=J), rows(tin, b)).then_inc(loaded[lane].sem, 16)
                        for lane in lanes:
                            b = i * EL + lane
                            if add_resid or kind == "gnn":
                                hold(sp, chain[lane].sem, S.start(lane, i))
                            elif scans:
                                hold(sp, chain[lane].sem, S.after(lane, i - 1, "mean" if kind == "sage" else "scan"))
                            if kind == "gnn" and l > 0:
                                hold(sp, stored[lane].sem, S.dma("stored", lane, i, rounds=0))
                            if kind in ("sage", "gnn", "gin"):
                                sp.dma_start(flags[lane][0:D, :], same_dst[ds(b * BLK, BLK)].partition_broadcast(D)).then_inc(more_loaded[lane].sem, 16)
                            if kind in ("sage", "gnn"):
                                sp.dma_start(inverse[lane][0:D, :], inv_deg[ds(b * BLK, BLK)].partition_broadcast(D)).then_inc(more_loaded[lane].sem, 16)
                            if add_resid:
                                sp.dma_start(resid[lane][:, :].rearrange("p (j d) -> p j d", j=J), rows(sd_resid, b)).then_inc(more_loaded[lane].sem, 16)
                            if kind == "gnn":
                                if l > 0:
                                    sp.dma_start(edge_in[lane][D:P, :], edge_state[ds(b, 1), :, :].rearrange("o f e -> (o f) e")).then_inc(more_loaded[lane].sem, 16)
                                elif isinstance(i, int) and i * EL + lane == EB - 1:
                                    n_last = (E - (EB - 1) * BLK) // J
                                    sp.dma_start(edge_rows[lane][0:n_last, :].rearrange("p (j d) -> p j d", j=J)[:, :, D:P],
                                                 t["edge_attr_64"][(EB - 1) * BLK:E, :].rearrange("(p j) d -> p j d", j=J)).then_inc(more_loaded[lane].sem, 16)
                                else:
                                    sp.dma_start(edge_rows[lane][:, :].rearrange("p (j d) -> p j d", j=J)[:, :, D:P],
                                                 rows(t["edge_attr_64"], b)).then_inc(more_loaded[lane].sem, 16)
                    S.run_in_order(sp, body, beside)

                @block.gpsimd
                def _(pool):
                    def body(i, lanes):
                        for lane in lanes:
                            b = i * EL + lane
                            if source == "rows":
                                continue
                            if source == "links":
                                tables = [(link_idx, 0)] + [(home_idx, D)] * homes
                                hold(pool, loaded[lane].sem, S.dma("loaded", lane, i))
                            else:
                                tables = [(src_clamped, 0), (dst_clamped, D)]
                                hold(pool, chain[lane].sem, S.after(lane, i - 1, reads_rows))
                                if save_resid:
                                    hold(pool, resid_saved[lane].sem, i * 16 + saved0[lane])
                            hold(pool, gathered[lane].sem, S.dma("gathered", lane, i, rounds=0))
                            for k, (table, _) in enumerate(tables):
                                pool.tensor_copy(idx_stage[lane][:, k * J:(k + 1) * J], table[:, ds(b * J, J)]).then_inc(gather_ready[lane].sem, 1)
                            hold(pool, gather_ready[lane].sem, i * len(tables) + (stage0[lane] + len(tables)))
                            for k, (_, at) in enumerate(tables):
                                for j in range(J):
                                    pool.indirect_dma_start(
                                        rows_in[lane][:, j * P + at:j * P + at + D], None, slots if source == "links" else nodes[:, :],
                                        bass.IndirectOffsetOnAxis(idx_stage[lane][:, k * J + j:k * J + j + 1], 0),
                                        bounds_check=(2 * EP - 1) if source == "links" else N - 1,
                                        oob_is_err=False).then_inc(gathered[lane].sem, 16)
                    S.run_in_order(pool, body)

                def rows_ready(engine, lane, i):
                    if gathers:
                        engine.wait_ge(gathered[lane].sem, S.dma("gathered", lane, i))
                    else:
                        engine.wait_ge(loaded[lane].sem, S.dma("loaded", lane, i))

                @block.tensor
                def _(pe):
                    if kind == "gin":
                        pe.matmul(gram_edges[0:D, 0:D + 1], zeros[:, 0:D], zeros[:, 0:D + 1], start=True, stop=True)

                    def body(at):
                        for i, lane in at("t_in"):
                            A = edge_psum(lane)
                            if ln:
                                pe.wait_ge(chain[lane].sem, S.after(lane, i, "ln_out"))
                            else:
                                pe.wait_ge(chain[lane].sem, S.start(lane, i))
                                rows_ready(pe, lane, i)
                            src = centered[lane] if ln else rows_in[lane]
                            for j in range(J):
                                op = pe.transpose(A[:, j * P:(j + 1) * P], src[:, j * P:(j + 1) * P], ident[:, :])
                            op.then_inc(chain[lane].sem, 1)
                        if kind == "gnn":
                            for i, lane in at("edge_mm" if l else "edge_t"):
                                A = edge_psum(lane)
                                pe.wait_ge(chain[lane].sem, S.after(lane, i, "feat"))
                                pe.wait_ge(more_loaded[lane].sem, S.dma("more", lane, i))
                                if l == 0:
                                    for j in range(J):
                                        op = pe.transpose(A[:, j * P:(j + 1) * P], edge_rows[lane][:, j * P:(j + 1) * P], ident[:, :])
                                else:
                                    for h in range(2):
                                        c = slice(h * 512, (h + 1) * 512)
                                        pe.matmul(A[:, c], w["edge_nodes"][:, :], feat[lane][:, c], start=True, stop=False)
                                        op = pe.matmul(A[:, c], w["edge_own"][:, :], edge_in[lane][:, c], start=False, stop=True)
                                op.then_inc(chain[lane].sem, 1)
                            for i, lane in at("msg_mm"):
                                A = edge_psum(lane)
                                pe.wait_ge(chain[lane].sem, S.after(lane, i, "edge_pair"))
                                for h in range(2):
                                    c = slice(h * 512, (h + 1) * 512)
                                    op = pe.matmul(A[0:D, c], w["msg"][:, :], edge_in[lane][:, c], start=True, stop=True)
                                op.then_inc(chain[lane].sem, 1)
                        if kind in ("sage", "gnn", "proj"):
                            for i, lane in at("mm"):
                                A = edge_psum(lane)
                                pe.wait_ge(chain[lane].sem, S.after(lane, i, "feat" if kind == "proj" else "mean"))
                                for h in range(2):
                                    c = slice(h * 512, (h + 1) * 512)
                                    op = pe.matmul(A[:, c], w["own"][:, :], feat[lane][:, c], start=True, stop=kind == "proj")
                                    if kind != "proj":
                                        op = pe.matmul(A[:, c], w["agg"][0:D, :], mean_agg[lane][0:D, c], start=False, stop=True)
                                op.then_inc(chain[lane].sem, 1)
                            for i, lane in at("t_out"):
                                A = edge_psum(lane)
                                pe.wait_ge(chain[lane].sem, S.after(lane, i, "act"))
                                for j in range(J):
                                    op = pe.transpose(A[:, j * P:(j + 1) * P], tiles_of(feat_out[lane][:, :], j), ident[:, :])
                                op.then_inc(chain[lane].sem, 1)
                        if kind == "gin":
                            for i, lane in at("z"):
                                A = edge_psum(lane)
                                pe.wait_ge(chain[lane].sem, S.after(lane, i, "scan"))
                                for j in range(J):
                                    c = slice(j * D, (j + 1) * D)
                                    pe.matmul(A[:, c], tiles_of(feat[lane][:, :], j), w["keep_ident"][:, :], start=True, stop=False)
                                    op = pe.matmul(A[:, c], tiles_of(agg[lane][0:D, 0:BLK], j), ident[0:D, 0:D], start=False, stop=True)
                                op.then_inc(chain[lane].sem, 1)
                            for i, lane in at("gram"):
                                pe.wait_ge(chain[lane].sem, S.after(lane, i, "z_mask"))
                                zm = masked[lane][:, :].rearrange("p (j d) -> p j d", j=J)
                                for j in range(J):
                                    op = pe.matmul(gram_edges[0:D, 0:D + 1], squares[lane][:, j * D:(j + 1) * D], zm[:, j, :],
                                                   start=False, stop=False, skip_group_check=True)
                                op.then_inc(chain[lane].sem, 1)
                        if kind == "qkv":
                            for i, lane in at("qk_mm"):
                                A = edge_psum(lane)
                                pe.wait_ge(chain[lane].sem, S.after(lane, i, "feat"))
                                for j in range(J):
                                    pe.matmul(A[:, j * D:(j + 1) * D], tiles_of(feat[lane][0:D, :], j), w_qkv[0:D, 0:D], start=True, stop=True)
                                for j in range(J):
                                    op = pe.matmul(A[:, W + j * D:W + (j + 1) * D], tiles_of(feat[lane][D:P, :], j), w_qkv[D:P, 0:D], start=True, stop=True)
                                op.then_inc(chain[lane].sem, 1)
                            for i, lane in at("v_mm"):
                                A = edge_psum(lane)
                                pe.wait_ge(chain[lane].sem, S.after(lane, i, "k_bias"))
                                for j in range(J):
                                    op = pe.matmul(A[:, j * D:(j + 1) * D], tiles_of(feat[lane][D:P, :], j), w_qkv[D:P, D:2 * D], start=True, stop=True)
                                op.then_inc(chain[lane].sem, 1)
                    S.run(pe, body, beside, beside and (lambda at: beside.tensor(pe, at)))

                @block.scalar
                def _(act):
                    def body(at):
                        if save_resid:
                            for i, lane in at("ln_sum"):
                                b = i * EL + lane
                                rows_ready(act, lane, i)
                                act.dma_start(rows(sd_resid, b), rows_in[lane][:, :].rearrange("p (j d) -> p j d", j=J)).then_inc(resid_saved[lane].sem, 16)
                        if ln:
                            ln_scalar(act, S, at, centered, squares, 2 * J)
                        for i, lane in at("feat"):
                            A = edge_psum(lane)
                            act.wait_ge(chain[lane].sem, S.after(lane, i, "t_in"))
                            if kind == "gin":
                                act.wait_ge(stored[lane].sem, S.dma("stored", lane, i, rounds=0))
                            act.activation(in_order(feat[lane][:, :]), by_tile(A), ACT.Copy).then_inc(chain[lane].sem, 1)
                        if kind == "gnn":
                            for i, lane in at("edge_act" if l else "edge_feat"):
                                A = edge_psum(lane)
                                if l == 0:
                                    act.wait_ge(chain[lane].sem, S.after(lane, i, "edge_t"))
                                    act.wait_ge(stored[lane].sem, S.dma("stored", lane, i, rounds=0))
                                    act.activation(in_order(edge_in[lane][D:P, :]), by_tile(A)[D:P], ACT.Copy).then_inc(chain[lane].sem, 1)
                                else:
                                    act.wait_ge(chain[lane].sem, S.after(lane, i, "edge_mm"))
                                    act.activation(edge_in[lane][D:P, :], A[D:P, :], ACT.Relu, bias=w["edge_b"][D:P, :]).then_inc(chain[lane].sem, 1)
                            for i, lane in at("edge_pair"):
                                act.wait_ge(chain[lane].sem, S.after(lane, i, "edge_act" if l else "edge_feat"))
                                act.activation(edge_in[lane][0:D, :], feat[lane][0:D, :], ACT.Copy).then_inc(chain[lane].sem, 1)
                            for i, lane in at("msg_mm"):
                                b = i * EL + lane
                                if l < 2:
                                    act.dma_start(edge_state[ds(b, 1), :, :].rearrange("o f e -> (o f) e"), edge_in[lane][D:P, :]).then_inc(stored[lane].sem, 16)
                            for i, lane in at("msg_act"):
                                A = edge_psum(lane)
                                act.wait_ge(chain[lane].sem, S.after(lane, i, "msg_mm"))
                                act.activation(messages[lane][0:D, :], A[0:D, :], ACT.Relu, bias=w["msg_b"][0:D, :]).then_inc(chain[lane].sem, 1)
                        if kind in ("sage", "gnn", "proj"):
                            for i, lane in at("act"):
                                A = edge_psum(lane)
                                act.wait_ge(chain[lane].sem, S.after(lane, i, "mm"))
                                act.activation(feat_out[lane][:, :], A, relu, bias=w["bias"][:, :]).then_inc(chain[lane].sem, 1)
                            if kind == "gnn":
                                for i, lane in at("l2_square"):
                                    A = edge_psum(lane)
                                    act.wait_ge(chain[lane].sem, S.after(lane, i, "t_out"))
                                    act.activation(squares[lane][:, :], A, ACT.Square).then_inc(chain[lane].sem, 1)
                                for i, lane in at("l2_root"):
                                    act.wait_ge(chain[lane].sem, S.after(lane, i, "l2_sum"))
                                    act.activation(stats[lane][:, 16:32], stats[lane][:, 0:16], ACT.Sqrt).then_inc(chain[lane].sem, 1)
                            for i, lane in at("end"):
                                b = i * EL + lane
                                act.wait_ge(chain[lane].sem, S.after(lane, i, last))
                                act.dma_start(rows(tout, b), rows_out[lane][:, :].rearrange("p (j d) -> p j d", j=J)).then_inc(stored[lane].sem, 16)
                        if kind == "gin":
                            for i, lane in at("z"):
                                b = i * EL + lane
                                act.wait_ge(chain[lane].sem, S.after(lane, i, "scan"))
                                act.dma_start(gin_x[ds(b, 1), :, :].rearrange("o f e -> (o f) e"), feat[lane][:, :]).then_inc(stored[lane].sem, 16)
                                act.dma_start(gin_agg[ds(b, 1), :, :].rearrange("o f e -> (o f) e"), agg[lane][0:D, 0:BLK]).then_inc(stored[lane].sem, 16)
                        if kind == "qkv":
                            for i, lane in at("end"):
                                b = i * EL + lane
                                act.wait_ge(chain[lane].sem, S.after(lane, i, last))
                                act.dma_start(rows(records, b), record_rows[lane][:, 0:J * REC].rearrange("p (j d) -> p j d", j=J)).then_inc(stored[lane].sem, 16)
                    S.run(act, body, beside, beside and (lambda at: beside.scalar(act, at)))
                    if beside:
                        beside.stored_all(act)
                    for lane in range(EL):
                        n = S.blocks_of(lane)
                        act.wait_ge(stored[lane].sem, S.at["stored"][lane] + n * S.per["stored"])
                        if save_resid:
                            act.wait_ge(resid_saved[lane].sem, saved0[lane] + 16 * n)

                @block.vector
                def _(dve):
                    def body(at):
                        if ln:
                            def ready(i, lane):
                                dve.wait_ge(chain[lane].sem, S.start(lane, i))
                                rows_ready(dve, lane, i)

                            ln_vector(dve, S, at, ready, rows_in, centered, squares, 2 * J)
                        if scans:
                            for i, lane in at("scan"):
                                msg = messages[lane][0:D, :] if kind == "gnn" else feat[lane][0:D, :]
                                dve.wait_ge(chain[lane].sem, S.after(lane, i, "msg_act" if kind == "gnn" else "feat"))
                                dve.wait_ge(more_loaded[lane].sem, S.dma("more", lane, i))
                                if kind == "gin":
                                    dve.wait_ge(stored[lane].sem, S.dma("stored", lane, i, rounds=0))
                                if lane == 0:
                                    dve.wait_ge(chain[EL - 1].sem, S.after(EL - 1, i - 1, "scan"))
                                else:
                                    dve.wait_ge(chain[lane - 1].sem, S.after(lane - 1, i, "scan"))
                                before = agg[(lane - 1) % EL]
                                dve.tensor_tensor_scan(agg[lane][0:D, 0:BLK], flags[lane][0:D, :], msg, before[0:D, BLK - 1:BLK],
                                                       ALU.mult, ALU.add).then_inc(chain[lane].sem, 1)
                        if kind in ("sage", "gnn"):
                            for i, lane in at("mean"):
                                dve.wait_ge(chain[lane].sem, S.after(lane, i, "scan"))
                                dve.tensor_tensor(mean_agg[lane][0:D, 0:BLK], agg[lane][0:D, 0:BLK], inverse[lane][0:D, :], ALU.mult).then_inc(chain[lane].sem, 1)
                        if kind in ("sage", "proj"):
                            for i, lane in at("rows"):
                                A = edge_psum(lane)
                                dve.wait_ge(chain[lane].sem, S.after(lane, i, "t_out"))
                                dve.wait_ge(stored[lane].sem, S.dma("stored", lane, i, rounds=0))
                                if add_resid:
                                    dve.wait_ge(more_loaded[lane].sem, S.dma("more", lane, i))
                                    dve.tensor_tensor(rows_out[lane][:, :], A, resid[lane][:, :], ALU.add).then_inc(chain[lane].sem, 1)
                                else:
                                    dve.tensor_copy(rows_out[lane][:, :], A).then_inc(chain[lane].sem, 1)
                        if kind == "gnn":
                            for i, lane in at("l2_sum"):
                                A = edge_psum(lane)
                                st = stats[lane]
                                dve.wait_ge(chain[lane].sem, S.after(lane, i, "l2_square"))
                                dve.tensor_reduce(st[:, 0:16], squares[lane][:, :].rearrange("p (t d) -> p t d", d=D), AX, ALU.add).then_inc(chain[lane].sem, 1)
                            for i, lane in at("l2_floor"):
                                dve.wait_ge(chain[lane].sem, S.after(lane, i, "l2_root"))
                                dve.tensor_scalar(stats[lane][:, 32:48], stats[lane][:, 16:32], L2_EPS, None, ALU.max).then_inc(chain[lane].sem, 1)
                            for i, lane in at("l2_inverse"):
                                dve.wait_ge(chain[lane].sem, S.after(lane, i, "l2_floor"))
                                dve.reciprocal(stats[lane][:, 48:64], stats[lane][:, 32:48]).then_inc(chain[lane].sem, 1)
                            for i, lane in at("rows"):
                                A = edge_psum(lane)
                                dve.wait_ge(chain[lane].sem, S.after(lane, i, "l2_inverse"))
                                dve.wait_ge(stored[lane].sem, S.dma("stored", lane, i, rounds=0) + 16 * (l < 2))
                                dve.tensor_tensor(rows_out[lane][:, :].rearrange("p (t d) -> p t d", d=D), A.rearrange("p (t d) -> p t d", d=D),
                                                  stats[lane][:, 48:64].unsqueeze(2).broadcast_to([P, 2 * J, D]), ALU.mult).then_inc(chain[lane].sem, 1)
                            if add_resid:
                                for i, lane in at("add_resid"):
                                    dve.wait_ge(chain[lane].sem, S.after(lane, i, "rows"))
                                    dve.tensor_tensor(rows_out[lane][:, :], rows_out[lane][:, :], resid[lane][:, :], ALU.add).then_inc(chain[lane].sem, 1)
                        if kind == "gin":
                            for i, lane in at("z_rows"):
                                dve.wait_ge(chain[lane].sem, S.after(lane, i, "z"))
                                dve.tensor_copy(squares[lane][:, 0:W], edge_psum(lane)[:, 0:W]).then_inc(chain[lane].sem, 1)
                            for i, lane in at("z_masked"):
                                zm = masked[lane][:, :].rearrange("p (j d) -> p j d", j=J)
                                mask = rep_mask[:, ds((i * EL + lane) * J, J)]
                                dve.wait_ge(chain[lane].sem, S.after(lane, i, "z_rows"))
                                dve.tensor_tensor(zm[:, :, 0:D], squares[lane][:, 0:W].rearrange("p (j d) -> p j d", j=J),
                                                  mask.unsqueeze(2).broadcast_to([P, J, D]), ALU.mult).then_inc(chain[lane].sem, 1)
                                dve.tensor_copy(zm[:, :, D], mask).then_inc(chain[lane].sem, 1)
                        if kind == "qkv":
                            def as_rows(v):
                                return v.rearrange("p (j d) -> p j d", j=J)

                            def bias_of(n):
                                return b_qkv[:, n, :].unsqueeze(1).broadcast_to([P, J, D])

                            def record(lane):
                                return record_rows[lane][:, 0:J * REC].rearrange("p (j d) -> p j d", j=J)

                            for i, lane in at("q_bias"):
                                A = edge_psum(lane)
                                q, k = squares[lane][:, 0:W], squares[lane][:, W:2 * W]
                                dve.wait_ge(chain[lane].sem, S.after(lane, i, "qk_mm"))
                                dve.tensor_tensor(as_rows(q), as_rows(A[:, 0:W]), bias_of(0), ALU.add).then_inc(chain[lane].sem, 1)
                                dve.tensor_tensor(as_rows(k), as_rows(A[:, W:2 * W]), bias_of(1), ALU.add).then_inc(chain[lane].sem, 1)
                            for i, lane in at("v_bias"):
                                dve.wait_ge(chain[lane].sem, S.after(lane, i, "v_mm"))
                                dve.wait_ge(stored[lane].sem, S.dma("stored", lane, i, rounds=0))
                                dve.tensor_tensor(record(lane)[:, :, 0:D], as_rows(edge_psum(lane)[:, 0:W]), bias_of(2), ALU.add).then_inc(chain[lane].sem, 1)
                            for i, lane in at("q_times_k"):
                                dve.wait_ge(chain[lane].sem, S.after(lane, i, "v_bias"))
                                dve.tensor_tensor(centered[lane][:, 0:W], squares[lane][:, 0:W], squares[lane][:, W:2 * W], ALU.mult).then_inc(chain[lane].sem, 1)
                            for i, lane in at("dot"):
                                dve.wait_ge(chain[lane].sem, S.after(lane, i, "q_times_k"))
                                dve.tensor_reduce(stats[lane][:, 0:J * HEADS], centered[lane][:, 0:W].rearrange("p (t d) -> p t d", d=HD), AX, ALU.add).then_inc(chain[lane].sem, 1)
                            for i, lane in at("score"):
                                dve.wait_ge(chain[lane].sem, S.after(lane, i, "dot"))
                                dve.tensor_scalar(record(lane)[:, :, D:D + HEADS], stats[lane][:, 0:J * HEADS].rearrange("p (j h) -> p j h", h=HEADS),
                                                  1.0 / float(np.sqrt(HD)), None, ALU.mult).then_inc(chain[lane].sem, 1)
                            for i, lane in at("max_score"):
                                dve.wait_ge(chain[lane].sem, S.after(lane, i, "score"))
                                dve.tensor_reduce(record(lane)[:, :, D + HEADS], record(lane)[:, :, D:D + HEADS], AX, ALU.max).then_inc(chain[lane].sem, 1)
                    S.run(dve, body, beside, beside and (lambda at: beside.vector(dve, at)))
            S.close()
            if beside:
                beside.S.close()
            for lane in range(EL):
                n = S.blocks_of(lane)
                if source != "rows":
                    gather_ready[lane].base += n * (1 if source == "links" and not homes else 2)
                if save_resid:
                    resid_saved[lane].base += 16 * n

        def gin_edge_phase(l, tout, add_resid):
            w = gin[l]
            S = Steps(["s_mm", "s_act", "d_mm", "d_act", "y_mm", "y_act", "t_out", "rows"], EL, EB,
                      loads=2 + add_resid, stores=1)
            with nc.Block() as block:
                @block.sync
                def _(sp):
                    def body(i, lanes):
                        for lane in lanes:
                            b = i * EL + lane
                            hold(sp, chain[lane].sem, S.start(lane, i))
                            sp.dma_start(rows_in[lane][:, :], gin_x[ds(b, 1), :, :].rearrange("o f e -> (o f) e")).then_inc(loaded[lane].sem, 16)
                            sp.dma_start(flags[lane][0:D, :], gin_agg[ds(b, 1), :, :].rearrange("o f e -> (o f) e")).then_inc(loaded[lane].sem, 16)
                            if add_resid:
                                sp.dma_start(resid[lane][:, :].rearrange("p (j d) -> p j d", j=J), rows(sd_resid, b)).then_inc(loaded[lane].sem, 16)
                    S.run_in_order(sp, body)

                @block.tensor
                def _(pe):
                    def body(at):
                        for i, lane in at("s_mm"):
                            A = edge_psum(lane)
                            pe.wait_ge(chain[lane].sem, S.start(lane, i))
                            pe.wait_ge(loaded[lane].sem, S.dma("loaded", lane, i))
                            for h in range(2):
                                c = slice(h * 512, (h + 1) * 512)
                                op = pe.matmul(A[:, c], w["w1_own"][0:D, :], rows_in[lane][0:D, c], start=True, stop=True)
                            op.then_inc(chain[lane].sem, 1)
                        for i, lane in at("d_mm"):
                            A = edge_psum(lane)
                            pe.wait_ge(chain[lane].sem, S.after(lane, i, "s_act"))
                            for h in range(2):
                                c = slice(h * 512, (h + 1) * 512)
                                pe.matmul(A[:, c], w["w1_dst"][:, :], rows_in[lane][:, c], start=True, stop=False)
                                op = pe.matmul(A[:, c], w["w1"][0:D, :], flags[lane][0:D, c], start=False, stop=True)
                            op.then_inc(chain[lane].sem, 1)
                        for i, lane in at("y_mm"):
                            A = edge_psum(lane)
                            pe.wait_ge(chain[lane].sem, S.after(lane, i, "d_act"))
                            for h in range(2):
                                c = slice(h * 512, (h + 1) * 512)
                                pe.matmul(A[:, c], w["w2_src"][:, :], centered[lane][:, c], start=True, stop=False)
                                op = pe.matmul(A[:, c], w["w2_dst"][:, :], squares[lane][:, c], start=False, stop=True)
                            op.then_inc(chain[lane].sem, 1)
                        for i, lane in at("t_out"):
                            A = edge_psum(lane)
                            pe.wait_ge(chain[lane].sem, S.after(lane, i, "y_act"))
                            for j in range(J):
                                op = pe.transpose(A[:, j * P:(j + 1) * P], tiles_of(feat_out[lane][:, :], j), ident[:, :])
                            op.then_inc(chain[lane].sem, 1)
                    S.run(pe, body)

                @block.scalar
                def _(act):
                    def body(at):
                        for mm, dest in (("s_mm", centered), ("d_mm", squares)):
                            for i, lane in at(mm.replace("mm", "act")):
                                A = edge_psum(lane)
                                act.wait_ge(chain[lane].sem, S.after(lane, i, mm))
                                act.activation(dest[lane][:, :], A, ACT.Relu, bias=w["shift"][:, :], scale=w["scale"][:, :]).then_inc(chain[lane].sem, 1)
                        for i, lane in at("y_act"):
                            A = edge_psum(lane)
                            act.wait_ge(chain[lane].sem, S.after(lane, i, "y_mm"))
                            act.activation(feat_out[lane][:, :], A, ACT.Identity, bias=w["b2"][:, :]).then_inc(chain[lane].sem, 1)
                        for i, lane in at("end"):
                            b = i * EL + lane
                            act.wait_ge(chain[lane].sem, S.after(lane, i, "rows"))
                            act.dma_start(rows(tout, b), rows_out[lane][:, :].rearrange("p (j d) -> p j d", j=J)).then_inc(stored[lane].sem, 16)
                    S.run(act, body)
                    for lane in range(EL):
                        act.wait_ge(stored[lane].sem, S.at["stored"][lane] + S.blocks_of(lane) * 16)

                @block.vector
                def _(dve):
                    def body(at):
                        for i, lane in at("rows"):
                            A = edge_psum(lane)
                            dve.wait_ge(chain[lane].sem, S.after(lane, i, "t_out"))
                            dve.wait_ge(stored[lane].sem, S.dma("stored", lane, i, rounds=0))
                            if add_resid:
                                dve.tensor_tensor(rows_out[lane][:, :], A, resid[lane][:, :], ALU.add).then_inc(chain[lane].sem, 1)
                            else:
                                dve.tensor_copy(rows_out[lane][:, :], A).then_inc(chain[lane].sem, 1)
                    S.run(dve, body)
            S.close()

        def attention_phase(beside=None):
            R72 = D + HEADS
            EL = beside.seats.edge_lanes if beside else 3
            S = Steps(["t_in", "feat", "max_mm", "carry", "run_max", "score_mm", "unit", "below_max", "max_step",
                       "max_step_neg", "weight", "rescale", "weighted", "sums", "t_out", "guard", "inverse", "rows"],
                      EL, EB, loads=0, more=1, stores=0, gathers=J)
            n0, done0, ready0 = ([c.base for c in cs] for cs in (scattered, scatter_done, scatter_ready))
            stage0 = [g.base for g in gather_ready]
            with nc.Block() as block:
                @block.sync
                def _(sp):
                    def body(i, lanes):
                        for lane in lanes:
                            b = i * EL + lane
                            hold(sp, chain[lane].sem, S.start(lane, i))
                            sp.dma_start(flags[lane][0:R72, :], neg_start[ds(b * BLK, BLK)].partition_broadcast(R72)).then_inc(more_loaded[lane].sem, 16)
                    S.run_in_order(sp, body, beside)

                @block.gpsimd
                def _(pool):
                    def gather(i, lanes):
                        for lane in lanes:
                            b = i * EL + lane
                            hold(pool, chain[lane].sem, S.after(lane, i - 1, "t_in"))
                            pool.tensor_copy(idx_stage[lane][:, 0:J], sorted_edge[:, ds(b * J, J)]).then_inc(gather_ready[lane].sem, 1)
                            hold(pool, gather_ready[lane].sem, i + (stage0[lane] + 1))
                            for j in range(J):
                                pool.indirect_dma_start(rows_in[lane][:, j * REC:(j + 1) * REC], None, records[:, :],
                                                        bass.IndirectOffsetOnAxis(idx_stage[lane][:, j:j + 1], 0),
                                                        bounds_check=EP - 1, oob_is_err=False).then_inc(gathered[lane].sem, 16)

                    def scatter(i, lanes):
                        for lane in lanes:
                            b = i * EL + lane
                            pool.tensor_copy(idx_stage[lane][:, J:2 * J], attn_out_idx[:, ds(b * J, J)]).then_inc(scatter_ready[lane].sem, 1)
                            hold(pool, scatter_ready[lane].sem, i + (ready0[lane] + 1))
                            hold(pool, chain[lane].sem, S.after(lane, i, "rows"))
                            for j in range(J):
                                pool.indirect_dma_start(attn_nodes[:, :], bass.IndirectOffsetOnAxis(idx_stage[lane][:, J + j:J + j + 1], 0),
                                                        rows_out[lane][:, j * D:(j + 1) * D], None,
                                                        bounds_check=N - 1, oob_is_err=False).then_inc(scattered[lane].sem, 16)
                        for lane in lanes:
                            hold(pool, scattered[lane].sem, i * (16 * J) + (n0[lane] + 16 * J))
                            pool.sem_inc(scatter_done[lane].sem, 1)

                    pool.wait_ge(attn_zeroed.sem, 16 * NB)
                    gather(0, range(min(EL, EB)))
                    if S.rounds > 1:
                        with pool.Fori(1, S.rounds) as i:
                            gather(i, range(EL))
                            scatter(i - 1, range(EL))
                    if S.rounds and S.rest:
                        gather(S.rounds, range(S.rest))
                    if S.rounds:
                        scatter(S.rounds - 1, range(EL))
                    if S.rest:
                        scatter(S.rounds, range(S.rest))

                @block.tensor
                def _(pe):
                    def body(at):
                        for i, lane in at("t_in"):
                            A = edge_psum(lane)
                            pe.wait_ge(chain[lane].sem, S.start(lane, i))
                            pe.wait_ge(gathered[lane].sem, S.dma("gathered", lane, i))
                            for j in range(J):
                                op = pe.transpose(A[0:REC, j * P:(j + 1) * P], rows_in[lane][:, j * REC:(j + 1) * REC], ident[:, :])
                            op.then_inc(chain[lane].sem, 1)
                        for step, before, pick in (("max_mm", "feat", pick_max), ("score_mm", "run_max", pick_score)):
                            for i, lane in at(step):
                                A = edge_psum(lane)
                                pe.wait_ge(chain[lane].sem, S.after(lane, i, before))
                                for h in range(2):
                                    c = slice(h * 512, (h + 1) * 512)
                                    op = pe.matmul(A[0:R72, c], pick[0:REC, :], feat[lane][0:REC, c], start=True, stop=True)
                                op.then_inc(chain[lane].sem, 1)
                        for i, lane in at("t_out"):
                            A = edge_psum(lane)
                            pe.wait_ge(chain[lane].sem, S.after(lane, i, "sums"))
                            for j in range(J):
                                op = pe.transpose(A[:, j * P:j * P + R72], tiles_of(feat_out[lane][0:R72, :], j), ident[0:R72, 0:R72])
                            op.then_inc(chain[lane].sem, 1)
                    S.run(pe, body, beside, beside and (lambda at: beside.tensor(pe, at)))

                @block.scalar
                def _(act):
                    def body(at):
                        for i, lane in at("feat"):
                            A = edge_psum(lane)
                            act.wait_ge(chain[lane].sem, S.after(lane, i, "t_in"))
                            act.activation(in_order(feat[lane][0:REC, :]), by_tile(A)[0:REC], ACT.Copy).then_inc(chain[lane].sem, 1)
                        for i, lane in at("weight"):
                            act.wait_ge(chain[lane].sem, S.after(lane, i, "max_step_neg"))
                            act.activation(centered[lane][0:R72, :], centered[lane][0:R72, :], ACT.Exp).then_inc(chain[lane].sem, 1)
                            act.activation(squares[lane][0:R72, :], squares[lane][0:R72, :], ACT.Exp).then_inc(chain[lane].sem, 1)
                    S.run(act, body, beside, beside and (lambda at: beside.scalar(act, at)))
                    if beside:
                        beside.stored_all(act)

                @block.vector
                def _(dve):
                    def body(at):
                        def other_lane(i, lane):
                            return (EL - 1, i - 1) if lane == 0 else (lane - 1, i)

                        for i, lane in at("carry"):
                            other, round_of = other_lane(i, lane)
                            dve.wait_ge(chain[lane].sem, S.after(lane, i, "max_mm"))
                            dve.wait_ge(chain[other].sem, S.after(other, round_of, "run_max"))
                            dve.tensor_copy(running_max[lane][0:R72, 0:1], running_max[other][0:R72, BLK:BLK + 1]).then_inc(chain[lane].sem, 1)
                        for i, lane in at("run_max"):
                            m = running_max[lane]
                            dve.wait_ge(chain[lane].sem, S.after(lane, i, "carry"))
                            dve.wait_ge(more_loaded[lane].sem, S.dma("more", lane, i))
                            dve.tensor_tensor_scan(m[0:R72, 1:BLK + 1], flags[lane][0:R72, :], edge_psum(lane)[0:R72, :], m[0:R72, 0:1],
                                                   ALU.add, ALU.max).then_inc(chain[lane].sem, 1)
                        for i, lane in at("unit"):
                            m = running_max[lane]
                            dve.wait_ge(chain[lane].sem, S.after(lane, i, "score_mm"))
                            dve.memset(feat[lane][D:R72, :], 1.0).then_inc(chain[lane].sem, 1)
                            dve.tensor_tensor(centered[lane][0:R72, :], edge_psum(lane)[0:R72, :], m[0:R72, 1:BLK + 1], ALU.subtract).then_inc(chain[lane].sem, 1)
                            dve.tensor_tensor(squares[lane][0:R72, :], m[0:R72, 0:BLK], m[0:R72, 1:BLK + 1], ALU.subtract).then_inc(chain[lane].sem, 1)
                        for i, lane in at("max_step_neg"):
                            r = squares[lane][0:R72, :]
                            dve.wait_ge(chain[lane].sem, S.after(lane, i, "max_step"))
                            dve.tensor_tensor(r, r, flags[lane][0:R72, :], ALU.add).then_inc(chain[lane].sem, 1)
                        for i, lane in at("weighted"):
                            d = centered[lane][0:R72, :]
                            dve.wait_ge(chain[lane].sem, S.after(lane, i, "rescale"))
                            dve.tensor_tensor(d, d, feat[lane][0:R72, :], ALU.mult).then_inc(chain[lane].sem, 1)
                        for i, lane in at("sums"):
                            other, round_of = other_lane(i, lane)
                            dve.wait_ge(chain[lane].sem, S.after(lane, i, "weighted"))
                            dve.wait_ge(chain[other].sem, S.after(other, round_of, "sums"))
                            dve.tensor_tensor_scan(feat_out[lane][0:R72, :], squares[lane][0:R72, :], centered[lane][0:R72, :],
                                                   feat_out[other][0:R72, BLK - 1:BLK], ALU.mult, ALU.add).then_inc(chain[lane].sem, 1)
                        for i, lane in at("guard"):
                            a = edge_psum(lane).rearrange("p (j f) -> p j f", j=J)
                            dve.wait_ge(chain[lane].sem, S.after(lane, i, "t_out"))
                            dve.tensor_scalar(stats[lane][:, 0:J * HEADS].rearrange("p (j h) -> p j h", h=HEADS), a[:, :, D:R72],
                                              SM_EPS, None, ALU.add).then_inc(chain[lane].sem, 1)
                        for i, lane in at("inverse"):
                            dve.wait_ge(chain[lane].sem, S.after(lane, i, "guard"))
                            dve.reciprocal(masked[lane][:, 0:J * HEADS], stats[lane][:, 0:J * HEADS]).then_inc(chain[lane].sem, 1)
                        for i, lane in at("rows"):
                            a = edge_psum(lane).rearrange("p (j f) -> p j f", j=J)
                            inv = masked[lane][:, 0:J * HEADS]
                            dve.wait_ge(chain[lane].sem, S.after(lane, i, "inverse"))
                            dve.wait_ge(scatter_done[lane].sem, i + done0[lane])
                            dve.tensor_tensor(rows_out[lane][:, 0:J * D].rearrange("p (j h d) -> p j h d", h=HEADS, d=HD),
                                              a[:, :, 0:D].rearrange("p j (h d) -> p j h d", d=HD),
                                              inv.rearrange("p (j h) -> p j h", h=HEADS).unsqueeze(3).broadcast_to([P, J, HEADS, HD]),
                                              ALU.mult).then_inc(chain[lane].sem, 1)
                    S.run(dve, body, beside, beside and (lambda at: beside.vector(dve, at)))
            S.close()
            if beside:
                beside.S.close()
            for lane in range(EL):
                n = S.blocks_of(lane)
                gather_ready[lane].base += n
                scatter_ready[lane].base += n
                scattered[lane].base += 16 * J * n
                scatter_done[lane].base += n

        def scatter_phase(tin):
            S = Steps(["none"], EL, EB, loads=1, stores=0, gathers=J)
            stage0 = [g.base for g in gather_ready]
            with nc.Block() as block:
                @block.sync
                def _(sp):
                    def body(i, lanes):
                        for lane in lanes:
                            hold(sp, gathered[lane].sem, S.dma("gathered", lane, i, rounds=0))
                            sp.dma_start(rows_in[lane][:, :].rearrange("p (j d) -> p j d", j=J), rows(tin, i * EL + lane)).then_inc(loaded[lane].sem, 16)
                    S.run_in_order(sp, body)

                @block.gpsimd
                def _(pool):
                    def body(i, lanes):
                        for lane in lanes:
                            b = i * EL + lane
                            hold(pool, gathered[lane].sem, S.dma("gathered", lane, i, rounds=0))
                            pool.tensor_copy(idx_stage[lane][:, 0:J], last_dst_idx[:, ds(b * J, J)]).then_inc(gather_ready[lane].sem, 1)
                            hold(pool, gather_ready[lane].sem, i + (stage0[lane] + 1))
                            hold(pool, loaded[lane].sem, S.dma("loaded", lane, i))
                            for j in range(J):
                                pool.indirect_dma_start(out[:, :], bass.IndirectOffsetOnAxis(idx_stage[lane][:, j:j + 1], 0),
                                                        rows_in[lane][:, j * P + D:(j + 1) * P], None,
                                                        bounds_check=N - 1, oob_is_err=False).then_inc(gathered[lane].sem, 16)
                    S.run_in_order(pool, body)
                    for lane in range(EL):
                        pool.wait_ge(gathered[lane].sem, S.at["gathered"][lane] + S.blocks_of(lane) * 16 * J)

        def node_rows(S, table, i, lane):
            b = S.block(lane, i)
            if isinstance(b, int) and b == NB - 1:
                return table[N - BLK:N, :].rearrange("(p j) d -> p j d", j=J)
            return rows(table, b)

        def as3(tile):
            return tile.rearrange("p (j d) -> p j d", j=J)

        def node_store(act, S, i, lane, table, tile, sem):
            b = S.block(lane, i)
            first = OVER if isinstance(b, int) and b == NB - 1 else 0
            act.dma_start(node_rows(S, table, i, lane)[first:P, :, :], as3(tile)[first:P, :, :]).then_inc(sem, 16)

        def node_sums_vector(dve, S, lane, i, h):
            hm = as3(masked[lane][:, :])
            b = S.block(lane, i)
            mask = node_mask[:, b * J:(b + 1) * J] if isinstance(b, int) else node_mask[:, ds(b * J, J)]
            dve.tensor_tensor(hm[:, :, 0:D], as3(h), mask.unsqueeze(2).broadcast_to([P, J, D]), ALU.mult).then_inc(chain[lane].sem, 1)
            dve.tensor_copy(hm[:, :, D], mask).then_inc(chain[lane].sem, 1)

        def node_sums_tensor(pe, S, lane, i, h):
            hm = as3(masked[lane][:, :])
            for j in range(J):
                op = pe.matmul(gram_nodes[0:D, 0:D + 1], h[:, j * D:(j + 1) * D], hm[:, j, :],
                               start=False, stop=False, skip_group_check=True)
            op.then_inc(chain[lane].sem, 1)

        def transpose4(pe, bank, src):
            for q in range(4):
                op = pe.transpose(bank[:, q * P:(q + 1) * P], src[:, q * P:(q + 1) * P], ident[:, :])
            return op

        class Part:

            def __init__(self, S, pace, seats):
                self.S, self.pace, self.seats = S, pace, seats

            def stored_all(self, act):
                for lane in self.S.all_lanes():
                    act.wait_ge(stored[lane].sem, self.S.at["stored"][lane] + self.S.blocks_of(lane) * self.S.per["stored"])

            def run_alone(self, pool_work=None):
                with nc.Block() as block:
                    @block.sync
                    def _(sp):
                        def body(i, lanes):
                            self.sync(sp, i, lanes)
                            self.sync_late(sp, i, lanes)
                        self.S.run_in_order(sp, body)

                    @block.tensor
                    def _(pe):
                        self.open_sums(pe)
                        self.S.run(pe, lambda at: self.tensor(pe, at))

                    @block.scalar
                    def _(act):
                        self.S.run(act, lambda at: self.scalar(act, at))
                        self.stored_all(act)

                    @block.vector
                    def _(dve):
                        self.S.run(dve, lambda at: self.vector(dve, at))

                    if pool_work:
                        @block.gpsimd
                        def _(pool):
                            pool_work(pool)
                self.S.close()

            def open_sums(self, pe):
                pass

            def sync_late(self, sp, i, lanes):
                pass

        def node_sage_part():
            blocks, pace, edge_lanes = (0, NB), 0, 0
            names = LN + ["t_in", "feat"] + [s + str(k) for k in range(3) for s in ("mm", "act")] + ["t_out", "x1"] \
                + ["again_" + s for s in LN] + ["masked", "mask", "gram"]
            seats = Seats(edge_lanes)
            tile = seats.tile
            S = Steps(names, seats.lanes, blocks[1] - blocks[0], loads=1, stores=2,
                      first_lane=seats.first, first_block=blocks[0])
            part = Part(S, pace, seats)

            def sync(sp, i, lanes):
                for lane in lanes:
                    hold(sp, chain[lane].sem, S.after(lane, i - 1, "x1"))
                    sp.dma_start(as3(tile("rows_in", lane)), node_rows(S, t["x"], i, lane)).then_inc(loaded[lane].sem, 16)

            def tensor(pe, at):
                for i, lane in at("t_in"):
                    A = seats.banks[lane]
                    pe.wait_ge(chain[lane].sem, S.after(lane, i, "ln_out"))
                    transpose4(pe, A, tile("centered", lane)).then_inc(chain[lane].sem, 1)
                for k in range(3):
                    for i, lane in at(f"mm{k}"):
                        A = seats.banks[lane]
                        pe.wait_ge(chain[lane].sem, S.after(lane, i, f"act{k - 1}" if k else "feat"))
                        pe.matmul(A, sage[k]["own"][:, :], tile("feat", lane), start=True, stop=True).then_inc(chain[lane].sem, 1)
                for i, lane in at("t_out"):
                    A = seats.banks[lane]
                    pe.wait_ge(chain[lane].sem, S.after(lane, i, "act2"))
                    transpose4(pe, A, tile("feat", lane)).then_inc(chain[lane].sem, 1)
                for i, lane in at("gram"):
                    pe.wait_ge(chain[lane].sem, S.after(lane, i, "mask"))
                    node_sums_tensor(pe, S, lane, i, tile("centered", lane))

            def scalar(act, at):
                ln_scalar(act, S, at, seats.tiles["centered"], seats.tiles["squares"], J)
                for i, lane in at("feat"):
                    A = seats.banks[lane]
                    act.wait_ge(chain[lane].sem, S.after(lane, i, "t_in"))
                    act.activation(tile("feat", lane), A, ACT.Copy).then_inc(chain[lane].sem, 1)
                for k in range(3):
                    for i, lane in at(f"act{k}"):
                        A = seats.banks[lane]
                        act.wait_ge(chain[lane].sem, S.after(lane, i, f"mm{k}"))
                        act.activation(tile("feat", lane), A, ACT.Relu, bias=sage[k]["bias"][:, :]).then_inc(chain[lane].sem, 1)
                for i, lane in at("again_ln_sum"):
                    act.wait_ge(chain[lane].sem, S.after(lane, i, "x1"))
                    node_store(act, S, i, lane, x1_nodes, tile("rows_out", lane), stored[lane].sem)
                ln_scalar(act, S, at, seats.tiles["centered"], seats.tiles["squares"], J, "again_")
                for i, lane in at("masked"):
                    act.wait_ge(chain[lane].sem, S.after(lane, i, "again_ln_out"))
                    node_store(act, S, i, lane, h_nodes[0], tile("centered", lane), stored[lane].sem)

            def vector(dve, at):
                def ready(i, lane):
                    dve.wait_ge(chain[lane].sem, S.start(lane, i))
                    dve.wait_ge(stored[lane].sem, S.dma("stored", lane, i, rounds=0))
                    dve.wait_ge(loaded[lane].sem, S.dma("loaded", lane, i))

                ln_vector(dve, S, at, ready, seats.tiles["rows_in"], seats.tiles["centered"], seats.tiles["squares"], J)
                for i, lane in at("x1"):
                    A = seats.banks[lane]
                    dve.wait_ge(chain[lane].sem, S.after(lane, i, "t_out"))
                    dve.tensor_tensor(tile("rows_out", lane), A, tile("rows_in", lane), ALU.add).then_inc(chain[lane].sem, 1)
                def ready(i, lane):
                    dve.wait_ge(chain[lane].sem, S.after(lane, i, "x1"))

                ln_vector(dve, S, at, ready, seats.tiles["rows_out"], seats.tiles["centered"], seats.tiles["squares"], J, "again_")
                for i, lane in at("masked"):
                    dve.wait_ge(chain[lane].sem, S.after(lane, i, "again_ln_out"))
                    node_sums_vector(dve, S, lane, i, tile("centered", lane))

            def open_sums(pe):
                pe.matmul(gram_nodes[0:D, 0:D + 1], zeros[:, 0:D], zeros[:, 0:D + 1], start=True, stop=True)

            part.sync, part.tensor, part.scalar, part.vector = sync, tensor, scalar, vector
            part.open_sums = open_sums
            return part

        def node_gin_part(l, blocks=(0, NB), pace=0, edge_lanes=0):
            w = gin[l]
            final = l == 2
            tin, tout = h_nodes[l % 2], x2_nodes if final else h_nodes[(l + 1) % 2]
            names = ["t_in", "feat", "w1_even", "norm_even", "w1_odd", "norm_odd", "w2", "y", "t_out", "rows"] + ([] if final else ["masked", "mask", "gram"])
            seats = Seats(edge_lanes)
            tile = seats.tile
            S = Steps(names, seats.lanes, blocks[1] - blocks[0], loads=1, more=int(final), stores=1,
                      first_lane=seats.first, first_block=blocks[0])
            part = Part(S, pace, seats)

            def sync(sp, i, lanes):
                for lane in lanes:
                    hold(sp, chain[lane].sem, S.after(lane, i - 1, "t_in"))
                    sp.dma_start(as3(tile("rows_in", lane)), node_rows(S, tin, i, lane)).then_inc(loaded[lane].sem, 16)

            def sync_late(sp, i, lanes):
                if final:
                    for lane in lanes:
                        hold(sp, chain[lane].sem, S.start(lane, i))
                        sp.dma_start(as3(tile("resid", lane)), node_rows(S, x1_nodes, i, lane)).then_inc(more_loaded[lane].sem, 16)

            def tensor(pe, at):
                for i, lane in at("t_in"):
                    A = seats.banks[lane]
                    pe.wait_ge(chain[lane].sem, S.start(lane, i))
                    pe.wait_ge(loaded[lane].sem, S.dma("loaded", lane, i))
                    transpose4(pe, A, tile("rows_in", lane)).then_inc(chain[lane].sem, 1)
                for i, lane in at("w1_even"):
                    A = seats.banks[lane]
                    pe.wait_ge(chain[lane].sem, S.after(lane, i, "feat"))
                    pe.matmul(A, w["w1_own"][0:D, :], tile("feat", lane)[0:D, 0:W], start=True, stop=True).then_inc(chain[lane].sem, 1)
                for i, lane in at("w1_odd"):
                    A = seats.banks[lane]
                    pe.wait_ge(chain[lane].sem, S.after(lane, i, "norm_even"))
                    pe.matmul(A, w["w1_own"][D:P, :], tile("feat", lane)[D:P, 0:W], start=True, stop=True).then_inc(chain[lane].sem, 1)
                for i, lane in at("w2"):
                    A = seats.banks[lane]
                    pe.wait_ge(chain[lane].sem, S.after(lane, i, "norm_odd"))
                    pe.matmul(A, w["w2_src"][:, :], tile("centered", lane), start=True, stop=False)
                    pe.matmul(A, w["w2_dst"][:, :], tile("squares", lane), start=False, stop=True).then_inc(chain[lane].sem, 1)
                for i, lane in at("t_out"):
                    A = seats.banks[lane]
                    pe.wait_ge(chain[lane].sem, S.after(lane, i, "y"))
                    transpose4(pe, A, tile("feat_out", lane)).then_inc(chain[lane].sem, 1)
                if not final:
                    for i, lane in at("gram"):
                        pe.wait_ge(chain[lane].sem, S.after(lane, i, "mask"))
                        node_sums_tensor(pe, S, lane, i, tile("rows_out", lane))

            def scalar(act, at):
                for i, lane in at("feat"):
                    A = seats.banks[lane]
                    act.wait_ge(chain[lane].sem, S.after(lane, i, "t_in"))
                    act.activation(tile("feat", lane), A, ACT.Copy).then_inc(chain[lane].sem, 1)
                for rows_of, dest in (("even", seats.tiles["centered"]), ("odd", seats.tiles["squares"])):
                    for i, lane in at("norm_" + rows_of):
                        A = seats.banks[lane]
                        act.wait_ge(chain[lane].sem, S.after(lane, i, "w1_" + rows_of))
                        act.activation(dest[lane][:, 0:W], A, ACT.Relu, bias=w["shift"][:, :],
                                       scale=w["scale"][:, :]).then_inc(chain[lane].sem, 1)
                for i, lane in at("y"):
                    A = seats.banks[lane]
                    act.wait_ge(chain[lane].sem, S.after(lane, i, "w2"))
                    act.activation(tile("feat_out", lane), A, ACT.Identity, bias=w["b2"][:, :]).then_inc(chain[lane].sem, 1)
                for i, lane in at("end" if final else "masked"):
                    act.wait_ge(chain[lane].sem, S.after(lane, i, "rows"))
                    node_store(act, S, i, lane, tout, tile("rows_out", lane), stored[lane].sem)

            def vector(dve, at):
                for i, lane in at("rows"):
                    A = seats.banks[lane]
                    dve.wait_ge(chain[lane].sem, S.after(lane, i, "t_out"))
                    dve.wait_ge(stored[lane].sem, S.dma("stored", lane, i, rounds=0))
                    if final:
                        dve.wait_ge(more_loaded[lane].sem, S.dma("more", lane, i))
                        dve.tensor_tensor(tile("rows_out", lane), A, tile("resid", lane), ALU.add).then_inc(chain[lane].sem, 1)
                    else:
                        dve.tensor_copy(tile("rows_out", lane), A).then_inc(chain[lane].sem, 1)
                if not final:
                    for i, lane in at("masked"):
                        dve.wait_ge(chain[lane].sem, S.after(lane, i, "rows"))
                        node_sums_vector(dve, S, lane, i, tile("rows_out", lane))

            def open_sums(pe):
                if final:
                    return
                pe.matmul(gram_nodes[0:D, 0:D + 1], zeros[:, 0:D], zeros[:, 0:D + 1], start=True, stop=True)

            part.sync_late = sync_late
            part.sync, part.tensor, part.scalar, part.vector = sync, tensor, scalar, vector
            part.open_sums = open_sums
            return part

        def node_final_part(blocks=(0, NB), pace=0, edge_lanes=0):
            layer = ["t", "feat", "mm", "act", "back", "l2_square", "l2_sum", "l2_root", "l2_floor", "l2_inverse", "rows"]
            names = ["t_in", "feat", "mm", "act", "t_out", "x3"] + LN + [s + str(k) for k in range(3) for s in layer] + ["out"]
            seats = Seats(edge_lanes)
            tile = seats.tile
            S = Steps(names, seats.lanes, blocks[1] - blocks[0], loads=1, more=1, stores=1,
                      first_lane=seats.first, first_block=blocks[0])
            part = Part(S, pace, seats)

            def sync(sp, i, lanes):
                for lane in lanes:
                    hold(sp, chain[lane].sem, S.after(lane, i - 1, "t_in"))
                    sp.dma_start(as3(tile("rows_in", lane)), node_rows(S, attn_nodes, i, lane)).then_inc(loaded[lane].sem, 16)
                for lane in lanes:
                    hold(sp, chain[lane].sem, S.after(lane, i - 1, "x3"))
                    sp.dma_start(as3(tile("resid", lane)), node_rows(S, x2_nodes, i, lane)).then_inc(more_loaded[lane].sem, 16)

            def tensor(pe, at):
                for i, lane in at("t_in"):
                    A = seats.banks[lane]
                    pe.wait_ge(chain[lane].sem, S.start(lane, i))
                    pe.wait_ge(loaded[lane].sem, S.dma("loaded", lane, i))
                    transpose4(pe, A, tile("rows_in", lane)).then_inc(chain[lane].sem, 1)
                for i, lane in at("mm"):
                    A = seats.banks[lane]
                    pe.wait_ge(chain[lane].sem, S.after(lane, i, "feat"))
                    pe.matmul(A, w_o[:, :], tile("feat", lane), start=True, stop=True).then_inc(chain[lane].sem, 1)
                for i, lane in at("t_out"):
                    A = seats.banks[lane]
                    pe.wait_ge(chain[lane].sem, S.after(lane, i, "act"))
                    transpose4(pe, A, tile("feat_out", lane)).then_inc(chain[lane].sem, 1)
                for k in range(3):
                    for i, lane in at(f"t{k}"):
                        A = seats.banks[lane]
                        pe.wait_ge(chain[lane].sem, S.after(lane, i, f"rows{k - 1}" if k else "ln_out"))
                        transpose4(pe, A, tile("centered", lane)).then_inc(chain[lane].sem, 1)
                    for i, lane in at(f"mm{k}"):
                        A = seats.banks[lane]
                        pe.wait_ge(chain[lane].sem, S.after(lane, i, f"feat{k}"))
                        pe.matmul(A, gnn[k]["own"][:, :], tile("feat", lane), start=True, stop=True).then_inc(chain[lane].sem, 1)
                    for i, lane in at(f"back{k}"):
                        A = seats.banks[lane]
                        pe.wait_ge(chain[lane].sem, S.after(lane, i, f"act{k}"))
                        transpose4(pe, A, tile("feat_out", lane)).then_inc(chain[lane].sem, 1)

            def scalar(act, at):
                for i, lane in at("feat"):
                    A = seats.banks[lane]
                    act.wait_ge(chain[lane].sem, S.after(lane, i, "t_in"))
                    act.activation(tile("feat", lane), A, ACT.Copy).then_inc(chain[lane].sem, 1)
                for i, lane in at("act"):
                    A = seats.banks[lane]
                    act.wait_ge(chain[lane].sem, S.after(lane, i, "mm"))
                    act.activation(tile("feat_out", lane), A, ACT.Identity, bias=b_o[:, :]).then_inc(chain[lane].sem, 1)
                ln_scalar(act, S, at, seats.tiles["centered"], seats.tiles["squares"], J)
                for k in range(3):
                    for i, lane in at(f"feat{k}"):
                        A = seats.banks[lane]
                        act.wait_ge(chain[lane].sem, S.after(lane, i, f"t{k}"))
                        act.activation(tile("feat", lane), A, ACT.Copy).then_inc(chain[lane].sem, 1)
                    for i, lane in at(f"act{k}"):
                        A = seats.banks[lane]
                        act.wait_ge(chain[lane].sem, S.after(lane, i, f"mm{k}"))
                        act.activation(tile("feat_out", lane), A, ACT.Relu, bias=gnn[k]["bias"][:, :]).then_inc(chain[lane].sem, 1)
                    for i, lane in at(f"l2_square{k}"):
                        A = seats.banks[lane]
                        act.wait_ge(chain[lane].sem, S.after(lane, i, f"back{k}"))
                        act.activation(tile("squares", lane), A, ACT.Square).then_inc(chain[lane].sem, 1)
                    for i, lane in at(f"l2_root{k}"):
                        act.wait_ge(chain[lane].sem, S.after(lane, i, f"l2_sum{k}"))
                        act.activation(stats[lane][:, 16:16 + J], stats[lane][:, 0:J], ACT.Sqrt).then_inc(chain[lane].sem, 1)
                for i, lane in at("end"):
                    act.wait_ge(chain[lane].sem, S.after(lane, i, "out"))
                    node_store(act, S, i, lane, out, tile("rows_out", lane), stored[lane].sem)

            def vector(dve, at):
                for i, lane in at("x3"):
                    A = seats.banks[lane]
                    dve.wait_ge(chain[lane].sem, S.after(lane, i, "t_out"))
                    dve.wait_ge(stored[lane].sem, S.dma("stored", lane, i, rounds=0))
                    dve.wait_ge(more_loaded[lane].sem, S.dma("more", lane, i))
                    dve.tensor_tensor(tile("rows_out", lane), A, tile("resid", lane), ALU.add).then_inc(chain[lane].sem, 1)
                def ready(i, lane):
                    dve.wait_ge(chain[lane].sem, S.after(lane, i, "x3"))

                ln_vector(dve, S, at, ready, seats.tiles["rows_out"], seats.tiles["centered"], seats.tiles["squares"], J)
                for k in range(3):
                    for i, lane in at(f"l2_sum{k}"):
                        dve.wait_ge(chain[lane].sem, S.after(lane, i, f"l2_square{k}"))
                        dve.tensor_reduce(stats[lane][:, 0:J], as3(tile("squares", lane)), AX, ALU.add).then_inc(chain[lane].sem, 1)
                    for i, lane in at(f"l2_floor{k}"):
                        dve.wait_ge(chain[lane].sem, S.after(lane, i, f"l2_root{k}"))
                        dve.tensor_scalar(stats[lane][:, 32:32 + J], stats[lane][:, 16:16 + J], L2_EPS, None, ALU.max).then_inc(chain[lane].sem, 1)
                    for i, lane in at(f"l2_inverse{k}"):
                        dve.wait_ge(chain[lane].sem, S.after(lane, i, f"l2_floor{k}"))
                        dve.reciprocal(stats[lane][:, 48:48 + J], stats[lane][:, 32:32 + J]).then_inc(chain[lane].sem, 1)
                    for i, lane in at(f"rows{k}"):
                        dve.wait_ge(chain[lane].sem, S.after(lane, i, f"l2_inverse{k}"))
                        dve.tensor_tensor(as3(tile("centered", lane)), as3(seats.banks[lane]), stats[lane][:, 48:48 + J].unsqueeze(2).broadcast_to([P, J, D]),
                                          ALU.mult).then_inc(chain[lane].sem, 1)
                for i, lane in at("out"):
                    dve.wait_ge(chain[lane].sem, S.after(lane, i, "rows2"))
                    dve.tensor_tensor(tile("rows_out", lane), tile("rows_out", lane), tile("centered", lane), ALU.add).then_inc(chain[lane].sem, 1)

            part.sync, part.tensor, part.scalar, part.vector = sync, tensor, scalar, vector
            return part

        def coefficients_phase(l):
            w = gin[l]
            s0 = setup_step.base
            with nc.Block() as block:
                @block.vector
                def _(dve):
                    step = [s0]

                    def link(op):
                        step[0] += 1
                        op.then_inc(setup_step.sem, 1)
                        dve.wait_ge(setup_step.sem, step[0])

                    k = w["keep"][0:D, :]
                    link(dve.tensor_copy(moments_edges[:, :], gram_edges[0:D, 0:D + 1]))
                    link(dve.tensor_scalar(moments[:, :], gram_nodes[0:D, 0:D + 1], k, None, ALU.mult))
                    link(dve.tensor_scalar(moments[:, 0:D], moments[:, 0:D], k, None, ALU.mult))
                    link(dve.tensor_tensor(moments[:, :], moments[:, :], moments_edges[:, :], ALU.add))
                    link(dve.tensor_scalar(moments[:, :], moments[:, :], 1.0 / N, None, ALU.mult))
                    step[0] += 1
                    dve.wait_ge(setup_step.sem, step[0])
                    link(dve.tensor_tensor(w1_moments[:, :], work[0:D, 0:H], w["w1"][0:D, :], ALU.mult))
                    link(dve.tensor_copy(coef[:, 0:1], work[:, 512:513]))
                    link(dve.tensor_tensor(coef[:, 1:2], coef[:, 0:1], coef[:, 0:1], ALU.mult))
                    step[0] += 1
                    dve.wait_ge(setup_step.sem, step[0])
                    link(dve.tensor_tensor(coef[:, 2:3], work[:, 1024:1025], coef[:, 1:2], ALU.subtract))
                    link(dve.tensor_scalar(coef[:, 2:3], coef[:, 2:3], 0.0, None, ALU.max))
                    step[0] += 1
                    dve.wait_ge(setup_step.sem, step[0])
                    link(dve.reciprocal(coef[:, 4:5], coef[:, 3:4]))
                    link(dve.tensor_tensor(w["scale"][:, :], coef[:, 4:5], w["gamma"][:, :], ALU.mult))
                    link(dve.tensor_tensor(coef[:, 5:6], coef[:, 0:1], w["b1"][:, :], ALU.add))
                    link(dve.tensor_tensor(coef[:, 6:7], w["b1"][:, :], coef[:, 5:6], ALU.subtract))
                    link(dve.tensor_tensor(coef[:, 7:8], coef[:, 6:7], w["scale"][:, :], ALU.mult))
                    link(dve.tensor_tensor(w["shift"][:, :], coef[:, 7:8], w["beta"][:, :], ALU.add))

                @block.tensor
                def _(pe):
                    pe.wait_ge(setup_step.sem, s0 + 5)
                    pe.matmul(work[0:D, 0:H], moments[0:D, 0:D], w["w1"][0:D, :], start=True, stop=True)
                    pe.matmul(work[:, 512:513], w["w1"][0:D, :], moments[0:D, D:D + 1], start=True, stop=True).then_inc(setup_step.sem, 1)
                    pe.wait_ge(setup_step.sem, s0 + 9)
                    pe.matmul(work[:, 1024:1025], w1_moments[0:D, :], ones[0:D, 0:1], start=True, stop=True).then_inc(setup_step.sem, 1)

                @block.scalar
                def _(act):
                    act.wait_ge(setup_step.sem, s0 + 12)
                    act.activation(coef[:, 3:4], coef[:, 2:3], ACT.Sqrt, bias=eps_bn[:, :]).then_inc(setup_step.sem, 1)
            setup_step.base += 19

        node_sage_part().run_alone(beside_first_nodes)
        links_and_sorted_list()
        with ExitStack() as c:
            rep_src = sb("rep_src", [P, ET], f32, c)
            segment_phase(key_pad, "key", False, attn_out_idx[:, :], rep_src[:, :], neg_start)
        extra += [sb(f"extra{k}", [P, W])[:, :] for k in range(7)]
        edge_phase("sage", 0, "nodes", None, sd[0], ln=True)
        edge_phase("sage", 1, "links", sd[0], sd[1])
        edge_phase("sage", 2, "links", sd[1], sd[0], add_resid=True)
        edge_phase("gin", 0, "links", sd[0], None, ln=True)
        coefficients_phase(0)
        node_gin_part(0).run_alone()
        gin_edge_phase(0, sd[1], False)
        edge_phase("gin", 1, "links", sd[1], None)
        coefficients_phase(1)
        node_gin_part(1).run_alone()
        gin_edge_phase(1, sd[0], False)
        edge_phase("gin", 2, "links", sd[0], None)
        coefficients_phase(2)
        gin_edge_phase(2, sd[1], True)
        half = NB // 2
        edge_phase("qkv", 0, "links", sd[1], None, ln=True, beside=node_gin_part(2, (0, half), pace=1, edge_lanes=2))
        attention_phase(beside=node_gin_part(2, (half, NB), pace=1, edge_lanes=2))
        cuts = [0, NB // 4 + 2, NB - 2 * (NB // 5 - 1), NB - (NB // 5 - 1), NB]
        edge_phase("proj", 0, "attention", None, sd[0], add_resid=True, beside=node_final_part((cuts[0], cuts[1]), pace=2, edge_lanes=2))
        edge_phase("gnn", 0, "rows", sd[0], sd[1], ln=True, beside=node_final_part((cuts[1], cuts[2]), pace=2, edge_lanes=2))
        edge_phase("gnn", 1, "links", sd[1], sd[0], beside=node_final_part((cuts[2], cuts[3]), pace=1, edge_lanes=3))
        edge_phase("gnn", 2, "links", sd[0], sd[1], add_resid=True, beside=node_final_part((cuts[3], cuts[4]), pace=1, edge_lanes=3))
        scatter_phase(sd[1])


_CONST = None


def kernel(**inputs):
    import numpy as _np
    import concourse.bacc as _bacc
    from concourse import mybir as _mybir
    from concourse.bass_utils import run_bass_kernel_spmd as _run

    nc = _bacc.Bacc("TRN2", target_bir_lowering=False, num_devices=1)
    arrays, tensors = {}, {}
    for name, value in inputs.items():
        a = _np.asarray(value)
        if name.startswith("L0_gnn_w"):
            a = a.T
        a = _np.ascontiguousarray(a)
        arrays[f"in_{name}"] = a
        tensors[name] = nc.dram_tensor(f"in_{name}", a.shape, _mybir.dt.from_np(a.dtype), kind="ExternalInput").ap()
    shape = tuple(int(n) for n in inputs["x"].shape)
    out = nc.dram_tensor("out", shape, _mybir.dt.float32, kind="ExternalOutput").ap()
    build_program(nc, tensors, out)
    r = _run(nc, [arrays], core_ids=[0])
    return r.results[0]["out"]
```
